# Optimizing a Trainium2 kernel written in Bass

```python
import numpy as np
import jax
import jax.numpy as jnp

def _softmax(x, axis=-1):
    return jax.nn.softmax(x, axis=axis)

def _gelu(x):
    return jax.nn.gelu(x, approximate=True)

def _silu(x):
    return jax.nn.silu(x)

def _sigmoid(x):
    return jax.nn.sigmoid(x)

def _layernorm(x, axis=-1, eps=1e-05):
    m = jnp.mean(x, axis=axis, keepdims=True)
    v = jnp.var(x, axis=axis, keepdims=True)
    return (x - m) / jnp.sqrt(v + eps)

def _scatter_add(tgt, idx, src, axis=0):
    return tgt.at[idx].add(src)

def _segment_sum(src, seg, n):
    return jax.ops.segment_sum(src, seg, n)
kernel_name = 'mk_vit_tower_d1_tok_img1024_r4_0c5a11'

def setup_inputs(seed: int=0):
    np.random.seed(seed)
    _w = jnp.asarray

    def _rec_inputs():
        import jax
        import jax.numpy as jnp
        _rk = jax.random.key(seed)
        x = -0.00016672 + 0.999947 * jax.random.normal(jax.random.fold_in(_rk, 1), (16, 3, 96, 96), jnp.float32)
        return x
    x = _rec_inputs()

    def _L0_tok_setup():
        import jax, jax.numpy as jnp
        import numpy as np
        P = 16
        Q_EPS = 1e-05

        def _rms_norm(x):
            return x * jax.lax.rsqrt(jnp.mean(x * x, axis=-1, keepdims=True) + 1e-06)

        def _act_quant(x):
            scale = 127.0 / jnp.clip(jnp.max(jnp.abs(x), axis=-1, keepdims=True), Q_EPS, None)
            return jnp.clip(jnp.round(x * scale), -128.0, 127.0) / scale

        def _weight_quant(w):
            scale = 1.0 / jnp.clip(jnp.mean(jnp.abs(w)), Q_EPS, None)
            return jnp.clip(jnp.round(w * scale), -1.0, 1.0) / scale
        key = jax.random.key(seed)
        k1, k2, k3, k4 = jax.random.split(key, 4)
        B, C, H, W = (64, 3, 96, 96)
        D = 256
        Din = P * P * C
        return {'x': jax.random.normal(k1, (B, C, H, W), jnp.float32), 'weight': jax.random.normal(k2, (D, Din), jnp.float32) * 0.02, 'class_token': jax.random.normal(k3, (1, 1, D), jnp.float32), 'pos_embedding': jax.random.normal(k4, (1, 1, D), jnp.float32)}
    _L0_tok_all = _L0_tok_setup()
    _L0_tok_in = {k: v for k, v in _L0_tok_all.items() if k in ('weight', 'class_token', 'pos_embedding')}
    del _L0_tok_all

    def _L0_attn_setup():
        import jax, jax.numpy as jnp
        import numpy as np
        N_HEADS = 16

        def _rope_tables(C, d_head):
            i = jnp.arange(d_head // 2, dtype=jnp.float32)
            theta = jnp.power(10000.0, -2.0 * (i - 1.0) / d_head)
            ang = jnp.arange(C, dtype=jnp.float32)[:, None] * theta[None, :]
            return (jnp.cos(ang), jnp.sin(ang))

        def _rotate(t, cos, sin):
            te, to = (t[..., 0::2], t[..., 1::2])
            re = te * cos - to * sin
            ro = te * sin + to * cos
            return jnp.stack([re, ro], axis=-1).reshape(t.shape)
        key = jax.random.key(seed)
        k1, k2, k3 = jax.random.split(key, 3)
        B, C, D = (2, 512, 256)
        x = jax.random.normal(k1, (B, C, D), dtype=jnp.float32)
        Wqkv = jax.random.normal(k2, (D, 3 * D), dtype=jnp.float32) * 0.02
        Wout = jax.random.normal(k3, (D, D), dtype=jnp.float32) * 0.02
        bout = jnp.zeros((D,), dtype=jnp.float32)
        return {'x': x, 'Wqkv': Wqkv, 'Wout': Wout, 'bout': bout}
    _L0_attn_all = _L0_attn_setup()
    _L0_attn_in = {k: v for k, v in _L0_attn_all.items() if k in ('Wqkv', 'Wout', 'bout')}
    del _L0_attn_all

    def _L0_ffn_setup():
        import jax, jax.numpy as jnp
        import numpy as np
        B, N, DIM = (2, 512, 256)
        HEADS, DIM_HEAD, EXPERTS = (8, 64, 8)
        SCALE = DIM_HEAD ** (-0.5)
        key = jax.random.key(seed)
        ks = jax.random.split(key, 6)
        dim_inner = HEADS * DIM_HEAD
        return {'x': jax.random.normal(ks[0], (B, N, DIM), jnp.float32), 'w_q': jax.random.normal(ks[1], (DIM, dim_inner), jnp.float32) * 0.02, 'w_k': jax.random.normal(ks[2], (DIM, dim_inner), jnp.float32) * 0.02, 'w_gate': jax.random.normal(ks[3], (DIM, HEADS * EXPERTS), jnp.float32) * 0.02, 'value_experts': jax.random.normal(ks[4], (EXPERTS, HEADS, DIM, DIM_HEAD), jnp.float32) * 0.02, 'output_experts': jax.random.normal(ks[5], (EXPERTS, HEADS, DIM_HEAD, DIM), jnp.float32) * 0.02}
    _L0_ffn_all = _L0_ffn_setup()
    _L0_ffn_in = {k: v for k, v in _L0_ffn_all.items() if k in ('w_q', 'w_k', 'w_gate', 'value_experts', 'output_experts')}
    del _L0_ffn_all
    return {'x': x, 'L0_tok_weight': _L0_tok_in['weight'], 'L0_tok_class_token': _L0_tok_in['class_token'], 'L0_tok_pos_embedding': _L0_tok_in['pos_embedding'], 'L0_attn_Wqkv': _L0_attn_in['Wqkv'], 'L0_attn_Wout': _L0_attn_in['Wout'], 'L0_attn_bout': _L0_attn_in['bout'], 'L0_ffn_w_q': _L0_ffn_in['w_q'], 'L0_ffn_w_k': _L0_ffn_in['w_k'], 'L0_ffn_w_gate': _L0_ffn_in['w_gate'], 'L0_ffn_value_experts': _L0_ffn_in['value_experts'], 'L0_ffn_output_experts': _L0_ffn_in['output_experts']}

def reference(x, L0_tok_weight, L0_tok_class_token, L0_tok_pos_embedding, L0_attn_Wqkv, L0_attn_Wout, L0_attn_bout, L0_ffn_w_q, L0_ffn_w_k, L0_ffn_w_gate, L0_ffn_value_experts, L0_ffn_output_experts):
    import jax
    import jax.numpy as jnp

    def _L0_tok_ref(x, weight, class_token, pos_embedding):
        import jax, jax.numpy as jnp
        import numpy as np
        P = 16
        Q_EPS = 1e-05

        def _rms_norm(x):
            return x * jax.lax.rsqrt(jnp.mean(x * x, axis=-1, keepdims=True) + 1e-06)

        def _act_quant(x):
            scale = 127.0 / jnp.clip(jnp.max(jnp.abs(x), axis=-1, keepdims=True), Q_EPS, None)
            return jnp.clip(jnp.round(x * scale), -128.0, 127.0) / scale

        def _weight_quant(w):
            scale = 1.0 / jnp.clip(jnp.mean(jnp.abs(w)), Q_EPS, None)
            return jnp.clip(jnp.round(w * scale), -1.0, 1.0) / scale
        B, C, H, W = x.shape
        h, w = (H // P, W // P)
        patches = x.reshape(B, C, h, P, w, P).transpose(0, 2, 4, 3, 5, 1).reshape(B, h * w, P * P * C)
        xn = _rms_norm(patches)
        xq = xn + jax.lax.stop_gradient(_act_quant(xn) - xn)
        wq = weight + jax.lax.stop_gradient(_weight_quant(weight) - weight)
        proj = jnp.einsum('bnd,od->bno', xq, wq)
        cls = jnp.broadcast_to(class_token, (B, 1, proj.shape[-1]))
        out = jnp.concatenate([cls, proj], axis=1) + pos_embedding
        return out

    def _L0_attn_ref(x, Wqkv, Wout, bout):
        import jax, jax.numpy as jnp
        import numpy as np
        N_HEADS = 16

        def _rope_tables(C, d_head):
            i = jnp.arange(d_head // 2, dtype=jnp.float32)
            theta = jnp.power(10000.0, -2.0 * (i - 1.0) / d_head)
            ang = jnp.arange(C, dtype=jnp.float32)[:, None] * theta[None, :]
            return (jnp.cos(ang), jnp.sin(ang))

        def _rotate(t, cos, sin):
            te, to = (t[..., 0::2], t[..., 1::2])
            re = te * cos - to * sin
            ro = te * sin + to * cos
            return jnp.stack([re, ro], axis=-1).reshape(t.shape)
        B, C, D = x.shape
        H = N_HEADS
        dh = D // H
        qkv = x @ Wqkv
        q, k, v = jnp.split(qkv, 3, axis=-1)
        q = q.reshape(B, C, H, dh).transpose(0, 2, 1, 3)
        k = k.reshape(B, C, H, dh).transpose(0, 2, 1, 3)
        v = v.reshape(B, C, H, dh).transpose(0, 2, 1, 3)
        cos, sin = _rope_tables(C, dh)
        q_rot = _rotate(q, cos, sin)
        k_rot = _rotate(k, cos, sin)
        scale = 1.0 / jnp.sqrt(jnp.asarray(dh, dtype=x.dtype))
        num = jnp.exp(jnp.einsum('bhqd,bhkd->bhqk', q_rot, k_rot) * scale)
        den = jnp.sum(jnp.exp(jnp.einsum('bhqd,bhkd->bhqk', q, k) * scale), axis=-1, keepdims=True)
        attn = num / den
        causal = jnp.tril(jnp.ones((C, C), dtype=bool))
        attn = jnp.where(causal[None, None], attn, 0.0)
        y = jnp.einsum('bhqk,bhkd->bhqd', attn, v)
        y = y.transpose(0, 2, 1, 3).reshape(B, C, D)
        return y @ Wout + bout

    def _L0_ffn_ref(x, w_q, w_k, w_gate, value_experts, output_experts):
        import jax, jax.numpy as jnp
        import numpy as np
        B, N, DIM = (2, 512, 256)
        HEADS, DIM_HEAD, EXPERTS = (8, 64, 8)
        SCALE = DIM_HEAD ** (-0.5)
        b, n, _ = x.shape
        q = (x @ w_q).reshape(b, n, HEADS, DIM_HEAD).transpose(0, 2, 1, 3)
        k = (x @ w_k).reshape(b, n, HEADS, DIM_HEAD).transpose(0, 2, 1, 3)
        gates = jax.nn.sigmoid((x @ w_gate).reshape(b, n, HEADS, EXPERTS).transpose(0, 2, 1, 3))
        sel = jnp.argmax(gates, axis=-1)
        gm = jax.nn.one_hot(sel, EXPERTS, dtype=x.dtype) * gates
        values = jnp.einsum('bhne,ehdk,bnd->bhnk', gm, value_experts, x)
        sim = jnp.einsum('bhid,bhjd->bhij', q * SCALE, k)
        causal_mask = jnp.triu(jnp.ones((n, n), dtype=bool), 1)
        sim = jnp.where(causal_mask, jnp.finfo(sim.dtype).min, sim)
        attn = jax.nn.softmax(sim, axis=-1)
        out = jnp.einsum('bhij,bhjk->bhik', attn, values)
        out = jnp.einsum('bhne,ehkd,bhnk->bhnd', gm, output_experts, out)
        return out.sum(axis=1)
    h = _L0_tok_ref(x, L0_tok_weight, L0_tok_class_token, L0_tok_pos_embedding)
    h = h + _L0_attn_ref(_layernorm(h, axis=-1), L0_attn_Wqkv, L0_attn_Wout, L0_attn_bout)
    h = h + _L0_ffn_ref(_layernorm(h, axis=-1), L0_ffn_w_q, L0_ffn_w_k, L0_ffn_w_gate, L0_ffn_value_experts, L0_ffn_output_experts)
    return h

_drawn_inputs = setup_inputs


def setup_inputs(seed=0):
    import zlib

    import numpy as np

    out = dict(_drawn_inputs(seed))
    spreads = {'L0_attn_bout': (0.0, 0.1)}
    factors = {'L0_ffn_w_q': 8.0, 'L0_ffn_w_k': 8.0}
    for name, (base, spread) in spreads.items():
        noise = np.random.default_rng([zlib.crc32(name.encode()), seed]).standard_normal(out[name].shape)
        drawn = base * np.exp(spread * noise) if base else spread * noise
        out[name] = jnp.asarray(drawn.astype(out[name].dtype))
    for name, factor in factors.items():
        out[name] = (out[name] * factor).astype(out[name].dtype)
    return out
```

```python
from contextlib import ExitStack

import numpy as np

import concourse.bass as bass
from concourse import mybir
from concourse.alu_op_type import AluOpType as ALU

ACT = mybir.ActivationFunctionType
AX = mybir.AxisListType.X
F32 = mybir.dt.float32
F32R = mybir.dt.float32r
BF16 = mybir.dt.bfloat16
U8 = mybir.dt.uint8

P = 128
B, CH, IMG, PATCH = 16, 3, 96, 16
SIDE = IMG // PATCH
NPATCH = SIDE * SIDE
S = NPATCH + 1
D = 256
KC = D // P
DIN = PATCH * PATCH * CH
DC = DIN // P
T = B * S
GI = 3
G = -(-B // GI)
R = GI * S
TP = G * R
HALF = T // 2
NH1, DH1 = 16, 16
PAIRS = NH1 // 2
JP = 4
BI = 4
NB = B // BI
UN = KC * BI
NH2, DH2, NE = 8, 64, 8
C2 = NH2 // 2
OEU = 4
NOU = C2 * NE // OEU
ROUND = 12582912.0
Q_EPS = 1e-5
BIG = 3.0e38

_C = {}
_w = 0
for _n, _k in (("ident", 128), ("cos", S), ("sin", S), ("par", 4), ("keep", S), ("cbias", S),
               ("blk2", 32), ("blk3", GI), ("rank", NE), ("rowsel", 2 * R), ("hsel", NH2)):
    _C[_n] = (_w, _w + _k)
    _w += _k
NCONST = _w


def shape_constants():
    c = np.zeros((P, NCONST), np.float32)

    def put(name, a):
        c[:a.shape[0], _C[name][0]:_C[name][0] + a.shape[1]] = a

    r = np.arange(P)
    put("ident", np.eye(P, dtype=np.float32))
    i = ((r % DH1) // 2).astype(np.float32)
    theta = np.power(np.float32(10000.0), np.float32(-2.0) * (i - np.float32(1.0)) / np.float32(DH1))
    ang = (np.arange(S, dtype=np.float32)[None, :] * theta[:, None].astype(np.float32)).astype(np.float32)
    put("cos", np.cos(ang))
    put("sin", np.sin(ang) * np.where(r % 2 == 0, -1.0, 1.0)[:, None].astype(np.float32))
    scale2 = DH2 ** -0.5
    put("par", np.stack([(r // DH1) % 2 == 0, (r // DH1) % 2 == 1, (r < DH2) * scale2, (r >= DH2) * scale2], 1))
    r2, k2 = np.arange(2 * S), np.arange(S)
    put("keep", ((r2 % S)[:, None] <= k2[None, :]).astype(np.float32))
    put("cbias", np.where(k2[None, :] > (r2 % S)[:, None], -BIG, 0.0).astype(np.float32))
    put("blk2", ((r2 // S)[:, None] == np.arange(32)[None, :] // DH1).astype(np.float32))
    put("blk3", (np.arange(R)[:, None] // S == np.arange(GI)[None, :]).astype(np.float32))
    put("rank", np.tile(np.arange(NE, 0, -1, dtype=np.float32), (P, 1)))
    rows = np.zeros((3, 2 * R), np.float32)
    rows[0, :R] = 1.0
    rows[1, :R] = np.arange(R) % S == 0
    rows[2, R:] = 1.0
    put("rowsel", rows)
    put("hsel", (np.arange(NH2 * NE)[:, None] // NE == np.arange(NH2)[None, :]).astype(np.float32))
    return c


def bcast(ap, axis, n):
    v = ap.unsqueeze(axis)
    shape = list(v.shape)
    shape[axis] = n
    return v.to_broadcast(shape)


def vit_block(nc, x, tokw, vecs, consts, wqkv, wout, w2, ve, oe, out):
    with ExitStack() as ctx:
        def sem(name):
            return ctx.enter_context(nc.semaphore(name))

        def sbuf(stack, name, shape, dt=F32):
            return stack.enter_context(nc.sbuf_tensor(name, shape, dt))

        cst = sbuf(ctx, "cst", [P, NCONST])
        ident_bf = sbuf(ctx, "ident_bf", [P, P], BF16)
        mask_sel = sbuf(ctx, "mask_sel", [NH2 * NE, C2, NE, 2, DH2], BF16)
        gate_sel = sbuf(ctx, "gate_sel", [NH2 * NE, NH2, DH2])
        ones = sbuf(ctx, "ones", [P, P])
        half_neg = sbuf(ctx, "half_neg", [P, GI])
        h = sbuf(ctx, "h", [R, G, D])
        x2hi = sbuf(ctx, "x2hi", [P, KC, TP], F32R)
        x2lo = sbuf(ctx, "x2lo", [P, KC, TP], F32R)
        W2C = 2 * NH2 * DH2 + NH2 * NE
        w2hi = sbuf(ctx, "w2hi", [P, KC, W2C], F32R)
        w2lo = sbuf(ctx, "w2lo", [P, KC, W2C], F32R)
        NVR = 2
        veraw = sbuf(ctx, "veraw", [P, NVR, KC, NH2 * DH2])
        vehi = sbuf(ctx, "vehi", [P, NVR, KC, NH2 * DH2], F32R)
        velo = sbuf(ctx, "velo", [P, NVR, KC, NH2 * DH2], F32R)
        stat6 = sbuf(ctx, "stat6", [R, 2, 6])
        mv = sbuf(ctx, "mv", [R, 2, G, 2])
        lnv = sbuf(ctx, "lnv", [R, 2, G])
        rstd = sbuf(ctx, "rstd", [R, 2, G])
        xhat = sbuf(ctx, "xhat", [R, 2, D])

        first = ExitStack()
        x1hi = sbuf(first, "x1hi", [P, KC, TP], F32R)
        x1lo = sbuf(first, "x1lo", [P, KC, TP], F32R)
        wqhi = sbuf(first, "wqhi", [P, KC, 5, D], F32R)
        wqlo = sbuf(first, "wqlo", [P, KC, 5, D], F32R)
        wo = sbuf(first, "wo", [P, KC, D])
        biasb = sbuf(first, "biasb", [R, 2, D])
        vsplit = sbuf(first, "vsplit", [R, 2, G, PAIRS, 2, DH1])
        tok = ExitStack()
        xp = sbuf(tok, "xp", [R, G, DIN])
        yround = sbuf(tok, "yround", [R, 2, DIN])
        sqjunk = sbuf(tok, "sqjunk", [R, 2, DIN])
        qb = sbuf(tok, "qb", [R, 2, DIN], BF16)
        qT = sbuf(tok, "qT", [P, 2, DC, R + 1], BF16)
        tw = sbuf(tok, "tw", [P, DC * D])
        tern = sbuf(tok, "tern", [P, DC * D], BF16)
        vrow = sbuf(tok, "vrow", [3, D])
        wqraw = sbuf(tok, "wqraw", [P, KC, 5, D])
        w2raw = sbuf(tok, "w2raw", [P, KC, W2C])
        small = sbuf(tok, "small", [P, 8])
        amax = sbuf(tok, "amax", [R, G])
        ssq = sbuf(tok, "ssq", [R, G])
        msq = sbuf(tok, "msq", [R, G])
        rrms = sbuf(tok, "rrms", [R, G])
        amn = sbuf(tok, "amn", [R, G])
        amc = sbuf(tok, "amc", [R, G])
        iam = sbuf(tok, "iam", [R, G])
        qsc = sbuf(tok, "qsc", [R, G])
        dqs = sbuf(tok, "dqs", [R, G])
        tok.close()
        raw = sbuf(first, "raw", [P, KC, 4, T])
        ropet = sbuf(first, "ropet", [P, T])
        qrot = sbuf(first, "qrot", [P, KC, T])
        kun = sbuf(first, "kun", [P, KC, B, 2, S])
        krot = sbuf(first, "krot", [P, KC, B, 2, S])
        vblk = sbuf(first, "vblk", [2 * S, B, PAIRS, 2, DH1])
        en = sbuf(first, "en", [2 * S, 2, JP, UN * S])
        ed = sbuf(first, "ed", [2 * S, JP, UN * S])
        rden = sbuf(first, "rden", [P, UN * S])
        yT = sbuf(first, "yT", [P, KC, TP])
        first.close()

        last = ctx
        h1T = sbuf(last, "h1T", [P, KC, TP])
        v2 = sbuf(last, "v2", [R, G, NH2, DH2])
        ez = sbuf(last, "ez", [R, 2, NH2 * NE])
        gate = sbuf(last, "gate", [R, 2, NH2, NE])
        gtop = sbuf(last, "gtop", [R, G, NH2])
        geq = sbuf(last, "geq", [R, 2, NH2, NE])
        grk = sbuf(last, "grk", [R, 2, NH2])
        onehot = sbuf(last, "onehot", [R, G, NH2, NE], U8)
        gm = sbuf(last, "gm", [R, G, NH2, NE])
        gmT = sbuf(last, "gmT", [NH2 * NE, TP])
        maskT = sbuf(last, "maskT", [NH2 * NE, TP], BF16)
        gateb = sbuf(last, "gateb", [P, C2, T])
        sc = sbuf(last, "sc", [2 * S, 2, C2 * GI, S])
        pe2 = sbuf(last, "pe2", [2 * S, 2, C2 * GI, S])
        mx2 = sbuf(last, "mx2", [2 * S, 2, C2 * GI])
        sm2 = sbuf(last, "sm2", [2 * S, 2, C2 * GI])
        rs2 = sbuf(last, "rs2", [2 * S, 2, C2 * GI])
        ptb = sbuf(last, "ptb", [R, G, NH2, GI, S])
        ot = sbuf(last, "ot", [P, T])
        oThi = sbuf(last, "oThi", [P, C2, T], F32R)
        oTlo = sbuf(last, "oTlo", [P, C2, T], F32R)
        NGR = 2
        ghi = sbuf(last, "ghi", [P, NGR, 2, HALF], F32R)
        glo = sbuf(last, "glo", [P, NGR, 2, HALF], F32R)
        yo = sbuf(last, "yo", [P, KC, 2, HALF])
        qk = ExitStack()
        q2 = sbuf(qk, "q2", [P, C2, B, 2, S])
        k2 = sbuf(qk, "k2", [P, C2, T])
        qk.close()
        NOR = 2
        oeraw = sbuf(last, "oeraw", [P, NOR, OEU, D])
        oehi = sbuf(last, "oehi", [P, NOR, OEU, D], F32R)
        oelo = sbuf(last, "oelo", [P, NOR, OEU, D], F32R)

        ps = ctx.enter_context(nc.psum_tensor("ps", [P, 8, 512], F32))

        x_in = [sem(f"x_in{g}") for g in range(G)]
        tokw_in, const_in, vec_in, wqkv_in, w2_in, wout_in = (
            sem(n) for n in ("tokw_in", "const_in", "vec_in", "wqkv_in", "w2_in", "wout_in"))
        ve_in = [sem(f"ve_in{e}") for e in range(NVR)]
        oe_in = [sem(f"oe_in{e}") for e in range(NOR)]
        out_done = sem("out_done")
        v_in = sem("v_in")
        names = """pool_setup ident_ready bias_ps bias_sb wabs tot_ps wscale clip_t tern_pre tern_ready sq_done msq_ready rrms_ready
            qpar amaxed yround_ready qb_ready qT_ps qT_sb proj_ps h0_ready lnv_ready rstd_ready xhat_ready x1T_ps x1hi_ready
            x1lo_ready wqhi_ready wqlo_ready w2hi_ready w2lo_ready qk_ps raw_ready rope_t rope1 v_ps vsplit_zero vsplit_ready
            s_ps exp_ready en_ready pv_ps den_ps rden_ready yT_ready yT_pad op_ps h0b_ready h1_ready x2T_ps x2hi_ready
            x2lo_ready qk2_ps qk2_ready gate_ps ez_ready gchain gm_ready gmT_ps gmT_ready maskT_ready gateb_ps gateb_ready
            s2_ps sc_ready e2_ready schain p2_ready p2n pt_ps ptb_ready vehi_ready velo_ready ve_ps sel0_ready sel_ready
            v2_ready aux_ps aux_done oT_tmp oT_hi g_ready main_ps oehi_ready oelo_ready acc_done out_ready qchain lnchain""".split()
        sm = {n: sem(n) for n in names}

        def cols(name, rows=P):
            a, b = _C[name]
            return cst[0:rows, a:b]

        def images(g):
            return min(GI, B - g * GI)

        def split3(pe, o, lhi, llo, rhi, rlo, start, stop):
            pe.matmul(o, llo, rhi, start=start, stop=False)
            pe.matmul(o, lhi, rlo, start=False, stop=False)
            return pe.matmul(o, lhi, rhi, start=False, stop=stop)

        QKJ = [(c, kind, hf) for c in range(KC) for kind in range(4) for hf in range(2)]
        block = ctx.enter_context(nc.Block())

        AUX = []
        for c in range(C2):
            if c == 0:
                AUX.append(("pv", 0))
            for e in range(NE):
                AUX.append(("mask", c * NE + e))
                if e == NE - 4 and c + 1 < C2:
                    AUX.append(("pv", c + 1))
        mask_at = {k: n for n, (kind, k) in enumerate(AUX) if kind == "mask"}

        SOFT = [G + 1 + G * g for g in range(G)]

        @block.sync
        def _(sp):
            sp.dma_start(xp[:, 0, :], x[0]).then_inc(x_in[0], 16)
            sp.dma_start(tw[:], tokw).then_inc(tokw_in, 16)
            sp.dma_start(xp[:, 1, :], x[1]).then_inc(x_in[1], 16)
            sp.dma_start(cst[:], consts).then_inc(const_in, 16)
            sp.dma_start(vrow[:], vecs).then_inc(vec_in, 16)
            for g in range(2, G):
                sp.dma_start(xp[:, g, :], x[g]).then_inc(x_in[g], 16)
            sp.dma_start(wqraw[:], wqkv).then_inc(wqkv_in, 16)
            sp.dma_start(w2raw[:], w2).then_inc(w2_in, 16)
            sp.dma_start(wo[:], wout).then_inc(wout_in, 16)
            sp.wait_ge(sm["vsplit_ready"], G)
            for ii in range(GI):
                for p_ in range(2):
                    ng = len(range(ii, B, GI))
                    sp.dma_start(vblk[p_ * S:(p_ + 1) * S, ii::GI], vsplit[ii * S:(ii + 1) * S, p_, 0:ng]).then_inc(
                        v_in, 16)
            for e in range(NE):
                if e >= NVR:
                    sp.wait_ge(sm["vehi_ready"], e - NVR + 1)
                    sp.wait_ge(sm["velo_ready"], e - NVR + 1)
                sp.dma_start(veraw[:, e % NVR], ve[e]).then_inc(ve_in[e % NVR], 16)
            for u in range(NOU):
                if u == 0:
                    sp.wait_ge(sm["s2_ps"], G)
                if u >= NOR:
                    sp.wait_ge(sm["oehi_ready"], u - NOR + 1)
                    sp.wait_ge(sm["oelo_ready"], u - NOR + 1)
                sp.dma_start(oeraw[:, u % NOR], oe[u]).then_inc(oe_in[u % NOR], 16)
            for m in range(KC):
                sp.wait_ge(sm["out_ready"], m + 1)
                sp.dma_start(out[m], yo[:, m]).then_inc(out_done, 16)
            sp.wait_ge(out_done, 16 * KC)

        @block.gpsimd
        def _(pool):
            pool.memset(ones[:], 1.0).then_inc(sm["pool_setup"], 1)
            pool.memset(half_neg[:], -0.5).then_inc(sm["pool_setup"], 1)
            pool.wait_ge(sm["pool_setup"], 2)

            pool.memset(vsplit[:], 0.0).then_inc(sm["vsplit_zero"], 1)

            def qkv_lo(b):
                pool.wait_ge(sm["wqhi_ready"], b + 1)
                pool.tensor_tensor(wqlo[:, :, b], wqraw[:, :, b], wqhi[:, :, b].bitcast(F32),
                                   ALU.subtract).then_inc(sm["wqlo_ready"], 1)

            for b in range(2):
                pool.wait_ge(sm["msq_ready"], b + 1)
                s_ = slice(GI * b, GI * b + GI)
                pool.tensor_tensor(rrms[:, s_], msq[:, s_], half_neg[0:R, :], ALU.pow).then_inc(sm["rrms_ready"], 1)
            for g in range(G):
                pool.wait_ge(sm["lnv_ready"], g + 1)
                pool.tensor_tensor(rstd[:, 0, g:g + 1], lnv[:, 0, g:g + 1], half_neg[0:R, 0:1],
                                   ALU.pow).then_inc(sm["rstd_ready"], 1)
                if g < 5:
                    qkv_lo(g)
            for g in range(G):
                pool.wait_ge(sm["xhat_ready"], g + 1)
                pool.tensor_tensor(h[:, g], h[:, g], biasb[:, 1], ALU.add).then_inc(sm["h0b_ready"], 1)
            pool.wait_ge(sm["w2hi_ready"], 1)
            pool.tensor_tensor(w2lo[:], w2raw[:], w2hi[:].bitcast(F32), ALU.subtract).then_inc(sm["w2lo_ready"], 1)
            pool.wait_ge(const_in, 16)
            for c in range(C2):
                src = cst[0:NH2 * NE, c * 16:(c + 1) * 16].rearrange("q (j e) -> q e j", j=2)
                pool.tensor_copy(mask_sel[:, c], bcast(src, 3, DH2)).then_inc(sm["pool_setup"], 1)
            pool.tensor_copy(gate_sel[:], bcast(cols("hsel", NH2 * NE), 2, DH2)).then_inc(sm["pool_setup"], 1)

            def ve_lo(e):
                if e >= NVR:
                    pool.wait_ge(sm["ve_ps"], G * (e - NVR + 1))
                pool.wait_ge(sm["vehi_ready"], e + 1)
                pool.tensor_tensor(velo[:, e % NVR], veraw[:, e % NVR], vehi[:, e % NVR].bitcast(F32),
                                   ALU.subtract).then_inc(sm["velo_ready"], 1)

            for e in range(NVR):
                ve_lo(e)
            for g in range(G):
                pool.wait_ge(sm["lnv_ready"], G + g + 1)
                pool.tensor_tensor(rstd[:, 1, g:g + 1], lnv[:, 1, g:g + 1], half_neg[0:R, 0:1],
                                   ALU.pow).then_inc(sm["rstd_ready"], 1)
            for e in range(NVR, NE):
                ve_lo(e)
            for u in range(NOU):
                if u >= NOR:
                    pool.wait_ge(sm["main_ps"], OEU * (u - NOR + 1))
                pool.wait_ge(sm["oehi_ready"], u + 1)
                pool.tensor_tensor(oelo[:, u % NOR], oeraw[:, u % NOR], oehi[:, u % NOR].bitcast(F32),
                                   ALU.subtract).then_inc(sm["oelo_ready"], 1)

        @block.scalar
        def _(act):
            def square(g):
                act.wait_ge(x_in[g], 16)
                if g >= 2:
                    act.wait_ge(sm["sq_done"], g - 1)
                act.activation(sqjunk[:, g % 2], xp[:, g], ACT.Square,
                               accum_out=ssq[:, g:g + 1]).then_inc(sm["sq_done"], 1)

            def round_up(g):
                act.wait_ge(sm["qpar"], g // GI + 1)
                if g >= 2:
                    act.wait_ge(sm["qb_ready"], g - 1)
                act.activation(yround[:, g % 2], xp[:, g], ACT.Copy, bias=ROUND,
                               scale=qsc[:, g:g + 1]).then_inc(sm["yround_ready"], 1)

            def x1_hi(g):
                act.wait_ge(sm["x1T_ps"], g + 1)
                act.activation(x1hi[:, :, g * R:(g + 1) * R],
                               ps[:, 4 + g % 2, 0:KC * R].rearrange("p (c t) -> p c t", c=KC),
                               ACT.Copy).then_inc(sm["x1hi_ready"], 1)

            for g in range(GI):
                square(g)
            act.wait_ge(sm["tern_pre"], 1)
            act.activation(tern[:], tw[:], ACT.Copy, bias=-ROUND).then_inc(sm["tern_ready"], 1)
            for g in range(GI, G):
                square(g)
            for g in range(3):
                round_up(g)
            act.wait_ge(wqkv_in, 16)
            for b in range(5):
                act.activation(wqhi[:, :, b], wqraw[:, :, b], ACT.Copy).then_inc(sm["wqhi_ready"], 1)
            for g in range(G):
                if g + 3 < G:
                    round_up(g + 3)
                x1_hi(g)
            act.wait_ge(w2_in, 16)
            act.activation(w2hi[:], w2raw[:], ACT.Copy).then_inc(sm["w2hi_ready"], 1)

            def qk_evac(n):
                c, kind, hf = QKJ[n]
                act.wait_ge(sm["qk_ps"], n + 1)
                if n == 0:
                    act.wait_ge(sm["w2lo_ready"], 1)
                    act.wait_ge(sm["x1lo_ready"], G)
                act.activation(raw[:, c, kind, hf * HALF:(hf + 1) * HALF], ps[:, n % 4, 0:HALF],
                               ACT.Copy).then_inc(sm["raw_ready"], 1)

            def v_evac(g):
                act.wait_ge(sm["v_ps"], g + 1)
                if g == 0:
                    act.wait_ge(sm["vsplit_zero"], 1)
                src = ps[0:R, 4 + g % 4, 0:D].rearrange("p (h a b) -> p h a b", h=PAIRS, a=2)
                for p_ in range(2):
                    ins = act.activation(vsplit[:, p_, g, :, p_], src[:, :, p_], ACT.Copy)
                ins.then_inc(sm["vsplit_ready"], 1)

            for n in range(8):
                qk_evac(n)
            for g in range(G):
                v_evac(g)
            for n in range(8, 16):
                qk_evac(n)

            def ve_hi(e):
                act.wait_ge(ve_in[e % NVR], 16 * (e // NVR + 1))
                if e >= NVR:
                    act.wait_ge(sm["ve_ps"], G * (e - NVR + 1))
                act.activation(vehi[:, e % NVR], veraw[:, e % NVR], ACT.Copy).then_inc(sm["vehi_ready"], 1)

            for e in range(NVR):
                ve_hi(e)
            for b in range(NB):
                for kind in range(2):
                    act.wait_ge(sm["s_ps"], 2 * b + kind + 1)
                    if kind == 0 and b >= 2:
                        act.wait_ge(sm["pv_ps"], b - 1)
                    if kind == 1 and b >= 1:
                        act.wait_ge(sm["den_ps"], b)
                    dst = en[:, b % 2] if kind == 0 else ed[:]
                    act.activation(dst, ps[0:2 * S, 0:JP, 0:UN * S], ACT.Exp,
                                   scale=DH1 ** -0.5).then_inc(sm["exp_ready"], 1)
            for g in range(G):
                act.wait_ge(sm["x2T_ps"], g + 1)
                src = ps[:, 2 + g % 2, 0:2 * KC * R].rearrange("p (a c t) -> p a c t", a=2, c=KC)
                act.activation(h1T[:, :, g * R:(g + 1) * R], src[:, 1], ACT.Copy)
                act.activation(x2hi[:, :, g * R:(g + 1) * R], src[:, 0], ACT.Copy).then_inc(sm["x2hi_ready"], 1)
            for g in range(2):
                act.wait_ge(sm["gate_ps"], g + 1)
                act.activation(ez[:, g % 2], ps[0:R, g % 2, 0:NH2 * NE], ACT.Exp, scale=-1.0).then_inc(sm["ez_ready"], 1)
            for n in range(4 * C2):
                u, hf = n // 2, n % 2
                act.wait_ge(sm["qk2_ps"], n + 1)
                src, col = ps[:, 4 + n % 4, 0:HALF], slice(hf * HALF, (hf + 1) * HALF)
                if u < C2:
                    act.activation(k2[:, u, col], src, ACT.Copy).then_inc(sm["qk2_ready"], 1)
                else:
                    for p_ in range(2):
                        ins = act.activation(q2[:, u - C2, 8 * hf:8 * hf + 8, p_], src.rearrange("p (i s) -> p i s", s=S), ACT.Copy,
                                             scale=cols("par")[:, 2 + p_:3 + p_])
                    ins.then_inc(sm["qk2_ready"], 1)
                if n % 4 == 3:
                    g = 2 + n // 4
                    act.wait_ge(sm["gate_ps"], g + 1)
                    act.wait_ge(sm["gm_ready"], g - 1)
                    act.activation(ez[:, g % 2], ps[0:R, g % 2, 0:NH2 * NE], ACT.Exp,
                                   scale=-1.0).then_inc(sm["ez_ready"], 1)

            def first_expert(g):
                act.wait_ge(sm["ve_ps"], g + 1)
                act.activation(v2[:, g].rearrange("p a b -> p (a b)"), ps[0:R, 4 + g % 4, :],
                               ACT.Copy).then_inc(sm["sel0_ready"], 1)

            def exp2(g):
                act.wait_ge(sm["sc_ready"], g + 1)
                if g >= 2:
                    act.wait_ge(sm["p2_ready"], g - 1)
                n = C2 * images(g)
                act.activation(pe2[:, g % 2, 0:n], sc[:, g % 2, 0:n], ACT.Exp).then_inc(sm["e2_ready"], 1)

            def gmT_evac(g):
                act.wait_ge(sm["gmT_ps"], g + 1)
                act.activation(gmT[:, g * R:(g + 1) * R], ps[0:NH2 * NE, g % 2, 0:R], ACT.Copy).then_inc(sm["gmT_ready"], 1)

            for g in range(G):
                first_expert(g)
                gmT_evac(g)
            ve_hi(NVR)
            for n in range(2 * C2):
                c, hf = n // 2, n % 2
                act.wait_ge(sm["gateb_ps"], n + 1)
                act.activation(gateb[:, c, hf * HALF:(hf + 1) * HALF], ps[:, hf, 0:HALF],
                               ACT.Copy).then_inc(sm["gateb_ready"], 1)
            for g in range(G):
                exp2(g)
                if g + NVR + 1 < NE:
                    ve_hi(g + NVR + 1)

            for u in range(NOU):
                act.wait_ge(oe_in[u % NOR], 16 * (u // NOR + 1))
                if u >= NOR:
                    act.wait_ge(sm["main_ps"], OEU * (u - NOR + 1))
                act.activation(oehi[:, u % NOR], oeraw[:, u % NOR], ACT.Copy).then_inc(sm["oehi_ready"], 1)

        @block.vector
        def _(dve):
            count = {}

            def step(name, ins):
                count[name] = count.get(name, 0) + 1
                ins.then_inc(sm[name], 1)
                dve.wait_ge(sm[name], count[name])

            def absmax(g):
                dve.wait_ge(x_in[g], 16)
                dve.tensor_reduce(amax[:, g:g + 1], xp[:, g], AX, ALU.max,
                                  apply_absolute_value=True).then_inc(sm["amaxed"], 1)

            def mean_square(b):
                dve.wait_ge(sm["sq_done"], GI * (b + 1))
                s_ = slice(GI * b, GI * b + GI)
                dve.tensor_scalar(msq[:, s_], ssq[:, s_], 1.0 / DIN, 1e-6, ALU.mult,
                                  ALU.add).then_inc(sm["msq_ready"], 1)

            def quant_scales(b):
                dve.wait_ge(sm["rrms_ready"], b + 1)
                s_ = slice(GI * b, GI * b + GI)
                step("qchain", dve.tensor_tensor(amn[:, s_], amax[:, s_], rrms[:, s_], ALU.mult))
                step("qchain", dve.tensor_scalar(amc[:, s_], amn[:, s_], Q_EPS, None, ALU.max))
                step("qchain", dve.reciprocal(iam[:, s_], amc[:, s_]))
                dve.scalar_tensor_tensor(out=qsc[:, s_], in0=rrms[:, s_], scalar=127.0, in1=iam[:, s_],
                                         op0=ALU.mult, op1=ALU.mult).then_inc(sm["qpar"], 1)
                step("qchain", dve.tensor_scalar(dqs[:, s_], amc[:, s_], small[0:R, 3:4], None, ALU.mult))

            for g in range(GI):
                absmax(g)
                if g == 0:
                    dve.wait_ge(tokw_in, 16)
                    dve.tensor_reduce(small[:, 0:1], tw[:], AX, ALU.add,
                                      apply_absolute_value=True).then_inc(sm["wabs"], 1)
            dve.wait_ge(const_in, 16)
            dve.tensor_copy(ident_bf[:], cols("ident")).then_inc(sm["ident_ready"], 1)
            dve.wait_ge(sm["amaxed"], GI)
            mean_square(0)
            dve.wait_ge(sm["tot_ps"], 1)
            step("wscale", dve.tensor_scalar(small[:, 1:2], ps[:, 6, 0:1], 1.0 / (D * DIN), Q_EPS, ALU.mult, ALU.max))
            step("wscale", dve.reciprocal(small[:, 2:3], small[:, 1:2]))
            step("wscale", dve.tensor_scalar(small[:, 3:4], small[:, 1:2], 1.0 / 127.0, None, ALU.mult))
            step("clip_t", dve.tensor_scalar(tw[:], tw[:], small[:, 2:3], 1.0, ALU.mult, ALU.min))
            dve.tensor_scalar(tw[:], tw[:], -1.0, ROUND, ALU.max, ALU.add).then_inc(sm["tern_pre"], 1)
            quant_scales(0)
            for g in range(GI, G):
                absmax(g)
            dve.wait_ge(sm["amaxed"], G)
            mean_square(1)
            dve.wait_ge(sm["bias_ps"], 1)
            step("bias_sb", dve.tensor_copy(biasb[:], ps[0:R, 7, :].rearrange("p (a d) -> p a d", a=2)))
            quant_scales(1)

            def quantised(g):
                dve.wait_ge(sm["yround_ready"], g + 1)
                if g >= 2:
                    dve.wait_ge(sm["qT_ps"], g - 1)
                dve.tensor_scalar(qb[:, g % 2], yround[:, g % 2], ROUND, 127.0, ALU.subtract,
                                  ALU.min).then_inc(sm["qb_ready"], 1)

            def quantised_T(g):
                dve.wait_ge(sm["qT_ps"], g + 1)
                if g >= 2:
                    dve.wait_ge(sm["proj_ps"], g - 1)
                src = ps[:, g % 2, :].bitcast(BF16)[:, 0:DC * (R + 1)].rearrange("p (c t) -> p c t", c=DC)
                dve.tensor_copy(qT[:, g % 2, :, 0:R], src[:, :, 0:R]).then_inc(sm["qT_sb"], 1)

            def ln_stats(which, g):
                step("lnchain", dve.bn_stats(stat6[:, which], h[:, g]))
                step("lnchain", dve.bn_aggr(mv[:, which, g], stat6[:, which]))
                dve.tensor_scalar(lnv[:, which, g:g + 1], mv[:, which, g, 1:2], 1e-5, None,
                                  ALU.add).then_inc(sm["lnv_ready"], 1)

            def ln_apply(which, g):
                n = which * G + g
                dve.wait_ge(sm["rstd_ready"], n + 1)
                if g >= 2:
                    dve.wait_ge(sm["x2T_ps" if which else "x1T_ps"], g - 1)
                dve.tensor_scalar(xhat[:, g % 2], h[:, g], mv[:, which, g, 0:1], rstd[:, which, g:g + 1],
                                  ALU.subtract, ALU.mult).then_inc(sm["xhat_ready"], 1)

            def embed(g):
                dve.wait_ge(sm["proj_ps"], g + 1)
                step("h0_ready", dve.scalar_tensor_tensor(
                    out=h[:, g], in0=ps[0:R, 2 + g % 2, 0:D], scalar=dqs[:, g:g + 1], in1=biasb[:, 0],
                    op0=ALU.mult, op1=ALU.add))
                ln_stats(0, g)

            def x1_lo(g):
                dve.wait_ge(sm["x1hi_ready"], g + 1)
                tc = slice(g * R, (g + 1) * R)
                dve.tensor_tensor(x1lo[:, :, tc], ps[:, 4 + g % 2, 0:KC * R].rearrange("p (c t) -> p c t", c=KC),
                                  x1hi[:, :, tc].bitcast(F32), ALU.subtract).then_inc(sm["x1lo_ready"], 1)

            for s_ in range(G + 4):
                if s_ < G:
                    quantised(s_)
                if 0 <= s_ - 1 < G:
                    quantised_T(s_ - 1)
                if 0 <= s_ - 2 < G:
                    embed(s_ - 2)
                if 0 <= s_ - 3 < G:
                    ln_apply(0, s_ - 3)
                if 0 <= s_ - 4 < G:
                    x1_lo(s_ - 4)

            def per_position(name):
                return bcast(cols(name), 1, B)

            def rope(c):
                def by_image(a):
                    return a.rearrange("p (i s) -> p i s", i=B)
                for kind in (0, 2):
                    dve.wait_ge(sm["raw_ready"], 8 * c + 2 * kind + 4)
                    dve.tensor_tensor(by_image(ropet[:]), by_image(raw[:, c, kind]), per_position("cos"),
                                      ALU.mult).then_inc(sm["rope_t"], 1)
                    count["rope_t"] = count.get("rope_t", 0) + 1
                    step("rope_t", dve.tensor_tensor(by_image(raw[:, c, kind + 1]), by_image(raw[:, c, kind + 1]),
                                                     per_position("sin"), ALU.mult))
                    if kind == 0:
                        step("rope_t", dve.tensor_tensor(qrot[:, c], ropet[:], raw[:, c, 1], ALU.add))
                    else:
                        step("rope_t", dve.tensor_tensor(ropet[:], ropet[:], raw[:, c, 3], ALU.add))
                        for p_ in range(2):
                            sel = cols("par")[:, p_:p_ + 1]
                            dve.tensor_scalar(kun[:, c, :, p_], by_image(raw[:, c, 2]), sel, None,
                                              ALU.mult).then_inc(sm["rope_t"], 1)
                            dve.tensor_scalar(krot[:, c, :, p_], by_image(ropet[:]), sel, None,
                                              ALU.mult).then_inc(sm["rope_t"], 1)
                            count["rope_t"] += 2
                        dve.wait_ge(sm["rope_t"], count["rope_t"])

            dve.memset(yT[:, :, T:TP], 0.0).then_inc(sm["yT_pad"], 1)
            for c in range(KC):
                rope(c)

            def causal(b):
                dve.wait_ge(sm["exp_ready"], 2 * b + 1)
                v = en[:, b % 2].rearrange("p j (u s) -> p (j u) s", s=S)
                dve.tensor_tensor(v, v, bcast(cols("keep", 2 * S), 1, JP * UN), ALU.mult).then_inc(sm["en_ready"], 1)

            def normalise(b):
                o = 4 + 2 * (b % 2)
                if b:
                    dve.wait_ge(sm["yT_ready"], b)
                dve.wait_ge(sm["den_ps"], b + 1)
                step("rden_ready", dve.reciprocal(rden[:], ps[:, o + 1, 0:UN * S]))
                dve.wait_ge(sm["pv_ps"], b + 1)
                dve.tensor_tensor(yT[:, :, b * BI * S:(b + 1) * BI * S],
                                  ps[:, o, 0:UN * S].rearrange("p (c t) -> p c t", c=KC),
                                  rden[:].rearrange("p (c t) -> p c t", c=KC), ALU.mult).then_inc(sm["yT_ready"], 1)

            for b in range(NB):
                causal(b)
                if b:
                    normalise(b - 1)
            normalise(NB - 1)

            def residual(g):
                dve.wait_ge(sm["op_ps"], g + 1)
                dve.wait_ge(sm["h0b_ready"], g + 1)
                step("h1_ready", dve.tensor_tensor(h[:, g], h[:, g], ps[0:R, g % 2, 0:D], ALU.add))
                ln_stats(1, g)

            def x2_lo(g):
                dve.wait_ge(sm["x2hi_ready"], g + 1)
                tc = slice(g * R, (g + 1) * R)
                dve.tensor_tensor(x2lo[:, :, tc], ps[:, 2 + g % 2, 0:KC * R].rearrange("p (c t) -> p c t", c=KC),
                                  x2hi[:, :, tc].bitcast(F32), ALU.subtract).then_inc(sm["x2lo_ready"], 1)

            for s_ in range(G + 2):
                if s_ < G:
                    residual(s_)
                if 0 <= s_ - 1 < G:
                    ln_apply(1, s_ - 1)
                if 0 <= s_ - 2 < G:
                    x2_lo(s_ - 2)

            def gates(g):
                k = g % 2
                dve.wait_ge(sm["ez_ready"], g + 1)
                z = ez[:, k]
                step("gchain", dve.tensor_scalar(z, z, 1.0, None, ALU.add))
                step("gchain", dve.reciprocal(gate[:, k].rearrange("p a b -> p (a b)"), z))
                step("gchain", dve.tensor_reduce(gtop[:, g], gate[:, k], AX, ALU.max))
                step("gchain", dve.tensor_tensor(geq[:, k], gate[:, k], bcast(gtop[:, g], 2, NE), ALU.is_equal))
                step("gchain", dve.tensor_tensor(geq[:, k], geq[:, k], bcast(cols("rank", R), 1, NH2), ALU.mult))
                step("gchain", dve.tensor_reduce(grk[:, k], geq[:, k], AX, ALU.max))
                step("gchain", dve.tensor_tensor(onehot[:, g], geq[:, k], bcast(grk[:, k], 2, NE), ALU.is_equal))
                dve.tensor_tensor(gm[:, g], onehot[:, g], gate[:, k], ALU.mult).then_inc(sm["gm_ready"], 1)

            def softmax_a(g):
                k, n = g % 2, C2 * images(g)
                dve.wait_ge(sm["s2_ps"], g + 1)
                src = ps[0:2 * S, 2 + g % 2, 0:n * S].rearrange("p (u s) -> p u s", s=S)
                step("schain", dve.tensor_tensor(sc[:, k, 0:n], src, bcast(cols("cbias", 2 * S), 1, n), ALU.add))
                step("schain", dve.tensor_reduce(mx2[:, k, 0:n], sc[:, k, 0:n], AX, ALU.max))
                dve.tensor_tensor(sc[:, k, 0:n], sc[:, k, 0:n], bcast(mx2[:, k, 0:n], 2, S),
                                  ALU.subtract).then_inc(sm["sc_ready"], 1)

            def softmax_b(g):
                k, n = g % 2, C2 * images(g)
                dve.wait_ge(sm["e2_ready"], g + 1)
                step("schain", dve.tensor_reduce(sm2[:, k, 0:n], pe2[:, k, 0:n], AX, ALU.add))
                step("schain", dve.reciprocal(rs2[:, k, 0:n], sm2[:, k, 0:n]))
                if g >= 2:
                    dve.wait_ge(sm["pt_ps"], g - 1)
                dve.tensor_tensor(pe2[:, k, 0:n], pe2[:, k, 0:n], bcast(rs2[:, k, 0:n], 2, S),
                                  ALU.mult).then_inc(sm["p2_ready"], 1)

            def spread_p(g):
                m = images(g) * S
                ni = images(g)
                dve.wait_ge(sm["pt_ps"], g + 1)
                src = ps[0:m, g % 2, 0:NH2 * S].rearrange("p (h s) -> p h s", h=NH2)
                dve.tensor_tensor(ptb[0:m, g, :, 0:ni], bcast(src, 2, ni),
                                  bcast(bcast(cols("blk3", m)[:, 0:ni], 1, NH2), 3, S),
                                  ALU.mult).then_inc(sm["ptb_ready"], 1)

            def mask_rows(g):
                dve.wait_ge(sm["gmT_ready"], g + 1)
                tc = slice(g * R, (g + 1) * R)
                dve.tensor_scalar(maskT[:, tc], gmT[:, tc], 0.0, None, ALU.is_gt).then_inc(sm["maskT_ready"], 1)

            def select(e, g):
                n = e * G + g
                dve.wait_ge(sm["ve_ps"], n + 1)
                if e == 1:
                    dve.wait_ge(sm["sel0_ready"], g + 1)
                else:
                    dve.wait_ge(sm["sel_ready"], (e - 2) * G + g + 1)
                dve.copy_predicated(v2[:, g], bcast(onehot[:, g, :, e], 2, DH2),
                                    ps[0:R, 4 + n % 4, :].rearrange("p (a b) -> p a b", a=NH2)).then_inc(sm["sel_ready"], 1)

            for g in range(G):
                gates(g)
            for g in range(G):
                mask_rows(g)
            for e in range(1, NE):
                for g in range(G):
                    select(e, g)
                    for f, lag in ((softmax_a, 1), (softmax_b, 3), (spread_p, 5)):
                        for gg in range(G):
                            if SOFT[gg] + lag == e * G + g:
                                f(gg)
                    if e == NE - 1:
                        dve.wait_ge(sm["sel_ready"], (NE - 2) * G + g + 1)
                        dve.tensor_tensor(v2[:, g], v2[:, g], bcast(gtop[:, g], 2, DH2),
                                          ALU.mult).then_inc(sm["v2_ready"], 1)

            for n, (kind, k) in enumerate(AUX):
                o = 4 + 2 * (n % 2)
                dve.wait_ge(sm["aux_ps"], n + 1)
                if kind == "pv":
                    if k == 0:
                        dve.wait_ge(sm["gateb_ready"], 2 * C2)
                    A = GI * R
                    dve.tensor_tensor(ot[:, 0:A], ps[:, o, 0:A], gateb[:, k, 0:A], ALU.mult)
                    dve.tensor_tensor(ot[:, A:T], ps[:, o + 1, 0:T - A], gateb[:, k, A:T],
                                      ALU.mult).then_inc(sm["aux_done"], 1)
                    dve.wait_ge(sm["aux_done"], n + 1)
                    step("oT_hi", dve.tensor_copy(oThi[:, k], ot[:]))
                    step("oT_hi", dve.tensor_tensor(oTlo[:, k], ot[:], oThi[:, k].bitcast(F32), ALU.subtract))
                else:
                    c = k // NE
                    if k >= NGR:
                        dve.wait_ge(sm["main_ps"], k - NGR + 1)
                    msk = ps[:, o:o + 2, 0:HALF]
                    dve.tensor_tensor(ghi[:, k % NGR], msk, oThi[:, c].bitcast(F32).rearrange(
                        "p (a t) -> p a t", a=2), ALU.mult).then_inc(sm["g_ready"], 1)
                    dve.tensor_tensor(glo[:, k % NGR], msk, oTlo[:, c].bitcast(F32).rearrange(
                        "p (a t) -> p a t", a=2), ALU.mult).then_inc(sm["aux_done"], 1)
            for m in range(KC):
                dve.wait_ge(sm["acc_done"], m + 1)
                dve.tensor_tensor(yo[:, m], ps[:, 2 * m:2 * m + 2, 0:HALF],
                                  h1T[:, m, 0:T].rearrange("p (a t) -> p a t", a=2), ALU.add).then_inc(sm["out_ready"], 1)

        @block.tensor
        def _(pe):
            pe.wait_ge(const_in, 16)
            pe.wait_ge(vec_in, 16)
            for a in range(2):
                ins = pe.matmul(ps[0:R, 7, a * D:(a + 1) * D], cols("rowsel", 3)[:, a * R:(a + 1) * R], vrow[:],
                                start=True, stop=True)
            ins.then_inc(sm["bias_ps"], 1)
            pe.wait_ge(sm["pool_setup"], 2)
            pe.wait_ge(sm["wabs"], 1)
            pe.matmul(ps[:, 6, 0:1], ones[:], small[:, 0:1], start=True, stop=True).then_inc(sm["tot_ps"], 1)

            def turn_q(g):
                pe.wait_ge(sm["qb_ready"], g + 1)
                if g == 0:
                    pe.wait_ge(sm["ident_ready"], 1)
                if g >= 2:
                    pe.wait_ge(sm["qT_sb"], g - 1)
                dst = ps[:, g % 2, :].bitcast(BF16)
                for c in range(DC):
                    ins = pe.transpose(dst[:, c * (R + 1):c * (R + 1) + R], qb[:, g % 2, c * P:(c + 1) * P],
                                       ident_bf[0:R, 0:R])
                ins.then_inc(sm["qT_ps"], 1)

            def embed(g):
                pe.wait_ge(sm["qT_sb"], g + 1)
                if g == 0:
                    pe.wait_ge(sm["tern_ready"], 1)
                if g >= 2:
                    pe.wait_ge(sm["h0_ready"], g - 1)
                for c in range(DC):
                    ins = pe.matmul(ps[0:R, 2 + g % 2, 0:D], qT[:, g % 2, c, 0:R], tern[:, c * D:(c + 1) * D],
                                    start=(c == 0), stop=(c == DC - 1))
                ins.then_inc(sm["proj_ps"], 1)

            def turn_x(g):
                pe.wait_ge(sm["xhat_ready"], g + 1)
                if g >= 2:
                    pe.wait_ge(sm["x1lo_ready"], g - 1)
                for c in range(KC):
                    ins = pe.transpose(ps[:, 4 + g % 2, c * R:(c + 1) * R], xhat[:, g % 2, c * P:(c + 1) * P],
                                       cst[0:R, 0:R])
                ins.then_inc(sm["x1T_ps"], 1)

            for s_ in range(G + 2):
                if s_ < G:
                    turn_q(s_)
                if 0 <= s_ - 1 < G:
                    embed(s_ - 1)
                if 0 <= s_ - 2 < G:
                    turn_x(s_ - 2)

            WB = (0, 2, 1, 3)

            def qk_job(n):
                c, kind, hf = QKJ[n]
                if n == 0:
                    pe.wait_ge(sm["x1lo_ready"], G)
                    pe.wait_ge(sm["wqlo_ready"], 5)
                if n >= 4:
                    pe.wait_ge(sm["raw_ready"], n - 3)
                wb, tc = WB[kind], slice(hf * HALF, (hf + 1) * HALF)
                for k in range(KC):
                    col = slice(c * P, (c + 1) * P)
                    ins = split3(pe, ps[:, n % 4, 0:HALF], wqhi[:, k, wb, col], wqlo[:, k, wb, col],
                                 x1hi[:, k, tc], x1lo[:, k, tc], k == 0, k == KC - 1)
                ins.then_inc(sm["qk_ps"], 1)

            def v_job(g):
                if g >= 4:
                    pe.wait_ge(sm["vsplit_ready"], g - 3)
                elif g == 0:
                    pe.wait_ge(sm["bias_sb"], 1)
                tc = slice(g * R, (g + 1) * R)
                for k in range(KC):
                    ins = split3(pe, ps[0:R, 4 + g % 4, 0:D], x1hi[:, k, tc], x1lo[:, k, tc],
                                 wqhi[:, k, 4], wqlo[:, k, 4], k == 0, k == KC - 1)
                ins.then_inc(sm["v_ps"], 1)

            for n in range(8):
                qk_job(n)
            for g in range(G):
                v_job(g)
            for n in range(8, 16):
                qk_job(n)

            def scores(b, kind):
                n = 2 * b + kind
                if n == 0:
                    pe.wait_ge(sm["raw_ready"], len(QKJ))
                    pe.wait_ge(sm["rope_t"], 20)
                else:
                    pe.wait_ge(sm["exp_ready"], n)
                for c in range(KC):
                    for ii in range(BI):
                        i = b * BI + ii
                        tc, u = slice(i * S, (i + 1) * S), c * BI + ii
                        for j in range(JP):
                            row = slice(32 * j, 32 * j + 32)
                            key = (kun if kind else krot)[row, c, i].rearrange("p a b -> p (a b)")
                            qry = raw[row, c, 0, tc] if kind else qrot[row, c, tc]
                            ins = pe.matmul(ps[0:2 * S, j, u * S:(u + 1) * S], key, qry, start=True, stop=True)
                ins.then_inc(sm["s_ps"], 1)

            def attend(b):
                pe.wait_ge(sm["en_ready"], b + 1)
                if b == 0:
                    pe.wait_ge(v_in, 16 * 2 * GI)
                if b >= 2:
                    pe.wait_ge(sm["yT_ready"], b - 1)
                for c in range(KC):
                    for ii in range(BI):
                        u = c * BI + ii
                        for j in range(JP):
                            vv = vblk[:, b * BI + ii, c * JP + j].rearrange("p a b -> p (a b)")
                            ins = pe.matmul(ps[32 * j:32 * j + 32, 4 + 2 * (b % 2), u * S:(u + 1) * S], vv,
                                            en[:, b % 2, j, u * S:(u + 1) * S], start=True, stop=True)
                ins.then_inc(sm["pv_ps"], 1)

            def denominators(b):
                pe.wait_ge(sm["exp_ready"], 2 * b + 2)
                if b >= 2:
                    pe.wait_ge(sm["yT_ready"], b - 1)
                for j in range(JP):
                    ins = pe.matmul(ps[32 * j:32 * j + 32, 5 + 2 * (b % 2), 0:UN * S], cols("blk2", 2 * S),
                                    ed[:, j], start=True, stop=True)
                ins.then_inc(sm["den_ps"], 1)

            for b in range(NB):
                scores(b, 0)
                if b:
                    denominators(b - 1)
                scores(b, 1)
                attend(b)
            denominators(NB - 1)

            def out_proj(g):
                if g == 0:
                    pe.wait_ge(sm["exp_ready"], 2 * NB)
                    pe.wait_ge(wout_in, 16)
                    pe.wait_ge(sm["yT_pad"], 1)
                if g >= 2:
                    pe.wait_ge(sm["h1_ready"], g - 1)
                pe.wait_ge(sm["yT_ready"], min(NB, -(-(g + 1) * R // (BI * S))))
                for k in range(KC):
                    ins = pe.matmul(ps[0:R, g % 2, 0:D], yT[:, k, g * R:(g + 1) * R], wo[:, k],
                                    start=(k == 0), stop=(k == KC - 1))
                ins.then_inc(sm["op_ps"], 1)

            def turn_x2(g):
                pe.wait_ge(sm["xhat_ready"], G + g + 1)
                if g >= 2:
                    pe.wait_ge(sm["x2lo_ready"], g - 1)
                for a in range(2):
                    for c in range(KC):
                        src = (h[:, g] if a else xhat[:, g % 2])[:, c * P:(c + 1) * P]
                        o = (a * KC + c) * R
                        ins = pe.transpose(ps[:, 2 + g % 2, o:o + R], src, cst[0:R, 0:R])
                ins.then_inc(sm["x2T_ps"], 1)

            for s_ in range(G + 1):
                if s_ < G:
                    out_proj(s_)
                if 0 <= s_ - 1 < G:
                    turn_x2(s_ - 1)

            NQ = NH2 * DH2

            def gate_job(g):
                if g < 2:
                    pe.wait_ge(sm["h1_ready"], G)
                else:
                    pe.wait_ge(sm["ez_ready"], g - 1)
                pe.wait_ge(sm["x2lo_ready"], g + 1)
                tc = slice(g * R, (g + 1) * R)
                for k in range(KC):
                    ins = split3(pe, ps[0:R, g % 2, 0:NH2 * NE], x2hi[:, k, tc], x2lo[:, k, tc],
                                 w2hi[:, k, 2 * NQ:], w2lo[:, k, 2 * NQ:], k == 0, k == KC - 1)
                ins.then_inc(sm["gate_ps"], 1)

            pe.wait_ge(sm["w2lo_ready"], 1)
            gate_job(0)
            gate_job(1)
            for n in range(4 * C2):
                u, hf = n // 2, n % 2
                if n < 4:
                    pe.wait_ge(sm["yT_ready"], NB)
                else:
                    pe.wait_ge(sm["qk2_ready"], n - 3)
                base = (NQ if u < C2 else 0) + (u % C2) * P
                tc = slice(hf * HALF, (hf + 1) * HALF)
                pe.wait_ge(sm["x2lo_ready"], 3 if hf == 0 else G)
                for k in range(KC):
                    ins = split3(pe, ps[:, 4 + n % 4, 0:HALF], w2hi[:, k, base:base + P], w2lo[:, k, base:base + P],
                                 x2hi[:, k, tc], x2lo[:, k, tc], k == 0, k == KC - 1)
                ins.then_inc(sm["qk2_ps"], 1)
                if n % 4 == 1:
                    gate_job(2 + n // 4)

            def value_job(e, g):
                n = e * G + g
                if n < 4:
                    pe.wait_ge(sm["qk2_ready"], 4 * C2)
                elif n - 4 < G:
                    pe.wait_ge(sm["sel0_ready"], n - 3)
                else:
                    pe.wait_ge(sm["sel_ready"], n - 4 - G + 1)
                if g == 0:
                    pe.wait_ge(sm["velo_ready"], e + 1)
                tc = slice(g * R, (g + 1) * R)
                for k in range(KC):
                    ins = split3(pe, ps[0:R, 4 + n % 4, :], x2hi[:, k, tc], x2lo[:, k, tc],
                                 vehi[:, e % NVR, k], velo[:, e % NVR, k], k == 0, k == KC - 1)
                ins.then_inc(sm["ve_ps"], 1)

            def turn_gates(g):
                pe.wait_ge(sm["gm_ready"], g + 1)
                if g < 2:
                    pe.wait_ge(sm["ez_ready"], G)
                else:
                    pe.wait_ge(sm["gmT_ready"], g - 1)
                pe.transpose(ps[0:NH2 * NE, g % 2, 0:R], gm[:, g].rearrange("p a b -> p (a b)"),
                             cst[0:R, 0:R]).then_inc(sm["gmT_ps"], 1)

            def gate_rows(n):
                c, hf = n // 2, n % 2
                if n < 2:
                    pe.wait_ge(sm["gmT_ready"], G)
                    pe.wait_ge(sm["pool_setup"], 2 + C2 + 1)
                else:
                    pe.wait_ge(sm["gateb_ready"], n - 1)
                pe.matmul(ps[:, hf, 0:HALF], gate_sel[:, 2 * c:2 * c + 2].rearrange("p a b -> p (a b)"),
                          gmT[:, hf * HALF:(hf + 1) * HALF], start=True, stop=True).then_inc(sm["gateb_ps"], 1)

            def scores2(g):
                if g < 2:
                    pe.wait_ge(sm["x2lo_ready"], G)
                else:
                    pe.wait_ge(sm["sc_ready"], g - 1)
                ni = images(g)
                for c in range(C2):
                    for ii in range(ni):
                        i = g * GI + ii
                        tc = slice(i * S, (i + 1) * S)
                        u = c * ni + ii
                        ins = pe.matmul(ps[0:2 * S, 2 + g % 2, u * S:(u + 1) * S], q2[:, c, i].rearrange("p a b -> p (a b)"), k2[:, c, tc],
                                        start=True, stop=True)
                ins.then_inc(sm["s2_ps"], 1)

            def turn_p(g):
                pe.wait_ge(sm["p2_ready"], g + 1)
                if g < 2:
                    pe.wait_ge(sm["gateb_ready"], 2 * C2)
                else:
                    pe.wait_ge(sm["ptb_ready"], g - 1)
                ni = images(g)
                for c in range(C2):
                    src = pe2[:, g % 2, c * ni:(c + 1) * ni].rearrange("p u s -> p (u s)")
                    ins = pe.transpose(ps[0:ni * S, g % 2, c * 2 * S:(c + 1) * 2 * S], src, cst[0:2 * S, 0:2 * S])
                ins.then_inc(sm["pt_ps"], 1)

            for g in range(G):
                value_job(0, g)
                turn_gates(g)
            for e in range(1, NE):
                for g in range(G):
                    value_job(e, g)
                    n = e * G + g
                    if G <= n < G + C2:
                        gate_rows(2 * (n - G))
                        gate_rows(2 * (n - G) + 1)
                    for gg in range(G):
                        if SOFT[gg] == n:
                            scores2(gg)
                        if SOFT[gg] + 4 == n:
                            turn_p(gg)

            def aux(n):
                kind, k = AUX[n]
                o = 4 + 2 * (n % 2)
                if n < 2:
                    pe.wait_ge(sm["v2_ready"], G)
                else:
                    pe.wait_ge(sm["aux_done"], n - 1)
                if kind == "pv":
                    pe.wait_ge(sm["ptb_ready"], G)
                    for g in range(G):
                        ni = images(g)
                        m = ni * S
                        for p_ in range(2):
                            hd = 2 * k + p_
                            q0 = (g % GI) * R
                            ins = pe.matmul(ps[DH2 * p_:DH2 * p_ + DH2, o + g // GI, q0:q0 + m], v2[0:m, g, hd],
                                            ptb[0:m, g, hd, 0:ni].rearrange("p a b -> p (a b)"), start=True, stop=True)
                else:
                    c, e = k // NE, k % NE
                    if k == 0:
                        pe.wait_ge(sm["maskT_ready"], G)
                    for hf in range(2):
                        ins = pe.matmul(ps[:, o + hf, 0:HALF], mask_sel[:, c, e].rearrange("p a b -> p (a b)"),
                                        maskT[:, hf * HALF:(hf + 1) * HALF], start=True, stop=True)
                ins.then_inc(sm["aux_ps"], 1)

            def main(k):
                u = k // OEU
                pe.wait_ge(sm["oelo_ready"], u + 1)
                pe.wait_ge(sm["aux_done"], mask_at[k] + 1)
                if k == 0:
                    pe.wait_ge(sm["ptb_ready"], G)
                for m in range(KC):
                    col = slice(m * P, (m + 1) * P)
                    w_hi, w_lo = oehi[:, u % NOR, k % OEU, col], oelo[:, u % NOR, k % OEU, col]
                    s0, s1 = k == 0, k == C2 * NE - 1
                    for hf in range(2):
                        o = ps[:, 2 * m + hf, 0:HALF]
                        g_hi, g_lo = ghi[:, k % NGR, hf], glo[:, k % NGR, hf]
                        ins = split3(pe, o, w_hi, w_lo, g_hi, g_lo, s0, s1)
                    if s1:
                        ins.then_inc(sm["acc_done"], 1)
                if not s1:
                    ins.then_inc(sm["main_ps"], 1)

            done = 0
            for k in range(C2 * NE):
                ahead = mask_at[min(k + 1, C2 * NE - 1)]
                while done <= ahead:
                    aux(done)
                    done += 1
                main(k)


def kernel(**inputs):
    import concourse.bacc as bacc
    from concourse.bass_utils import run_bass_kernel_spmd

    x = np.asarray(inputs["x"])
    patches = x.reshape(B, CH, SIDE, PATCH, SIDE, PATCH).transpose(0, 2, 4, 3, 5, 1).reshape(B, NPATCH, DIN)
    rows = np.zeros((G * GI, S, DIN), np.float32)
    rows[:B, 1:] = patches
    tokw = np.asarray(inputs["L0_tok_weight"]).T.reshape(DC, P, D).transpose(1, 0, 2).reshape(P, DC * D)
    vecs = np.concatenate([np.asarray(inputs["L0_tok_pos_embedding"]).reshape(1, D),
                           np.asarray(inputs["L0_tok_class_token"]).reshape(1, D),
                           np.asarray(inputs["L0_attn_bout"]).reshape(1, D)])
    w = np.asarray(inputs["L0_attn_Wqkv"])
    wq, wk, wv = w[:, :D], w[:, D:2 * D], w[:, 2 * D:]
    swap = np.arange(D) ^ 1
    wqkv = np.stack([wq, wk, wq[:, swap], wk[:, swap], wv], 1).reshape(KC, P, 5, D).transpose(1, 0, 2, 3)
    wout = np.asarray(inputs["L0_attn_Wout"]).reshape(KC, P, D).transpose(1, 0, 2)
    w2 = np.concatenate([np.asarray(inputs["L0_ffn_w_q"]), np.asarray(inputs["L0_ffn_w_k"]),
                         np.asarray(inputs["L0_ffn_w_gate"])], 1).reshape(KC, P, -1).transpose(1, 0, 2)
    ve = np.asarray(inputs["L0_ffn_value_experts"]).transpose(0, 2, 1, 3)
    ve = ve.reshape(NE, KC, P, NH2 * DH2).transpose(0, 2, 1, 3)
    oe = np.asarray(inputs["L0_ffn_output_experts"]).reshape(NE, C2, 2 * DH2, D).transpose(1, 0, 2, 3)
    oe = oe.reshape(C2, NE // OEU, OEU, P, D).transpose(0, 1, 3, 2, 4).reshape(NOU, P, OEU, D)
    arrays = {"x_rows": rows.reshape(G, R, DIN), "tok_weight": tokw, "vectors": vecs, "constants": shape_constants(),
              "w_qkv": wqkv, "w_out": wout, "w_qkgate": w2, "value_w": ve, "output_w": oe}
    arrays = {n: np.ascontiguousarray(a) for n, a in arrays.items()}

    nc = bacc.Bacc("TRN2", target_bir_lowering=False, num_devices=1)
    args = [nc.dram_tensor(n, a.shape, F32, kind="ExternalInput").ap() for n, a in arrays.items()]
    out = nc.dram_tensor("out", [KC, P, 2, HALF], F32, kind="ExternalOutput").ap()
    vit_block(nc, *args, out)
    r = run_bass_kernel_spmd(nc, [arrays], core_ids=[0])
    y = r.results[0]["out"].reshape(D, T)
    return np.ascontiguousarray(y.T).reshape(B, S, D)
```

```python
from contextlib import ExitStack

import numpy as np

import concourse.bass as bass
from concourse import mybir
from concourse.alu_op_type import AluOpType as ALU

ACT = mybir.ActivationFunctionType
AX = mybir.AxisListType.X
F32 = mybir.dt.float32
F32R = mybir.dt.float32r
BF16 = mybir.dt.bfloat16
U8 = mybir.dt.uint8

P = 128
B, CH, IMG, PATCH = 16, 3, 96, 16
SIDE = IMG // PATCH
NPATCH = SIDE * SIDE
S = NPATCH + 1
D = 256
KC = D // P
DIN = PATCH * PATCH * CH
DC = DIN // P
T = B * S
GI = 3
G = -(-B // GI)
R = GI * S
TP = G * R
HALF = T // 2
NH1, DH1 = 16, 16
PAIRS = NH1 // 2
JP = 4
BI = 4
NB = B // BI
UN = KC * BI
NH2, DH2, NE = 8, 64, 8
C2 = NH2 // 2
OEU = 4
NOU = C2 * NE // OEU
ROUND = 12582912.0
Q_EPS = 1e-5
BIG = 3.0e38

_C = {}
_w = 0
for _n, _k in (("ident", 128), ("cos", S), ("sin", S), ("par", 8), ("keep", S), ("cbias", S),
               ("blk2", 32), ("blk3", GI), ("rank", NE), ("rowsel", 2 * R), ("hsel", NH2)):
    _C[_n] = (_w, _w + _k)
    _w += _k
NCONST = _w


def shape_constants():
    c = np.zeros((P, NCONST), np.float32)

    def put(name, a):
        c[:a.shape[0], _C[name][0]:_C[name][0] + a.shape[1]] = a

    r = np.arange(P)
    put("ident", np.eye(P, dtype=np.float32))
    i = ((r % DH1) // 2).astype(np.float32)
    theta = np.power(np.float32(10000.0), np.float32(-2.0) * (i - np.float32(1.0)) / np.float32(DH1))
    ang = (np.arange(S, dtype=np.float32)[None, :] * theta[:, None].astype(np.float32)).astype(np.float32)
    put("cos", np.cos(ang))
    put("sin", np.sin(ang) * np.where(r % 2 == 0, -1.0, 1.0)[:, None].astype(np.float32))
    scale2 = DH2 ** -0.5
    put("par", np.stack([(r // DH1) % 2 == 0, (r // DH1) % 2 == 1, (r < DH2) * scale2, (r >= DH2) * scale2]
                    + [r // 32 == j for j in range(JP)], 1))
    r2, k2 = np.arange(2 * S), np.arange(S)
    put("keep", ((r2 % S)[:, None] <= k2[None, :]).astype(np.float32))
    put("cbias", np.where(k2[None, :] > (r2 % S)[:, None], -BIG, 0.0).astype(np.float32))
    put("blk2", ((r2 // S)[:, None] == np.arange(32)[None, :] // DH1).astype(np.float32))
    put("blk3", (np.arange(R)[:, None] // S == np.arange(GI)[None, :]).astype(np.float32))
    put("rank", np.tile(np.arange(NE, 0, -1, dtype=np.float32), (P, 1)))
    rows = np.zeros((3, 2 * R), np.float32)
    rows[0, :R] = 1.0
    rows[1, :R] = np.arange(R) % S == 0
    rows[2, R:] = 1.0
    put("rowsel", rows)
    put("hsel", (np.arange(NH2 * NE)[:, None] // NE == np.arange(NH2)[None, :]).astype(np.float32))
    return c


def bcast(ap, axis, n):
    v = ap.unsqueeze(axis)
    shape = list(v.shape)
    shape[axis] = n
    return v.to_broadcast(shape)


def vit_block(nc, x, tokw, vecs, consts, wqkv, wout, w2, ve, oe, out):
    with ExitStack() as ctx:
        def sem(name):
            return ctx.enter_context(nc.semaphore(name))

        def sbuf(stack, name, shape, dt=F32, side="left"):
            return stack.enter_context(nc.sbuf_tensor(name, shape, dt, side=side))

        cst = sbuf(ctx, "cst", [P, NCONST])
        ident_bf = sbuf(ctx, "ident_bf", [P, P], BF16)
        mask_sel = sbuf(ctx, "mask_sel", [NH2 * NE, C2, NE, 2, DH2], BF16)
        gate_sel = sbuf(ctx, "gate_sel", [NH2 * NE, NH2, DH2])
        ones = sbuf(ctx, "ones", [P, P])
        half_neg = sbuf(ctx, "half_neg", [P, GI])
        h = sbuf(ctx, "h", [R, G, D])
        W2C = 2 * NH2 * DH2 + NH2 * NE
        w2hi = sbuf(ctx, "w2hi", [P, KC, W2C], F32R)
        w2lo = sbuf(ctx, "w2lo", [P, KC, W2C], F32R)
        NVR = 2
        veraw = sbuf(ctx, "veraw", [P, NVR, KC, NH2 * DH2])
        vehi = sbuf(ctx, "vehi", [P, NVR, KC, NH2 * DH2], F32R)
        velo = sbuf(ctx, "velo", [P, NVR, KC, NH2 * DH2], F32R)
        stat6 = sbuf(ctx, "stat6", [R, 2, 6])
        mv = sbuf(ctx, "mv", [R, 2, G, 2])
        lnv = sbuf(ctx, "lnv", [R, 2, G])
        rstd = sbuf(ctx, "rstd", [R, 2, G])
        xhat = sbuf(ctx, "xhat", [R, 2, D])

        first = ExitStack()
        proj = ExitStack()
        x1hi = sbuf(proj, "x1hi", [P, KC, TP], F32R, "right")
        x1lo = sbuf(proj, "x1lo", [P, KC, TP], F32R, "right")
        wqhi = sbuf(proj, "wqhi", [P, KC, 5, D], F32R, "right")
        wqlo = sbuf(proj, "wqlo", [P, KC, 5, D], F32R, "right")
        wo = sbuf(first, "wo", [P, KC, D])
        biasb = sbuf(first, "biasb", [R, 2, D])
        vsplit = sbuf(first, "vsplit", [R, 2, G, PAIRS, 2, DH1])
        tok = ExitStack()
        xp = sbuf(tok, "xp", [R, G, DIN])
        sqjunk = sbuf(tok, "sqjunk", [R, 2, DIN])
        NQB = 3
        qb = sbuf(tok, "qb", [R, NQB, DIN], BF16)
        qT = sbuf(tok, "qT", [P, 2, DC, R + 1], BF16)
        tw = sbuf(tok, "tw", [P, DC * D])
        tern = sbuf(tok, "tern", [P, DC * D], BF16)
        vrow = sbuf(tok, "vrow", [3, D])
        wqraw = sbuf(tok, "wqraw", [P, KC, 5, D])
        w2raw = sbuf(tok, "w2raw", [P, KC, W2C])
        small = sbuf(tok, "small", [P, 8])
        amax = sbuf(tok, "amax", [R, G])
        ssq = sbuf(tok, "ssq", [R, G])
        msq = sbuf(tok, "msq", [R, G])
        rrms = sbuf(tok, "rrms", [R, G])
        amn = sbuf(tok, "amn", [R, G])
        amc = sbuf(tok, "amc", [R, G])
        iam = sbuf(tok, "iam", [R, G])
        qsc = sbuf(tok, "qsc", [R, G])
        dqs = sbuf(tok, "dqs", [R, G])
        tok.close()
        raw = sbuf(first, "raw", [P, KC, 4, T])
        ropet = sbuf(first, "ropet", [P, T])
        qun = sbuf(first, "qun", [P, KC, B, JP, S])
        qrot = sbuf(first, "qrot", [P, KC, B, JP, S])
        kun = sbuf(first, "kun", [P, KC, B, 2, S])
        krot = sbuf(first, "krot", [P, KC, B, 2, S])
        vblk = sbuf(first, "vblk", [2 * S, B, PAIRS, 2, DH1])
        proj.close()
        soft = ExitStack()
        en = sbuf(soft, "en", [2 * S, 2, BI, KC, JP, S], F32, "right")
        ed = sbuf(soft, "ed", [2 * S, BI, KC, JP, S], F32, "right")
        rden = sbuf(soft, "rden", [P, UN * S], F32, "right")
        yT = sbuf(soft, "yT", [P, KC, TP], F32, "right")
        soft.close()
        first.close()

        last = ctx
        v2 = sbuf(last, "v2", [R, G, NH2, DH2])
        x2hi = sbuf(ctx, "x2hi", [P, KC, TP], F32R)
        x2lo = sbuf(ctx, "x2lo", [P, KC, TP], F32R)
        h1T = sbuf(last, "h1T", [P, KC, TP])
        ez = sbuf(last, "ez", [R, 2, NH2 * NE])
        gate = sbuf(last, "gate", [R, 2, NH2, NE])
        gtop = sbuf(last, "gtop", [R, G, NH2])
        geq = sbuf(last, "geq", [R, 2, NH2, NE])
        grk = sbuf(last, "grk", [R, 2, NH2])
        onehot = sbuf(last, "onehot", [R, G, NH2, NE], U8)
        gm = sbuf(last, "gm", [R, G, NH2, NE])
        gmT = sbuf(last, "gmT", [NH2 * NE, TP])
        maskT = sbuf(last, "maskT", [NH2 * NE, TP], BF16)
        gateb = sbuf(last, "gateb", [P, C2, T])
        sc = sbuf(last, "sc", [2 * S, 2, C2 * GI, S])
        pe2 = sbuf(last, "pe2", [2 * S, 2, C2 * GI, S])
        mx2 = sbuf(last, "mx2", [2 * S, 2, C2 * GI])
        sm2 = sbuf(last, "sm2", [2 * S, 2, C2 * GI])
        rs2 = sbuf(last, "rs2", [2 * S, 2, C2 * GI])
        ptb = sbuf(last, "ptb", [R, G, NH2, GI, S])
        ot = sbuf(last, "ot", [P, T])
        oThi = sbuf(last, "oThi", [P, C2, T], F32R)
        oTlo = sbuf(last, "oTlo", [P, C2, T], F32R)
        NGR = 2
        ghi = sbuf(last, "ghi", [P, NGR, 2, HALF], F32R)
        glo = sbuf(last, "glo", [P, NGR, 2, HALF], F32R)
        yo = sbuf(last, "yo", [P, KC, 2, HALF])
        qk = ExitStack()
        q2 = sbuf(qk, "q2", [P, C2, B, 2, S])
        k2 = sbuf(qk, "k2", [P, C2, T])
        qk.close()
        NOR = 2
        oeraw = sbuf(last, "oeraw", [P, NOR, OEU, D])
        oehi = sbuf(last, "oehi", [P, NOR, OEU, D], F32R)
        oelo = sbuf(last, "oelo", [P, NOR, OEU, D], F32R)

        ps = ctx.enter_context(nc.psum_tensor("ps", [P, 8, 512], F32))

        x_in = [sem(f"x_in{g}") for g in range(G)]
        tokw_in, const_in, vec_in, wqkv_in, w2_in, wout_in = (
            sem(n) for n in ("tokw_in", "const_in", "vec_in", "wqkv_in", "w2_in", "wout_in"))
        ve_in = [sem(f"ve_in{e}") for e in range(NVR)]
        oe_in = [sem(f"oe_in{e}") for e in range(NOR)]
        out_done = sem("out_done")
        v_in = sem("v_in")
        names = """pool_setup ident_ready bias_ps bias_sb wabs tot_ps wscale clip_t tern_pre tern_ready sq_done msq_ready rrms_ready
            qpar amaxed yround_ready qb_ready qT_ps qT_sb proj_ps h0_ready lnv_ready rstd_ready xhat_ready x1T_ps x1hi_ready
            x1lo_ready wqhi_ready wqlo_ready w2hi_ready w2lo_ready proj_sb rope_t proj1_ps vsplit_zero qun_ready
            s_ps exp_ready en_ready pv_ps den_ps rden_ready yT_ready yT_pad op_ps h0b_ready h1_ready x2T_ps x2hi_ready
            x2lo_ready qk2_ps qk2_ready gate_ps ez_ready gchain gm_ready gmT_ps gmT_ready maskT_ready gateb_ps gateb_ready
            s2_ps sc_ready e2_ready schain p2_ready p2n pt_ps ptb_ready vehi_ready velo_ready ve_ps sel0_ready sel_ready
            v2_ready aux_ps aux_done oT_tmp oT_hi g_ready main_ps oehi_ready oelo_ready acc_done out_ready qchain lnchain""".split()
        sm = {n: sem(n) for n in names}

        def cols(name, rows=P):
            a, b = _C[name]
            return cst[0:rows, a:b]

        def images(g):
            return min(GI, B - g * GI)

        def split3(pe, o, lhi, llo, rhi, rlo, start, stop):
            pe.matmul(o, llo, rhi, start=start, stop=False)
            pe.matmul(o, lhi, rlo, start=False, stop=False)
            return pe.matmul(o, lhi, rhi, start=False, stop=stop)

        PJ = []
        for hf in range(2):
            PJ += [("qk", hf, c, kind) for c in range(KC) for kind in range(4)]
            PJ += [("v", g, 0, 0) for g in range(hf * GI, hf * GI + GI)]
        NPJ, NEARLY = len(PJ), KC * 4
        PJB = [6 + n % 2 if n < NEARLY else 4 + n % 4 for n in range(NPJ)]
        PJPREV = [max([m for m in range(n) if PJB[m] == PJB[n]], default=-1) for n in range(NPJ)]

        def raw_jobs(hf, c):
            n = PJ.index(("qk", hf, c, 0))
            return n + 2, n + 4

        QK2 = [(hf, u) for hf in range(2) for u in range(2 * C2)]
        block = ctx.enter_context(nc.Block())

        AUX = []
        for c in range(C2):
            if c == 0:
                AUX.append(("pv", 0))
            for e in range(NE):
                AUX.append(("mask", c * NE + e))
                if e == NE - 4 and c + 1 < C2:
                    AUX.append(("pv", c + 1))
        mask_at = {k: n for n, (kind, k) in enumerate(AUX) if kind == "mask"}

        OPB = (0, 1, 4, 5, 6, 7)
        SOFT = [G + 1 + G * g for g in range(G)]

        @block.sync
        def _(sp):
            sp.dma_start(xp[:, 0, :], x[0]).then_inc(x_in[0], 16)
            sp.dma_start(tw[:], tokw).then_inc(tokw_in, 16)
            sp.dma_start(xp[:, 1, :], x[1]).then_inc(x_in[1], 16)
            sp.dma_start(cst[:], consts).then_inc(const_in, 16)
            sp.dma_start(vrow[:], vecs).then_inc(vec_in, 16)
            for g in range(2, G):
                sp.dma_start(xp[:, g, :], x[g]).then_inc(x_in[g], 16)
            sp.dma_start(wqraw[:], wqkv).then_inc(wqkv_in, 16)
            sp.dma_start(w2raw[:], w2).then_inc(w2_in, 16)
            sp.dma_start(wo[:], wout).then_inc(wout_in, 16)
            for e in range(NVR):
                sp.dma_start(veraw[:, e], ve[e]).then_inc(ve_in[e], 16)
            sp.wait_ge(sm["proj_sb"], NPJ)
            for ii in range(GI):
                for p_ in range(2):
                    ng = len(range(ii, B, GI))
                    sp.dma_start(vblk[p_ * S:(p_ + 1) * S, ii::GI], vsplit[ii * S:(ii + 1) * S, p_, 0:ng]).then_inc(
                        v_in, 16)
            for e in range(NVR, NE):
                sp.wait_ge(sm["vehi_ready"], e - NVR + 1)
                sp.wait_ge(sm["velo_ready"], e - NVR + 1)
                sp.dma_start(veraw[:, e % NVR], ve[e]).then_inc(ve_in[e % NVR], 16)
            for u in range(NOU):
                if u == 0:
                    sp.wait_ge(sm["s2_ps"], G)
                if u >= NOR:
                    sp.wait_ge(sm["oehi_ready"], u - NOR + 1)
                    sp.wait_ge(sm["oelo_ready"], u - NOR + 1)
                sp.dma_start(oeraw[:, u % NOR], oe[u]).then_inc(oe_in[u % NOR], 16)
            for m in range(KC):
                sp.wait_ge(sm["out_ready"], m + 1)
                sp.dma_start(out[m], yo[:, m]).then_inc(out_done, 16)
            sp.wait_ge(out_done, 16 * KC)

        @block.gpsimd
        def _(pool):
            pool.memset(ones[:], 1.0).then_inc(sm["pool_setup"], 1)
            pool.memset(half_neg[:], -0.5).then_inc(sm["pool_setup"], 1)
            pool.wait_ge(sm["pool_setup"], 2)

            pool.memset(vsplit[:], 0.0).then_inc(sm["vsplit_zero"], 1)

            def qkv_lo(b):
                pool.wait_ge(sm["wqhi_ready"], b + 1)
                pool.tensor_tensor(wqlo[:, :, b], wqraw[:, :, b], wqhi[:, :, b].bitcast(F32),
                                   ALU.subtract).then_inc(sm["wqlo_ready"], 1)

            for b in range(2):
                pool.wait_ge(sm["msq_ready"], b + 1)
                s_ = slice(GI * b, GI * b + GI)
                pool.tensor_tensor(rrms[:, s_], msq[:, s_], half_neg[0:R, :], ALU.pow).then_inc(sm["rrms_ready"], 1)
            def w2_lo(n):
                pool.wait_ge(sm["w2hi_ready"], n + 1)
                part = slice(n % 2 * W2C // 2, (n % 2 + 1) * W2C // 2)
                pool.tensor_tensor(w2lo[:, n // 2, part], w2raw[:, n // 2, part], w2hi[:, n // 2, part].bitcast(F32),
                                   ALU.subtract).then_inc(sm["w2lo_ready"], 1)

            for g in range(G):
                pool.wait_ge(sm["lnv_ready"], g + 1)
                pool.tensor_tensor(rstd[:, 0, g:g + 1], lnv[:, 0, g:g + 1], half_neg[0:R, 0:1],
                                   ALU.pow).then_inc(sm["rstd_ready"], 1)
                if g < 5:
                    qkv_lo(g)
            for n in range(4):
                w2_lo(n)
            for g in range(G):
                pool.wait_ge(sm["xhat_ready"], g + 1)
                pool.tensor_tensor(h[:, g], h[:, g], biasb[:, 1], ALU.add).then_inc(sm["h0b_ready"], 1)
            pool.wait_ge(const_in, 16)
            for c in range(C2):
                src = cst[0:NH2 * NE, c * 16:(c + 1) * 16].rearrange("q (j e) -> q e j", j=2)
                pool.tensor_copy(mask_sel[:, c], bcast(src, 3, DH2)).then_inc(sm["pool_setup"], 1)
            pool.tensor_copy(gate_sel[:], bcast(cols("hsel", NH2 * NE), 2, DH2)).then_inc(sm["pool_setup"], 1)

            def ve_lo(e):
                if e >= NVR:
                    pool.wait_ge(sm["ve_ps"], G * (e - NVR + 1))
                pool.wait_ge(sm["vehi_ready"], e + 1)
                pool.tensor_tensor(velo[:, e % NVR], veraw[:, e % NVR], vehi[:, e % NVR].bitcast(F32),
                                   ALU.subtract).then_inc(sm["velo_ready"], 1)

            for e in range(NVR):
                ve_lo(e)
            for g in range(G):
                pool.wait_ge(sm["lnv_ready"], G + g + 1)
                pool.tensor_tensor(rstd[:, 1, g:g + 1], lnv[:, 1, g:g + 1], half_neg[0:R, 0:1],
                                   ALU.pow).then_inc(sm["rstd_ready"], 1)
            for e in range(NVR, NE):
                ve_lo(e)
            for u in range(NOU):
                if u >= NOR:
                    pool.wait_ge(sm["main_ps"], OEU * (u - NOR + 1))
                pool.wait_ge(sm["oehi_ready"], u + 1)
                pool.tensor_tensor(oelo[:, u % NOR], oeraw[:, u % NOR], oehi[:, u % NOR].bitcast(F32),
                                   ALU.subtract).then_inc(sm["oelo_ready"], 1)

        @block.scalar
        def _(act):
            def square(g):
                act.wait_ge(x_in[g], 16)
                if g >= 2:
                    act.wait_ge(sm["sq_done"], g - 1)
                act.activation(sqjunk[:, g % 2], xp[:, g], ACT.Square,
                               accum_out=ssq[:, g:g + 1]).then_inc(sm["sq_done"], 1)

            def round_up(g):
                act.wait_ge(sm["qpar"], g // GI + 1)
                act.activation(xp[:, g], xp[:, g], ACT.Copy, bias=ROUND,
                               scale=qsc[:, g:g + 1]).then_inc(sm["yround_ready"], 1)

            def x1_hi(g):
                act.wait_ge(sm["x1T_ps"], g + 1)
                act.activation(x1hi[:, :, g * R:(g + 1) * R],
                               ps[:, 4 + g % 2, 0:KC * R].rearrange("p (c t) -> p c t", c=KC),
                               ACT.Copy).then_inc(sm["x1hi_ready"], 1)

            for g in range(G):
                square(g)
            act.wait_ge(sm["tern_pre"], 1)
            act.activation(tern[:], tw[:], ACT.Copy, bias=-ROUND).then_inc(sm["tern_ready"], 1)
            for g in range(G):
                round_up(g)
            act.wait_ge(wqkv_in, 16)
            for b in range(5):
                act.activation(wqhi[:, :, b], wqraw[:, :, b], ACT.Copy).then_inc(sm["wqhi_ready"], 1)

            def w2_hi(n):
                part = slice(n % 2 * W2C // 2, (n % 2 + 1) * W2C // 2)
                act.wait_ge(w2_in, 16)
                act.activation(w2hi[:, n // 2, part], w2raw[:, n // 2, part], ACT.Copy).then_inc(sm["w2hi_ready"], 1)

            for g in range(G):
                x1_hi(g)
                if g < 4:
                    w2_hi(g)

            def proj_evac(n):
                kind_, a, c, kind = PJ[n]
                act.wait_ge(sm["proj1_ps"], n + 1)
                if kind_ == "qk":
                    if n == 0:
                        act.wait_ge(sm["w2lo_ready"], 4)
                        act.wait_ge(sm["x1lo_ready"], G)
                    act.activation(raw[:, c, kind, a * HALF:(a + 1) * HALF], ps[:, PJB[n], 0:HALF],
                                   ACT.Copy).then_inc(sm["proj_sb"], 1)
                else:
                    act.wait_ge(sm["vsplit_zero"], 1)
                    src = ps[0:R, PJB[n], 0:D].rearrange("p (h a b) -> p h a b", h=PAIRS, a=2)
                    act.activation(vsplit[:, 0, a, :, 0], src[:, :, 0], ACT.Copy)
                    act.activation(vsplit[:, 1, a, :, 1], src[:, :, 1], ACT.Copy).then_inc(sm["proj_sb"], 1)

            def q_strips(hf, c):
                col, im = slice(hf * HALF, (hf + 1) * HALF), slice(hf * B // 2, (hf + 1) * B // 2)
                act.wait_ge(sm["proj_sb"], raw_jobs(hf, c)[0])
                for j in range(JP):
                    act.activation(qun[:, c, im, j], raw[:, c, 0, col].rearrange("p (i s) -> p i s", s=S), ACT.Copy,
                                   scale=cols("par")[:, 4 + j:5 + j]).then_inc(sm["qun_ready"], 1)

            for n, job in enumerate(PJ):
                proj_evac(n)
                if job[0] == "qk" and job[3] == 3:
                    q_strips(job[1], job[2])

            def ve_hi(e):
                act.wait_ge(ve_in[e % NVR], 16 * (e // NVR + 1))
                if e >= NVR:
                    act.wait_ge(sm["ve_ps"], G * (e - NVR + 1))
                act.activation(vehi[:, e % NVR], veraw[:, e % NVR], ACT.Copy).then_inc(sm["vehi_ready"], 1)

            for e in range(NVR):
                ve_hi(e)
            for b in range(NB):
                for kind in range(2):
                    act.wait_ge(sm["s_ps"], 2 * b + kind + 1)
                    if kind == 0 and b >= 2:
                        act.wait_ge(sm["pv_ps"], b - 1)
                    if kind == 1 and b >= 1:
                        act.wait_ge(sm["den_ps"], b)
                    dst = (en[:, b % 2] if kind == 0 else ed[:]).rearrange("p i c j s -> p i (c j s)")
                    act.activation(dst, ps[0:2 * S, 0:BI, 0:KC * JP * S], ACT.Exp,
                                   scale=DH1 ** -0.5).then_inc(sm["exp_ready"], 1)
            for g in range(G):
                act.wait_ge(sm["x2T_ps"], g + 1)
                src = ps[:, 2 + g % 2, 0:2 * KC * R].rearrange("p (a c t) -> p a c t", a=2, c=KC)
                act.activation(h1T[:, :, g * R:(g + 1) * R], src[:, 1], ACT.Copy)
                act.activation(x2hi[:, :, g * R:(g + 1) * R], src[:, 0], ACT.Copy).then_inc(sm["x2hi_ready"], 1)
            for g in range(2):
                act.wait_ge(sm["gate_ps"], g + 1)
                act.activation(ez[:, g % 2], ps[0:R, g % 2, 0:NH2 * NE], ACT.Exp, scale=-1.0).then_inc(sm["ez_ready"], 1)
            for n in range(4 * C2):
                hf, u = QK2[n]
                act.wait_ge(sm["qk2_ps"], n + 1)
                src, col = ps[:, 4 + n % 4, 0:HALF], slice(hf * HALF, (hf + 1) * HALF)
                if u < C2:
                    act.activation(k2[:, u, col], src, ACT.Copy).then_inc(sm["qk2_ready"], 1)
                else:
                    for p_ in range(2):
                        ins = act.activation(q2[:, u - C2, 8 * hf:8 * hf + 8, p_], src.rearrange("p (i s) -> p i s", s=S), ACT.Copy,
                                             scale=cols("par")[:, 2 + p_:3 + p_])
                    ins.then_inc(sm["qk2_ready"], 1)
                if n % 4 == 3:
                    g = 2 + n // 4
                    act.wait_ge(sm["gate_ps"], g + 1)
                    act.wait_ge(sm["gm_ready"], g - 1)
                    act.activation(ez[:, g % 2], ps[0:R, g % 2, 0:NH2 * NE], ACT.Exp,
                                   scale=-1.0).then_inc(sm["ez_ready"], 1)

            def first_expert(g):
                act.wait_ge(sm["ve_ps"], g + 1)
                act.activation(v2[:, g].rearrange("p a b -> p (a b)"), ps[0:R, 4 + g % 4, :],
                               ACT.Copy).then_inc(sm["sel0_ready"], 1)

            def exp2(g):
                act.wait_ge(sm["sc_ready"], g + 1)
                if g >= 2:
                    act.wait_ge(sm["p2_ready"], g - 1)
                n = C2 * images(g)
                act.activation(pe2[:, g % 2, 0:n], sc[:, g % 2, 0:n], ACT.Exp).then_inc(sm["e2_ready"], 1)

            def gmT_evac(g):
                act.wait_ge(sm["gmT_ps"], g + 1)
                act.activation(gmT[:, g * R:(g + 1) * R], ps[0:NH2 * NE, g % 2, 0:R], ACT.Copy).then_inc(sm["gmT_ready"], 1)

            for g in range(G):
                first_expert(g)
                gmT_evac(g)
            ve_hi(NVR)
            for n in range(2 * C2):
                c, hf = n // 2, n % 2
                act.wait_ge(sm["gateb_ps"], n + 1)
                act.activation(gateb[:, c, hf * HALF:(hf + 1) * HALF], ps[:, hf, 0:HALF],
                               ACT.Copy).then_inc(sm["gateb_ready"], 1)
            for g in range(G):
                exp2(g)
                if g + NVR + 1 < NE:
                    ve_hi(g + NVR + 1)

            for u in range(NOU):
                act.wait_ge(oe_in[u % NOR], 16 * (u // NOR + 1))
                if u >= NOR:
                    act.wait_ge(sm["main_ps"], OEU * (u - NOR + 1))
                act.activation(oehi[:, u % NOR], oeraw[:, u % NOR], ACT.Copy).then_inc(sm["oehi_ready"], 1)

        @block.vector
        def _(dve):
            count = {}

            def step(name, ins):
                count[name] = count.get(name, 0) + 1
                ins.then_inc(sm[name], 1)
                dve.wait_ge(sm[name], count[name])

            def absmax(g):
                dve.wait_ge(x_in[g], 16)
                dve.tensor_reduce(amax[:, g:g + 1], xp[:, g], AX, ALU.max,
                                  apply_absolute_value=True).then_inc(sm["amaxed"], 1)

            def mean_square(b):
                dve.wait_ge(sm["sq_done"], GI * (b + 1))
                s_ = slice(GI * b, GI * b + GI)
                dve.tensor_scalar(msq[:, s_], ssq[:, s_], 1.0 / DIN, 1e-6, ALU.mult,
                                  ALU.add).then_inc(sm["msq_ready"], 1)

            def quant_scales(b):
                dve.wait_ge(sm["rrms_ready"], b + 1)
                s_ = slice(GI * b, GI * b + GI)
                step("qchain", dve.tensor_tensor(amn[:, s_], amax[:, s_], rrms[:, s_], ALU.mult))
                step("qchain", dve.tensor_scalar(amc[:, s_], amn[:, s_], Q_EPS, None, ALU.max))
                step("qchain", dve.reciprocal(iam[:, s_], amc[:, s_]))
                dve.scalar_tensor_tensor(out=qsc[:, s_], in0=rrms[:, s_], scalar=127.0, in1=iam[:, s_],
                                         op0=ALU.mult, op1=ALU.mult).then_inc(sm["qpar"], 1)
                step("qchain", dve.tensor_scalar(dqs[:, s_], amc[:, s_], small[0:R, 3:4], None, ALU.mult))

            for g in range(GI):
                absmax(g)
                if g == 0:
                    dve.wait_ge(tokw_in, 16)
                    dve.tensor_reduce(small[:, 0:1], tw[:], AX, ALU.add,
                                      apply_absolute_value=True).then_inc(sm["wabs"], 1)
            dve.wait_ge(const_in, 16)
            dve.tensor_copy(ident_bf[:], cols("ident")).then_inc(sm["ident_ready"], 1)
            dve.wait_ge(sm["amaxed"], GI)
            mean_square(0)
            dve.wait_ge(sm["tot_ps"], 1)
            step("wscale", dve.tensor_scalar(small[:, 1:2], ps[:, 6, 0:1], 1.0 / (D * DIN), Q_EPS, ALU.mult, ALU.max))
            step("wscale", dve.reciprocal(small[:, 2:3], small[:, 1:2]))
            step("wscale", dve.tensor_scalar(small[:, 3:4], small[:, 1:2], 1.0 / 127.0, None, ALU.mult))
            step("clip_t", dve.tensor_scalar(tw[:], tw[:], small[:, 2:3], 1.0, ALU.mult, ALU.min))
            dve.tensor_scalar(tw[:], tw[:], -1.0, ROUND, ALU.max, ALU.add).then_inc(sm["tern_pre"], 1)
            for g in range(GI, G):
                absmax(g)
            dve.wait_ge(sm["amaxed"], G)
            mean_square(1)
            quant_scales(0)
            dve.wait_ge(sm["bias_ps"], 1)
            step("bias_sb", dve.tensor_copy(biasb[:], ps[0:R, 7, :].rearrange("p (a d) -> p a d", a=2)))
            quant_scales(1)

            def quantised(g):
                dve.wait_ge(sm["yround_ready"], g + 1)
                if g >= NQB:
                    dve.wait_ge(sm["qT_ps"], g - NQB + 1)
                dve.tensor_scalar(qb[:, g % NQB], xp[:, g], ROUND, 127.0, ALU.subtract,
                                  ALU.min).then_inc(sm["qb_ready"], 1)

            def quantised_T(g):
                dve.wait_ge(sm["qT_ps"], g + 1)
                if g >= 2:
                    dve.wait_ge(sm["proj_ps"], g - 1)
                src = ps[:, g % 2, :].bitcast(BF16)[:, 0:DC * (R + 1)].rearrange("p (c t) -> p c t", c=DC)
                dve.tensor_copy(qT[:, g % 2, :, 0:R], src[:, :, 0:R]).then_inc(sm["qT_sb"], 1)

            def ln_stats(which, g):
                step("lnchain", dve.bn_stats(stat6[:, which], h[:, g]))
                step("lnchain", dve.bn_aggr(mv[:, which, g], stat6[:, which]))
                dve.tensor_scalar(lnv[:, which, g:g + 1], mv[:, which, g, 1:2], 1e-5, None,
                                  ALU.add).then_inc(sm["lnv_ready"], 1)

            def ln_apply(which, g):
                n = which * G + g
                dve.wait_ge(sm["rstd_ready"], n + 1)
                if g >= 2:
                    dve.wait_ge(sm["x2T_ps" if which else "x1T_ps"], g - 1)
                dve.tensor_scalar(xhat[:, g % 2], h[:, g], mv[:, which, g, 0:1], rstd[:, which, g:g + 1],
                                  ALU.subtract, ALU.mult).then_inc(sm["xhat_ready"], 1)

            def embed(g):
                dve.wait_ge(sm["proj_ps"], g + 1)
                step("h0_ready", dve.scalar_tensor_tensor(
                    out=h[:, g], in0=ps[0:R, 2 + g % 2, 0:D], scalar=dqs[:, g:g + 1], in1=biasb[:, 0],
                    op0=ALU.mult, op1=ALU.add))
                ln_stats(0, g)

            def x1_lo(g):
                dve.wait_ge(sm["x1hi_ready"], g + 1)
                tc = slice(g * R, (g + 1) * R)
                dve.tensor_tensor(x1lo[:, :, tc], ps[:, 4 + g % 2, 0:KC * R].rearrange("p (c t) -> p c t", c=KC),
                                  x1hi[:, :, tc].bitcast(F32), ALU.subtract).then_inc(sm["x1lo_ready"], 1)

            for s_ in range(G + 5):
                if s_ < G:
                    quantised(s_)
                if 0 <= s_ - 1 < G:
                    quantised_T(s_ - 1)
                if 0 <= s_ - 2 < G:
                    embed(s_ - 2)
                if 0 <= s_ - 3 < G:
                    ln_apply(0, s_ - 3)
                if 0 <= s_ - 5 < G:
                    x1_lo(s_ - 5)

            def rope(hf, c):
                col, im = slice(hf * HALF, (hf + 1) * HALF), slice(hf * B // 2, (hf + 1) * B // 2)

                def by_image(a):
                    return a.rearrange("p (i s) -> p i s", s=S)

                def many(ins):
                    ins.then_inc(sm["rope_t"], 1)
                    count["rope_t"] = count.get("rope_t", 0) + 1

                tmp = by_image(ropet[:, col])
                cos, sin = bcast(cols("cos"), 1, B // 2), bcast(cols("sin"), 1, B // 2)
                for kind in (0, 2):
                    dve.wait_ge(sm["proj_sb"], raw_jobs(hf, c)[kind // 2])
                    own, other = by_image(raw[:, c, kind, col]), by_image(raw[:, c, kind + 1, col])
                    many(dve.tensor_tensor(tmp, own, cos, ALU.mult))
                    step("rope_t", dve.tensor_tensor(other, other, sin, ALU.mult))
                    step("rope_t", dve.tensor_tensor(tmp, tmp, other, ALU.add))
                    if kind == 0:
                        for j in range(JP):
                            many(dve.tensor_scalar(qrot[:, c, im, j], tmp, cols("par")[:, 4 + j:5 + j], None, ALU.mult))
                    else:
                        for p_ in range(2):
                            sel = cols("par")[:, p_:p_ + 1]
                            many(dve.tensor_scalar(krot[:, c, im, p_], tmp, sel, None, ALU.mult))
                            many(dve.tensor_scalar(kun[:, c, im, p_], own, sel, None, ALU.mult))
                    dve.wait_ge(sm["rope_t"], count["rope_t"])

            for hf in range(2):
                for c in range(KC):
                    rope(hf, c)
            dve.wait_ge(sm["proj1_ps"], NPJ)
            dve.memset(yT[:, :, T:TP], 0.0).then_inc(sm["yT_pad"], 1)

            def causal(b):
                dve.wait_ge(sm["exp_ready"], 2 * b + 1)
                v = en[:, b % 2].rearrange("p i c j s -> p (i c j) s")
                dve.tensor_tensor(v, v, bcast(cols("keep", 2 * S), 1, JP * UN), ALU.mult).then_inc(sm["en_ready"], 1)

            def normalise(b):
                o = 4 + 2 * (b % 2)
                if b:
                    dve.wait_ge(sm["yT_ready"], b)
                dve.wait_ge(sm["den_ps"], b + 1)
                step("rden_ready", dve.reciprocal(rden[:], ps[:, o + 1, 0:UN * S]))
                dve.wait_ge(sm["pv_ps"], b + 1)
                dve.tensor_tensor(yT[:, :, b * BI * S:(b + 1) * BI * S],
                                  ps[:, o, 0:UN * S].rearrange("p (c t) -> p c t", c=KC),
                                  rden[:].rearrange("p (c t) -> p c t", c=KC), ALU.mult).then_inc(sm["yT_ready"], 1)

            for b in range(NB):
                causal(b)
                if b:
                    normalise(b - 1)
            normalise(NB - 1)

            def residual(g):
                dve.wait_ge(sm["op_ps"], g + 1)
                dve.wait_ge(sm["h0b_ready"], g + 1)
                step("h1_ready", dve.tensor_tensor(h[:, g], h[:, g], ps[0:R, OPB[g], 0:D], ALU.add))
                ln_stats(1, g)

            def x2_lo(g):
                dve.wait_ge(sm["x2hi_ready"], g + 1)
                tc = slice(g * R, (g + 1) * R)
                dve.tensor_tensor(x2lo[:, :, tc], ps[:, 2 + g % 2, 0:KC * R].rearrange("p (c t) -> p c t", c=KC),
                                  x2hi[:, :, tc].bitcast(F32), ALU.subtract).then_inc(sm["x2lo_ready"], 1)

            for s_ in range(G + 3):
                if s_ < G:
                    residual(s_)
                if 0 <= s_ - 1 < G:
                    ln_apply(1, s_ - 1)
                if 0 <= s_ - 3 < G:
                    x2_lo(s_ - 3)

            def gates(g):
                k = g % 2
                dve.wait_ge(sm["ez_ready"], g + 1)
                z = ez[:, k]
                step("gchain", dve.tensor_scalar(z, z, 1.0, None, ALU.add))
                step("gchain", dve.reciprocal(gate[:, k].rearrange("p a b -> p (a b)"), z))
                step("gchain", dve.tensor_reduce(gtop[:, g], gate[:, k], AX, ALU.max))
                step("gchain", dve.tensor_tensor(geq[:, k], gate[:, k], bcast(gtop[:, g], 2, NE), ALU.is_equal))
                step("gchain", dve.tensor_tensor(geq[:, k], geq[:, k], bcast(cols("rank", R), 1, NH2), ALU.mult))
                step("gchain", dve.tensor_reduce(grk[:, k], geq[:, k], AX, ALU.max))
                step("gchain", dve.tensor_tensor(onehot[:, g], geq[:, k], bcast(grk[:, k], 2, NE), ALU.is_equal))
                dve.tensor_tensor(gm[:, g], onehot[:, g], gate[:, k], ALU.mult).then_inc(sm["gm_ready"], 1)

            def softmax_a(g):
                k, n = g % 2, C2 * images(g)
                dve.wait_ge(sm["s2_ps"], g + 1)
                src = ps[0:2 * S, 2 + g % 2, 0:n * S].rearrange("p (u s) -> p u s", s=S)
                step("schain", dve.tensor_tensor(sc[:, k, 0:n], src, bcast(cols("cbias", 2 * S), 1, n), ALU.add))
                step("schain", dve.tensor_reduce(mx2[:, k, 0:n], sc[:, k, 0:n], AX, ALU.max))
                dve.tensor_tensor(sc[:, k, 0:n], sc[:, k, 0:n], bcast(mx2[:, k, 0:n], 2, S),
                                  ALU.subtract).then_inc(sm["sc_ready"], 1)

            def softmax_b(g):
                k, n = g % 2, C2 * images(g)
                dve.wait_ge(sm["e2_ready"], g + 1)
                step("schain", dve.tensor_reduce(sm2[:, k, 0:n], pe2[:, k, 0:n], AX, ALU.add))
                step("schain", dve.reciprocal(rs2[:, k, 0:n], sm2[:, k, 0:n]))
                if g >= 2:
                    dve.wait_ge(sm["pt_ps"], g - 1)
                dve.tensor_tensor(pe2[:, k, 0:n], pe2[:, k, 0:n], bcast(rs2[:, k, 0:n], 2, S),
                                  ALU.mult).then_inc(sm["p2_ready"], 1)

            def spread_p(g):
                m = images(g) * S
                ni = images(g)
                dve.wait_ge(sm["pt_ps"], g + 1)
                src = ps[0:m, g % 2, 0:NH2 * S].rearrange("p (h s) -> p h s", h=NH2)
                dve.tensor_tensor(ptb[0:m, g, :, 0:ni], bcast(src, 2, ni),
                                  bcast(bcast(cols("blk3", m)[:, 0:ni], 1, NH2), 3, S),
                                  ALU.mult).then_inc(sm["ptb_ready"], 1)

            def mask_rows(g):
                dve.wait_ge(sm["gmT_ready"], g + 1)
                tc = slice(g * R, (g + 1) * R)
                dve.tensor_scalar(maskT[:, tc], gmT[:, tc], 0.0, None, ALU.is_gt).then_inc(sm["maskT_ready"], 1)

            def select(e, g):
                n = e * G + g
                dve.wait_ge(sm["ve_ps"], n + 1)
                if e == 1:
                    dve.wait_ge(sm["sel0_ready"], g + 1)
                else:
                    dve.wait_ge(sm["sel_ready"], (e - 2) * G + g + 1)
                dve.copy_predicated(v2[:, g], bcast(onehot[:, g, :, e], 2, DH2),
                                    ps[0:R, 4 + n % 4, :].rearrange("p (a b) -> p a b", a=NH2)).then_inc(sm["sel_ready"], 1)

            for g in range(G):
                gates(g)
            for g in range(G):
                mask_rows(g)
            for e in range(1, NE):
                for g in range(G):
                    select(e, g)
                    for f, lag in ((softmax_a, 1), (softmax_b, 3), (spread_p, 5)):
                        for gg in range(G):
                            if SOFT[gg] + lag == e * G + g:
                                f(gg)
                    if e == NE - 1:
                        dve.wait_ge(sm["sel_ready"], (NE - 2) * G + g + 1)
                        dve.tensor_tensor(v2[:, g], v2[:, g], bcast(gtop[:, g], 2, DH2),
                                          ALU.mult).then_inc(sm["v2_ready"], 1)

            for n, (kind, k) in enumerate(AUX):
                o = 4 + 2 * (n % 2)
                dve.wait_ge(sm["aux_ps"], n + 1)
                if kind == "pv":
                    if k == 0:
                        dve.wait_ge(sm["gateb_ready"], 2 * C2)
                    A = GI * R
                    dve.tensor_tensor(ot[:, 0:A], ps[:, o, 0:A], gateb[:, k, 0:A], ALU.mult)
                    dve.tensor_tensor(ot[:, A:T], ps[:, o + 1, 0:T - A], gateb[:, k, A:T],
                                      ALU.mult).then_inc(sm["aux_done"], 1)
                    dve.wait_ge(sm["aux_done"], n + 1)
                    step("oT_hi", dve.tensor_copy(oThi[:, k], ot[:]))
                    step("oT_hi", dve.tensor_tensor(oTlo[:, k], ot[:], oThi[:, k].bitcast(F32), ALU.subtract))
                else:
                    c = k // NE
                    if k >= NGR:
                        dve.wait_ge(sm["main_ps"], k - NGR + 1)
                    msk = ps[:, o:o + 2, 0:HALF]
                    dve.tensor_tensor(ghi[:, k % NGR], msk, oThi[:, c].bitcast(F32).rearrange(
                        "p (a t) -> p a t", a=2), ALU.mult).then_inc(sm["g_ready"], 1)
                    dve.tensor_tensor(glo[:, k % NGR], msk, oTlo[:, c].bitcast(F32).rearrange(
                        "p (a t) -> p a t", a=2), ALU.mult).then_inc(sm["aux_done"], 1)
            for m in range(KC):
                dve.wait_ge(sm["acc_done"], m + 1)
                dve.tensor_tensor(yo[:, m], ps[:, 2 * m:2 * m + 2, 0:HALF],
                                  h1T[:, m, 0:T].rearrange("p (a t) -> p a t", a=2), ALU.add).then_inc(sm["out_ready"], 1)

        @block.tensor
        def _(pe):
            pe.wait_ge(const_in, 16)
            pe.wait_ge(vec_in, 16)
            for a in range(2):
                ins = pe.matmul(ps[0:R, 7, a * D:(a + 1) * D], cols("rowsel", 3)[:, a * R:(a + 1) * R], vrow[:],
                                start=True, stop=True)
            ins.then_inc(sm["bias_ps"], 1)
            pe.wait_ge(sm["pool_setup"], 2)
            pe.wait_ge(sm["wabs"], 1)
            pe.matmul(ps[:, 6, 0:1], ones[:], small[:, 0:1], start=True, stop=True).then_inc(sm["tot_ps"], 1)

            def turn_q(g):
                pe.wait_ge(sm["qb_ready"], g + 1)
                if g == 0:
                    pe.wait_ge(sm["ident_ready"], 1)
                if g >= 2:
                    pe.wait_ge(sm["qT_sb"], g - 1)
                dst = ps[:, g % 2, :].bitcast(BF16)
                for c in range(DC):
                    ins = pe.transpose(dst[:, c * (R + 1):c * (R + 1) + R], qb[:, g % NQB, c * P:(c + 1) * P],
                                       ident_bf[0:R, 0:R])
                ins.then_inc(sm["qT_ps"], 1)

            def embed(g):
                pe.wait_ge(sm["qT_sb"], g + 1)
                if g == 0:
                    pe.wait_ge(sm["tern_ready"], 1)
                if g >= 2:
                    pe.wait_ge(sm["h0_ready"], g - 1)
                for c in range(DC):
                    ins = pe.matmul(ps[0:R, 2 + g % 2, 0:D], qT[:, g % 2, c, 0:R], tern[:, c * D:(c + 1) * D],
                                    start=(c == 0), stop=(c == DC - 1))
                ins.then_inc(sm["proj_ps"], 1)

            def turn_x(g):
                pe.wait_ge(sm["xhat_ready"], g + 1)
                if g >= 2:
                    pe.wait_ge(sm["x1lo_ready"], g - 1)
                for c in range(KC):
                    ins = pe.transpose(ps[:, 4 + g % 2, c * R:(c + 1) * R], xhat[:, g % 2, c * P:(c + 1) * P],
                                       cst[0:R, 0:R])
                ins.then_inc(sm["x1T_ps"], 1)

            WB = (0, 2, 1, 3)

            def proj_job(n):
                kind_, a, c, kind = PJ[n]
                pe.wait_ge(sm["x1lo_ready"], min(G, GI + GI * (n >= NEARLY + GI)) if kind_ == "qk" or a < GI else G)
                pe.wait_ge(sm["wqlo_ready"], 5)
                if PJPREV[n] >= 0:
                    pe.wait_ge(sm["proj_sb"], PJPREV[n] + 1)
                elif PJB[n] >= 6:
                    pe.wait_ge(sm["bias_sb"], 1)
                if n == NEARLY:
                    pe.wait_ge(sm["x1lo_ready"], G)
                for k in range(KC):
                    if kind_ == "qk":
                        wb, tc, col = WB[kind], slice(a * HALF, (a + 1) * HALF), slice(c * P, (c + 1) * P)
                        ins = split3(pe, ps[:, PJB[n], 0:HALF], wqhi[:, k, wb, col], wqlo[:, k, wb, col],
                                     x1hi[:, k, tc], x1lo[:, k, tc], k == 0, k == KC - 1)
                    else:
                        tc = slice(a * R, (a + 1) * R)
                        ins = split3(pe, ps[0:R, PJB[n], 0:D], x1hi[:, k, tc], x1lo[:, k, tc],
                                     wqhi[:, k, 4], wqlo[:, k, 4], k == 0, k == KC - 1)
                ins.then_inc(sm["proj1_ps"], 1)

            for s_ in range(G + 4):
                if s_ < G:
                    turn_q(s_)
                if 0 <= s_ - 1 < G:
                    embed(s_ - 1)
                if 0 <= s_ - 4 < G:
                    turn_x(s_ - 4)
            for n in range(NPJ):
                proj_job(n)

            def scores(b, kind):
                n = 2 * b + kind
                if n == 0:
                    pe.wait_ge(sm["h0_ready"], G)
                    pe.wait_ge(sm["qT_sb"], G)
                else:
                    pe.wait_ge(sm["exp_ready"], n)
                late = b * BI * 2 // B + 1
                pe.wait_ge(sm["rope_t"], 14 * KC * late)
                pe.wait_ge(sm["qun_ready"], KC * JP * late)
                for ii in range(BI):
                    i = b * BI + ii
                    for c in range(KC):
                        key = (kun if kind else krot)[:, c, i].rearrange("p a b -> p (a b)")
                        qry = (qun if kind else qrot)[:, c, i].rearrange("p a b -> p (a b)")
                        ins = pe.matmul(ps[0:2 * S, ii, c * JP * S:(c + 1) * JP * S], key, qry, start=True, stop=True)
                ins.then_inc(sm["s_ps"], 1)

            def attend(b):
                pe.wait_ge(sm["en_ready"], b + 1)
                if b == 0:
                    pe.wait_ge(sm["proj_sb"], NPJ)
                    pe.wait_ge(v_in, 16 * 2 * GI)
                if b >= 2:
                    pe.wait_ge(sm["yT_ready"], b - 1)
                for c in range(KC):
                    for ii in range(BI):
                        u = c * BI + ii
                        for j in range(JP):
                            vv = vblk[:, b * BI + ii, c * JP + j].rearrange("p a b -> p (a b)")
                            ins = pe.matmul(ps[32 * j:32 * j + 32, 4 + 2 * (b % 2), u * S:(u + 1) * S], vv,
                                            en[:, b % 2, ii, c, j], start=True, stop=True)
                ins.then_inc(sm["pv_ps"], 1)

            def denominators(b):
                pe.wait_ge(sm["exp_ready"], 2 * b + 2)
                if b >= 2:
                    pe.wait_ge(sm["yT_ready"], b - 1)
                for j in range(JP):
                    ins = pe.matmul(ps[32 * j:32 * j + 32, 5 + 2 * (b % 2), 0:UN * S], cols("blk2", 2 * S),
                                    ed[:, :, :, j].rearrange("p i c s -> p c i s"), start=True, stop=True)
                ins.then_inc(sm["den_ps"], 1)

            for b in range(NB):
                scores(b, 0)
                if b:
                    denominators(b - 1)
                scores(b, 1)
                attend(b)
            denominators(NB - 1)

            def out_proj(g):
                if g == 0:
                    pe.wait_ge(sm["exp_ready"], 2 * NB)
                    pe.wait_ge(wout_in, 16)
                    pe.wait_ge(sm["yT_pad"], 1)
                pe.wait_ge(sm["yT_ready"], min(NB, -(-(g + 1) * R // (BI * S))))
                for k in range(KC):
                    ins = pe.matmul(ps[0:R, OPB[g], 0:D], yT[:, k, g * R:(g + 1) * R], wo[:, k],
                                    start=(k == 0), stop=(k == KC - 1))
                ins.then_inc(sm["op_ps"], 1)

            def turn_x2(g):
                pe.wait_ge(sm["xhat_ready"], G + g + 1)
                if g >= 2:
                    pe.wait_ge(sm["x2lo_ready"], g - 1)
                for a in range(2):
                    for c in range(KC):
                        src = (h[:, g] if a else xhat[:, g % 2])[:, c * P:(c + 1) * P]
                        o = (a * KC + c) * R
                        ins = pe.transpose(ps[:, 2 + g % 2, o:o + R], src, cst[0:R, 0:R])
                ins.then_inc(sm["x2T_ps"], 1)

            for s_ in range(G + 2):
                if s_ < G:
                    out_proj(s_)
                if 0 <= s_ - 2 < G:
                    turn_x2(s_ - 2)

            NQ = NH2 * DH2

            def gate_job(g):
                if g < 2:
                    pe.wait_ge(sm["h1_ready"], g + 1)
                else:
                    pe.wait_ge(sm["ez_ready"], g - 1)
                pe.wait_ge(sm["x2lo_ready"], g + 1)
                tc = slice(g * R, (g + 1) * R)
                for k in range(KC):
                    ins = split3(pe, ps[0:R, g % 2, 0:NH2 * NE], x2hi[:, k, tc], x2lo[:, k, tc],
                                 w2hi[:, k, 2 * NQ:], w2lo[:, k, 2 * NQ:], k == 0, k == KC - 1)
                ins.then_inc(sm["gate_ps"], 1)

            pe.wait_ge(sm["w2lo_ready"], 4)
            gate_job(0)
            gate_job(1)
            for n in range(4 * C2):
                hf, u = QK2[n]
                if n < 4:
                    pe.wait_ge(sm["h1_ready"], n + 3)
                else:
                    pe.wait_ge(sm["qk2_ready"], n - 3)
                base = (NQ if u < C2 else 0) + (u % C2) * P
                tc = slice(hf * HALF, (hf + 1) * HALF)
                pe.wait_ge(sm["x2lo_ready"], 3 if hf == 0 else G)
                for k in range(KC):
                    ins = split3(pe, ps[:, 4 + n % 4, 0:HALF], w2hi[:, k, base:base + P], w2lo[:, k, base:base + P],
                                 x2hi[:, k, tc], x2lo[:, k, tc], k == 0, k == KC - 1)
                ins.then_inc(sm["qk2_ps"], 1)
                if n % 4 == 1:
                    gate_job(2 + n // 4)

            def value_job(e, g):
                n = e * G + g
                if n < 4:
                    pe.wait_ge(sm["qk2_ready"], 4 * C2)
                elif n - 4 < G:
                    pe.wait_ge(sm["sel0_ready"], n - 3)
                else:
                    pe.wait_ge(sm["sel_ready"], n - 4 - G + 1)
                if g == 0:
                    pe.wait_ge(sm["velo_ready"], e + 1)
                tc = slice(g * R, (g + 1) * R)
                for k in range(KC):
                    ins = split3(pe, ps[0:R, 4 + n % 4, :], x2hi[:, k, tc], x2lo[:, k, tc],
                                 vehi[:, e % NVR, k], velo[:, e % NVR, k], k == 0, k == KC - 1)
                ins.then_inc(sm["ve_ps"], 1)

            def turn_gates(g):
                pe.wait_ge(sm["gm_ready"], g + 1)
                if g < 2:
                    pe.wait_ge(sm["ez_ready"], G)
                else:
                    pe.wait_ge(sm["gmT_ready"], g - 1)
                pe.transpose(ps[0:NH2 * NE, g % 2, 0:R], gm[:, g].rearrange("p a b -> p (a b)"),
                             cst[0:R, 0:R]).then_inc(sm["gmT_ps"], 1)

            def gate_rows(n):
                c, hf = n // 2, n % 2
                if n < 2:
                    pe.wait_ge(sm["gmT_ready"], G)
                    pe.wait_ge(sm["pool_setup"], 2 + C2 + 1)
                else:
                    pe.wait_ge(sm["gateb_ready"], n - 1)
                pe.matmul(ps[:, hf, 0:HALF], gate_sel[:, 2 * c:2 * c + 2].rearrange("p a b -> p (a b)"),
                          gmT[:, hf * HALF:(hf + 1) * HALF], start=True, stop=True).then_inc(sm["gateb_ps"], 1)

            def scores2(g):
                if g < 2:
                    pe.wait_ge(sm["x2lo_ready"], G)
                else:
                    pe.wait_ge(sm["sc_ready"], g - 1)
                ni = images(g)
                for c in range(C2):
                    for ii in range(ni):
                        i = g * GI + ii
                        tc = slice(i * S, (i + 1) * S)
                        u = c * ni + ii
                        ins = pe.matmul(ps[0:2 * S, 2 + g % 2, u * S:(u + 1) * S], q2[:, c, i].rearrange("p a b -> p (a b)"), k2[:, c, tc],
                                        start=True, stop=True)
                ins.then_inc(sm["s2_ps"], 1)

            def turn_p(g):
                pe.wait_ge(sm["p2_ready"], g + 1)
                if g < 2:
                    pe.wait_ge(sm["gateb_ready"], 2 * C2)
                else:
                    pe.wait_ge(sm["ptb_ready"], g - 1)
                ni = images(g)
                for c in range(C2):
                    src = pe2[:, g % 2, c * ni:(c + 1) * ni].rearrange("p u s -> p (u s)")
                    ins = pe.transpose(ps[0:ni * S, g % 2, c * 2 * S:(c + 1) * 2 * S], src, cst[0:2 * S, 0:2 * S])
                ins.then_inc(sm["pt_ps"], 1)

            for g in range(G):
                value_job(0, g)
                turn_gates(g)
            for e in range(1, NE):
                for g in range(G):
                    value_job(e, g)
                    n = e * G + g
                    if G <= n < G + C2:
                        gate_rows(2 * (n - G))
                        gate_rows(2 * (n - G) + 1)
                    for gg in range(G):
                        if SOFT[gg] == n:
                            scores2(gg)
                        if SOFT[gg] + 4 == n:
                            turn_p(gg)

            def aux(n):
                kind, k = AUX[n]
                o = 4 + 2 * (n % 2)
                if n < 2:
                    pe.wait_ge(sm["v2_ready"], G)
                else:
                    pe.wait_ge(sm["aux_done"], n - 1)
                if kind == "pv":
                    pe.wait_ge(sm["ptb_ready"], G)
                    for g in range(G):
                        ni = images(g)
                        m = ni * S
                        for p_ in range(2):
                            hd = 2 * k + p_
                            q0 = (g % GI) * R
                            ins = pe.matmul(ps[DH2 * p_:DH2 * p_ + DH2, o + g // GI, q0:q0 + m], v2[0:m, g, hd],
                                            ptb[0:m, g, hd, 0:ni].rearrange("p a b -> p (a b)"), start=True, stop=True)
                else:
                    c, e = k // NE, k % NE
                    if k == 0:
                        pe.wait_ge(sm["maskT_ready"], G)
                    for hf in range(2):
                        ins = pe.matmul(ps[:, o + hf, 0:HALF], mask_sel[:, c, e].rearrange("p a b -> p (a b)"),
                                        maskT[:, hf * HALF:(hf + 1) * HALF], start=True, stop=True)
                ins.then_inc(sm["aux_ps"], 1)

            def main(k):
                u = k // OEU
                pe.wait_ge(sm["oelo_ready"], u + 1)
                pe.wait_ge(sm["aux_done"], mask_at[k] + 1)
                if k == 0:
                    pe.wait_ge(sm["ptb_ready"], G)
                for m in range(KC):
                    col = slice(m * P, (m + 1) * P)
                    w_hi, w_lo = oehi[:, u % NOR, k % OEU, col], oelo[:, u % NOR, k % OEU, col]
                    s0, s1 = k == 0, k == C2 * NE - 1
                    for hf in range(2):
                        o = ps[:, 2 * m + hf, 0:HALF]
                        g_hi, g_lo = ghi[:, k % NGR, hf], glo[:, k % NGR, hf]
                        ins = split3(pe, o, w_hi, w_lo, g_hi, g_lo, s0, s1)
                    if s1:
                        ins.then_inc(sm["acc_done"], 1)
                if not s1:
                    ins.then_inc(sm["main_ps"], 1)

            done = 0
            for k in range(C2 * NE):
                ahead = mask_at[min(k + 1, C2 * NE - 1)]
                while done <= ahead:
                    aux(done)
                    done += 1
                main(k)


def kernel(**inputs):
    import concourse.bacc as bacc
    from concourse.bass_utils import run_bass_kernel_spmd

    x = np.asarray(inputs["x"])
    patches = x.reshape(B, CH, SIDE, PATCH, SIDE, PATCH).transpose(0, 2, 4, 3, 5, 1).reshape(B, NPATCH, DIN)
    rows = np.zeros((G * GI, S, DIN), np.float32)
    rows[:B, 1:] = patches
    tokw = np.asarray(inputs["L0_tok_weight"]).T.reshape(DC, P, D).transpose(1, 0, 2).reshape(P, DC * D)
    vecs = np.concatenate([np.asarray(inputs["L0_tok_pos_embedding"]).reshape(1, D),
                           np.asarray(inputs["L0_tok_class_token"]).reshape(1, D),
                           np.asarray(inputs["L0_attn_bout"]).reshape(1, D)])
    w = np.asarray(inputs["L0_attn_Wqkv"])
    wq, wk, wv = w[:, :D], w[:, D:2 * D], w[:, 2 * D:]
    swap = np.arange(D) ^ 1
    wqkv = np.stack([wq, wk, wq[:, swap], wk[:, swap], wv], 1).reshape(KC, P, 5, D).transpose(1, 0, 2, 3)
    wout = np.asarray(inputs["L0_attn_Wout"]).reshape(KC, P, D).transpose(1, 0, 2)
    w2 = np.concatenate([np.asarray(inputs["L0_ffn_w_q"]), np.asarray(inputs["L0_ffn_w_k"]),
                         np.asarray(inputs["L0_ffn_w_gate"])], 1).reshape(KC, P, -1).transpose(1, 0, 2)
    ve = np.asarray(inputs["L0_ffn_value_experts"]).transpose(0, 2, 1, 3)
    ve = ve.reshape(NE, KC, P, NH2 * DH2).transpose(0, 2, 1, 3)
    oe = np.asarray(inputs["L0_ffn_output_experts"]).reshape(NE, C2, 2 * DH2, D).transpose(1, 0, 2, 3)
    oe = oe.reshape(C2, NE // OEU, OEU, P, D).transpose(0, 1, 3, 2, 4).reshape(NOU, P, OEU, D)
    arrays = {"x_rows": rows.reshape(G, R, DIN), "tok_weight": tokw, "vectors": vecs, "constants": shape_constants(),
              "w_qkv": wqkv, "w_out": wout, "w_qkgate": w2, "value_w": ve, "output_w": oe}
    arrays = {n: np.ascontiguousarray(a) for n, a in arrays.items()}

    nc = bacc.Bacc("TRN2", target_bir_lowering=False, num_devices=1)
    args = [nc.dram_tensor(n, a.shape, F32, kind="ExternalInput").ap() for n, a in arrays.items()]
    out = nc.dram_tensor("out", [KC, P, 2, HALF], F32, kind="ExternalOutput").ap()
    vit_block(nc, *args, out)
    r = run_bass_kernel_spmd(nc, [arrays], core_ids=[0])
    y = r.results[0]["out"].reshape(D, T)
    return np.ascontiguousarray(y.T).reshape(B, S, D)
```

```python
from contextlib import ExitStack

import numpy as np

import concourse.bass as bass
from concourse import mybir
from concourse.alu_op_type import AluOpType as ALU

ACT = mybir.ActivationFunctionType
AX = mybir.AxisListType.X
F32 = mybir.dt.float32
F32R = mybir.dt.float32r
BF16 = mybir.dt.bfloat16
U8 = mybir.dt.uint8

P = 128
B, CH, IMG, PATCH = 16, 3, 96, 16
SIDE = IMG // PATCH
NPATCH = SIDE * SIDE
S = NPATCH + 1
D = 256
KC = D // P
DIN = PATCH * PATCH * CH
DC = DIN // P
T = B * S
GI = 3
G = -(-B // GI)
R = GI * S
TP = G * R
NT = -(-T // P)
HALF = T // 2
NH1, DH1 = 16, 16
PAIRS = NH1 // 2
JP = 4
BI = 4
NB = B // BI
UN = KC * BI
NH2, DH2, NE = 8, 64, 8
C2 = NH2 // 2
OEU = 4
NOU = C2 * NE // OEU
MEU = 2
NMU = C2 * NE // MEU
NMR = 4
TI = [range(t * P // S, (min((t + 1) * P, T) - 1) // S + 1) for t in range(NT)]
TI_MAX = max(len(i) for i in TI)
TROWS = [min(P, T - t * P) for t in range(NT)]
ROUND = 12582912.0
Q_EPS = 1e-5
BIG = 3.0e38

_C = {}
_w = 0
for _n, _k in (("ident", 128), ("cos", S), ("sin", S), ("par", 8), ("keep", S), ("cbias", S),
               ("blk2", 32), ("blk", NT * TI_MAX), ("rank", NE), ("rowsel", 2 * R), ("hsel", NH2)):
    _C[_n] = (_w, _w + _k)
    _w += _k
NCONST = _w


def shape_constants():
    c = np.zeros((P, NCONST), np.float32)

    def put(name, a):
        c[:a.shape[0], _C[name][0]:_C[name][0] + a.shape[1]] = a

    r = np.arange(P)
    put("ident", np.eye(P, dtype=np.float32))
    i = ((r % DH1) // 2).astype(np.float32)
    theta = np.power(np.float32(10000.0), np.float32(-2.0) * (i - np.float32(1.0)) / np.float32(DH1))
    ang = (np.arange(S, dtype=np.float32)[None, :] * theta[:, None].astype(np.float32)).astype(np.float32)
    put("cos", np.cos(ang))
    put("sin", np.sin(ang) * np.where(r % 2 == 0, -1.0, 1.0)[:, None].astype(np.float32))
    scale2 = DH2 ** -0.5
    put("par", np.stack([(r // DH1) % 2 == 0, (r // DH1) % 2 == 1, (r < DH2) * scale2, (r >= DH2) * scale2]
                    + [r // 32 == j for j in range(JP)], 1))
    r2, k2 = np.arange(2 * S), np.arange(S)
    put("keep", ((r2 % S)[:, None] <= k2[None, :]).astype(np.float32))
    put("cbias", np.where(k2[None, :] > (r2 % S)[:, None], -BIG, 0.0).astype(np.float32))
    put("blk2", ((r2 // S)[:, None] == np.arange(32)[None, :] // DH1).astype(np.float32))
    put("blk", np.concatenate([(t * P + r)[:, None] // S == t * P // S + np.arange(TI_MAX)[None, :]
                               for t in range(NT)], 1).astype(np.float32))
    put("rank", np.tile(np.arange(NE, 0, -1, dtype=np.float32), (P, 1)))
    rows = np.zeros((3, 2 * R), np.float32)
    rows[0, :R] = 1.0
    rows[1, :R] = np.arange(R) % S == 0
    rows[2, R:] = 1.0
    put("rowsel", rows)
    put("hsel", (np.arange(NH2 * NE)[:, None] // NE == np.arange(NH2)[None, :]).astype(np.float32))
    return c


def bcast(ap, axis, n):
    v = ap.unsqueeze(axis)
    shape = list(v.shape)
    shape[axis] = n
    return v.to_broadcast(shape)


def vit_block(nc, x, tokw, vecs, consts, wqkv, wout, w2, ve, oe, mask_rows, out):
    with ExitStack() as ctx:
        def sem(name):
            return ctx.enter_context(nc.semaphore(name))

        def sbuf(stack, name, shape, dt=F32, side="left"):
            return stack.enter_context(nc.sbuf_tensor(name, shape, dt, side=side))

        cst = sbuf(ctx, "cst", [P, NCONST])
        ident_bf = sbuf(ctx, "ident_bf", [P, P], BF16)
        gate_sel = sbuf(ctx, "gate_sel", [NH2 * NE, NH2, DH2], F32R)
        ones = sbuf(ctx, "ones", [P, P])
        half_neg = sbuf(ctx, "half_neg", [P, GI])
        h = sbuf(ctx, "h", [R, G, D])
        W2C = 2 * NH2 * DH2 + NH2 * NE
        w2s = ExitStack()
        w2hi = sbuf(w2s, "w2hi", [P, KC, W2C], F32R, "right")
        w2lo = sbuf(w2s, "w2lo", [P, KC, W2C], F32R, "right")
        NVR = 2
        veraw = sbuf(ctx, "veraw", [P, NVR, KC, NH2 * DH2])
        vehi = sbuf(ctx, "vehi", [P, NVR, KC, NH2 * DH2], F32R)
        velo = sbuf(ctx, "velo", [P, NVR, KC, NH2 * DH2], F32R)
        stat6 = sbuf(ctx, "stat6", [R, 2, 6])
        mv = sbuf(ctx, "mv", [R, 2, G, 2])
        lnv = sbuf(ctx, "lnv", [R, 2, G])
        rstd = sbuf(ctx, "rstd", [R, 2, G])
        xhat = sbuf(ctx, "xhat", [R, 2, D])

        first = ExitStack()
        proj = ExitStack()
        wqhi = sbuf(proj, "wqhi", [P, 5, KC, D], F32R, "right")
        wqlo = sbuf(proj, "wqlo", [P, 5, KC, D], F32R, "right")
        x1hi = sbuf(proj, "x1hi", [P, KC, TP], F32R, "right")
        x1lo = sbuf(proj, "x1lo", [P, KC, TP], F32R, "right")
        wo = sbuf(first, "wo", [P, KC, D])
        biasb = sbuf(first, "biasb", [R, 2, D])
        vsplit = sbuf(first, "vsplit", [R, 2, G, PAIRS, 2, DH1])
        tok = ExitStack()
        xp = sbuf(tok, "xp", [R, G, DIN])
        sqjunk = sbuf(tok, "sqjunk", [R, 2, DIN])
        NQB = 3
        qb = sbuf(tok, "qb", [R, NQB, DIN], BF16)
        qT = sbuf(tok, "qT", [P, 2, DC, R + 1], BF16)
        tw = sbuf(tok, "tw", [P, DC * D])
        tern = sbuf(tok, "tern", [P, DC * D], BF16)
        vrow = sbuf(tok, "vrow", [3, D])
        wqraw = sbuf(tok, "wqraw", [P, 5, KC, D])
        w2raw = sbuf(tok, "w2raw", [P, KC, W2C])
        small = sbuf(tok, "small", [P, 8])
        amax = sbuf(tok, "amax", [R, G])
        ssq = sbuf(tok, "ssq", [R, G])
        msq = sbuf(tok, "msq", [R, G])
        rrms = sbuf(tok, "rrms", [R, G])
        amn = sbuf(tok, "amn", [R, G])
        amc = sbuf(tok, "amc", [R, G])
        iam = sbuf(tok, "iam", [R, G])
        qsc = sbuf(tok, "qsc", [R, G])
        dqs = sbuf(tok, "dqs", [R, G])
        tok.close()
        raw = sbuf(first, "raw", [P, KC, 4, T])
        ropet = sbuf(first, "ropet", [P, T])
        qun = sbuf(first, "qun", [P, KC, B, JP, S])
        krot = sbuf(first, "krot", [P, KC, B, 2, S])
        vblk = sbuf(first, "vblk", [2 * S, B, PAIRS, 2, DH1])
        qrot = sbuf(first, "qrot", [P, KC, B, JP, S])
        kun = sbuf(first, "kun", [P, KC, B, 2, S])
        proj.close()
        soft = ExitStack()
        en = sbuf(soft, "en", [2 * S, 2, BI, KC, JP, S], F32, "right")
        ed = sbuf(soft, "ed", [2 * S, BI, KC, JP, S], F32, "right")
        rden = sbuf(soft, "rden", [P, UN * S], F32, "right")
        yT = sbuf(soft, "yT", [P, KC, TP], F32, "right")
        soft.close()
        first.close()

        last = ctx
        v2 = sbuf(last, "v2", [P, NT, NH2, DH2])
        x2hi = sbuf(ctx, "x2hi", [P, KC, TP], F32R)
        x2lo = sbuf(ctx, "x2lo", [P, KC, TP], F32R)
        h1T = sbuf(last, "h1T", [P, KC, TP])
        ez = sbuf(last, "ez", [P, NT, NH2 * NE])
        gate = sbuf(last, "gate", [P, NT, NH2, NE])
        gtop = sbuf(last, "gtop", [P, NT, NH2])
        geq = sbuf(last, "geq", [P, 2, NH2, NE])
        grk = sbuf(last, "grk", [P, 2, NH2])
        onehot = sbuf(last, "onehot", [P, NT, NH2, NE], U8)
        gm = sbuf(last, "gm", [P, NT, NH2, NE])
        gmThi = sbuf(last, "gmThi", [NH2 * NE, T], F32R)
        gmTlo = sbuf(last, "gmTlo", [NH2 * NE, T], F32R)
        maskT = sbuf(last, "maskT", [NH2 * NE, T], BF16)
        gateb = sbuf(last, "gateb", [P, C2, T])
        sc = sbuf(last, "sc", [2 * S, 2, C2 * GI, S])
        pe2 = sbuf(last, "pe2", [2 * S, 2, C2 * GI, S])
        mx2 = sbuf(last, "mx2", [2 * S, 2, C2 * GI])
        sm2 = sbuf(last, "sm2", [2 * S, 2, C2 * GI])
        rs2 = sbuf(last, "rs2", [2 * S, 2, C2 * GI])
        prob = sbuf(last, "prob", [2 * S, C2, T])
        ptb = sbuf(last, "ptb", [P, NT, NH2, TI_MAX, S])
        yo = sbuf(last, "yo", [P, KC, 2, HALF])
        qk = ExitStack()
        q2 = sbuf(qk, "q2", [P, C2, B, 2, S])
        k2 = sbuf(qk, "k2", [P, C2, T])
        qk.close()
        NOR = 2
        oeraw = sbuf(last, "oeraw", [P, NOR, OEU, D])
        oehi = sbuf(last, "oehi", [P, NOR, OEU, D], F32R)
        oelo = sbuf(last, "oelo", [P, NOR, OEU, D], F32R)
        maskb = sbuf(last, "maskb", [P, NMR, MEU, T], BF16)
        w2s.close()
        NGR = 3
        ot = sbuf(last, "ot", [P, T], F32, "right")
        oThi = sbuf(last, "oThi", [P, 2, T], F32R, "right")
        oTlo = sbuf(last, "oTlo", [P, 2, T], F32R, "right")
        ghi = sbuf(last, "ghi", [P, NGR, 2, HALF], F32R, "right")
        glo = sbuf(last, "glo", [P, NGR, 2, HALF], F32R, "right")

        ps = ctx.enter_context(nc.psum_tensor("ps", [P, 8, 512], F32))

        x_in = [sem(f"x_in{g}") for g in range(G)]
        tokw_in, const_in, vec_in, wqkv_in, w2_in, wout_in = (
            sem(n) for n in ("tokw_in", "const_in", "vec_in", "wqkv_in", "w2_in", "wout_in"))
        ve_in = [sem(f"ve_in{e}") for e in range(NVR)]
        oe_in = [sem(f"oe_in{e}") for e in range(NOR)]
        mask_out = sem("mask_out")
        mask_in = [sem(f"mask_in{w}") for w in range(NMR)]
        out_done = sem("out_done")
        v_in = sem("v_in")
        names = """pool_setup ident_ready bias_ps bias_sb wabs tot_ps wscale clip_t tern_pre tern_ready sq_done msq_ready rrms_ready
            qpar amaxed yround_ready qb_ready qT_ps qT_sb proj_ps h0_ready lnv_ready rstd_ready xhat_ready x1T_ps x1hi_ready
            x1lo_ready wqhi_ready wqlo_ready w2hi_ready w2lo_ready proj_sb rope_t proj1_ps vsplit_zero qun_ready kun_ready qT2_sb
            s_ps exp_ready en_ready pv_ps den_ps rden_ready yT_ready yT_pad op_ps h0b_ready h1_ready x2T_ps x2hi_ready
            x2lo_ready qk2_ps qk2_ready gate_ps ez_ready gchain gm_ready gmT_ps gmThi_ready gmTlo_ready maskT_ready gateb_ps gateb_ready
            s2_ps sc_ready sub_ready e2_ready schain rs_ready p2_ready pt_ps pv0_ps g0_ready pv2_ps ot_ready glo_ready ptb_ready vehi_ready velo_ready ve_ps sel0_ready sel_ready
            v2_ready oT_hi oThi_ready oTlo_ready g_ready main_ps oehi_ready oelo_ready acc_done out_ready qchain lnchain""".split()
        sm = {n: sem(n) for n in names}

        def cols(name, rows=P):
            a, b = _C[name]
            return cst[0:rows, a:b]

        def images(g):
            return min(GI, B - g * GI)

        def split3(pe, o, lhi, llo, rhi, rlo, start, stop):
            pe.matmul(o, llo, rhi, start=start, stop=False)
            pe.matmul(o, lhi, rlo, start=False, stop=False)
            return pe.matmul(o, lhi, rhi, start=False, stop=stop)

        PJ = []
        for hf in range(2):
            PJ += [("qk", hf, c, kind) for c in range(KC) for kind in range(4)]
            if hf == 0:
                PJ += [("v", g, 0, 0) for g in range(G)]
        NPJ, NEARLY = len(PJ), KC * 4
        PJB = [6 + n if n < 2 else 4 + n % 4 for n in range(NPJ)]
        PJPREV = [max([m for m in range(n) if PJB[m] == PJB[n]], default=-1) for n in range(NPJ)]

        def raw_jobs(hf, c):
            n = PJ.index(("qk", hf, c, 0))
            return n + 2, n + 4

        QK2 = [(hf, c, kind) for hf in range(2) for c in range(C2) for kind in "kq"]
        PV_AT = 1
        PVB = [4 + 2 * ((c - 1) % 2) for c in range(C2)]

        NOP = (NB - 1) * BI * S // R
        OPB = [(4 + g // 2, g % 2 * D) if g < NOP else (1, (g - NOP) * D) for g in range(G)]

        D_ORDER = [("turn", 0), ("turn", 1), ("turn", 2), ("gate", 0), ("qk", 0), ("out", 4), ("out", 5),
                   ("qk", 1), ("turn", 3), ("qk", 2), ("qk", 3), ("turn", 4), ("qk", 4), ("turn", 5),
                   ("gate", 1), ("qk", 5), ("qk", 6), ("gate", 2), ("qk", 7), ("gate", 3), ("qk", 8),
                   ("gate", 4)]
        D_ORDER += [("qk", n) for n in range(9, 4 * C2)]
        GATES = [range(t, min(t + 2, NT)) for t in range(0, NT, 2)]
        LAST = (NE - 1) * NT
        JOBS = [(e, t, 0, NH2) for e in range(NE - 1) for t in range(NT)]
        JOBS += [(NE - 1, t, k, k + NH2 // 2) for k in (0, NH2 // 2) for t in range(NT)]
        NJ = len(JOBS)
        JBANK = [4 + n % 4 for n in range(NJ)]
        JPREV = [max([m for m in range(n) if JBANK[m] == JBANK[n]], default=-1) for n in range(NJ)]
        SOFT = [NT - 1 + NT * g for g in range(G)]
        LAG_MAX, LAG_SUM, LAG_TURN = 1, 4, 8
        TILE_G = [TI[t][-1] // GI for t in range(NT)]

        def soft_at(n, lag):
            return [g for g in range(G) if SOFT[g] + lag == n]

        def turn_at(n):
            return [t for t in range(NT) if SOFT[TILE_G[t]] + LAG_TURN == n]

        def groups_of(t):
            return -(-min((t + 1) * P, T) // R)

        block = ctx.enter_context(nc.Block())

        @block.sync
        def _(sp):
            sp.dma_start(xp[:, 0, :], x[0]).then_inc(x_in[0], 16)
            sp.dma_start(tw[:], tokw).then_inc(tokw_in, 16)
            sp.dma_start(xp[:, 1, :], x[1]).then_inc(x_in[1], 16)
            sp.dma_start(cst[:], consts).then_inc(const_in, 16)
            sp.dma_start(vrow[:], vecs).then_inc(vec_in, 16)
            for g in range(2, G):
                sp.dma_start(xp[:, g, :], x[g]).then_inc(x_in[g], 16)
            sp.dma_start(wqraw[:], wqkv).then_inc(wqkv_in, 16)
            sp.dma_start(w2raw[:], w2).then_inc(w2_in, 16)
            sp.dma_start(wo[:], wout).then_inc(wout_in, 16)
            for e in range(NVR):
                sp.dma_start(veraw[:, e], ve[e]).then_inc(ve_in[e], 16)
            sp.wait_ge(sm["proj_sb"], NEARLY + G)
            sp.wait_ge(sm["w2lo_ready"], 4)
            for ii in range(GI):
                for p_ in range(2):
                    ng = len(range(ii, B, GI))
                    sp.dma_start(vblk[p_ * S:(p_ + 1) * S, ii::GI], vsplit[ii * S:(ii + 1) * S, p_, 0:ng]).then_inc(
                        v_in, 16)
            def ve_load(e):
                sp.wait_ge(sm["vehi_ready"], e - NVR + 1)
                sp.wait_ge(sm["velo_ready"], e - NVR + 1)
                sp.dma_start(veraw[:, e % NVR], ve[e]).then_inc(ve_in[e % NVR], 16)

            def oe_load(u):
                if u >= NOR:
                    sp.wait_ge(sm["oehi_ready"], u - NOR + 1)
                    sp.wait_ge(sm["oelo_ready"], u - NOR + 1)
                sp.dma_start(oeraw[:, u % NOR], oe[u]).then_inc(oe_in[u % NOR], 16)

            def mask_load(w):
                if w >= NMR:
                    sp.wait_ge(sm["glo_ready"], MEU * (w - NMR + 1))
                c, e = w * MEU // NE, w * MEU % NE
                for p_ in range(2):
                    r0 = (2 * c + p_) * NE + e
                    sp.dma_start(maskb[p_ * DH2:(p_ + 1) * DH2, w % NMR],
                                 bcast(mask_rows[r0:r0 + MEU], 0, DH2)).then_inc(mask_in[w % NMR], 16)

            ve_load(NVR)
            sp.wait_ge(sm["maskT_ready"], NT)
            sp.dma_start(mask_rows, maskT[:]).then_inc(mask_out, 16)
            ve_load(NVR + 1)
            sp.wait_ge(mask_out, 16)
            for e in range(NVR + 2, NE):
                ve_load(e)
            sp.wait_ge(sm["s2_ps"], G)
            oe_load(0)
            for w in range(NMR):
                mask_load(w)
            oe_load(1)
            oe_load(2)
            mask_load(NMR)
            for u in range(3, NOU):
                oe_load(u)
                mask_load(2 * u - 1)
                mask_load(2 * u)
            mask_load(NMU - 1)
            for m in range(KC):
                for hf in range(2):
                    sp.wait_ge(sm["out_ready"], 2 * m + hf + 1)
                    sp.dma_start(out[m, :, hf], yo[:, m, hf]).then_inc(out_done, 16)
            sp.wait_ge(out_done, 16 * 2 * KC)

        @block.gpsimd
        def _(pool):
            pool.memset(ones[:], 1.0).then_inc(sm["pool_setup"], 1)
            pool.memset(half_neg[:], -0.5).then_inc(sm["pool_setup"], 1)
            pool.wait_ge(sm["pool_setup"], 2)

            pool.memset(vsplit[:], 0.0).then_inc(sm["vsplit_zero"], 1)

            def qkv_lo(b):
                pool.wait_ge(sm["wqhi_ready"], b + 1)
                pool.tensor_tensor(wqlo[:, b], wqraw[:, b], wqhi[:, b].bitcast(F32),
                                   ALU.subtract).then_inc(sm["wqlo_ready"], 1)

            for b in range(2):
                pool.wait_ge(sm["msq_ready"], b + 1)
                s_ = slice(GI * b, GI * b + GI)
                pool.tensor_tensor(rrms[:, s_], msq[:, s_], half_neg[0:R, :], ALU.pow).then_inc(sm["rrms_ready"], 1)
            def w2_lo(n):
                pool.wait_ge(sm["w2hi_ready"], n + 1)
                part = slice(n % 2 * W2C // 2, (n % 2 + 1) * W2C // 2)
                pool.tensor_tensor(w2lo[:, n // 2, part], w2raw[:, n // 2, part], w2hi[:, n // 2, part].bitcast(F32),
                                   ALU.subtract).then_inc(sm["w2lo_ready"], 1)

            for g in range(G):
                pool.wait_ge(sm["lnv_ready"], g + 1)
                pool.tensor_tensor(rstd[:, 0, g:g + 1], lnv[:, 0, g:g + 1], half_neg[0:R, 0:1],
                                   ALU.pow).then_inc(sm["rstd_ready"], 1)
                if g < 5:
                    qkv_lo(g)
            for n in range(4):
                w2_lo(n)
            for g in range(G):
                pool.wait_ge(sm["xhat_ready"], g + 1)
                pool.tensor_tensor(h[:, g], h[:, g], biasb[:, 1], ALU.add).then_inc(sm["h0b_ready"], 1)
            for hf in range(2):
                for c in range(KC):
                    col, im = slice(hf * HALF, (hf + 1) * HALF), slice(hf * B // 2, (hf + 1) * B // 2)
                    pool.wait_ge(sm["proj_sb"], raw_jobs(hf, c)[1] - 1)
                    for p_ in range(2):
                        pool.tensor_scalar(kun[:, c, im, p_], raw[:, c, 2, col].rearrange("p (i s) -> p i s", s=S),
                                           cols("par")[:, p_:p_ + 1], None, ALU.mult).then_inc(sm["kun_ready"], 1)

            def ve_lo(e):
                if e >= NVR:
                    pool.wait_ge(sm["ve_ps"], NT * (e - NVR + 1))
                pool.wait_ge(sm["vehi_ready"], e + 1)
                pool.tensor_tensor(velo[:, e % NVR], veraw[:, e % NVR], vehi[:, e % NVR].bitcast(F32),
                                   ALU.subtract).then_inc(sm["velo_ready"], 1)

            for e in range(NVR):
                ve_lo(e)
            pool.wait_ge(const_in, 16)
            pool.tensor_copy(gate_sel[:], bcast(cols("hsel", NH2 * NE), 2, DH2)).then_inc(sm["pool_setup"], 1)
            for g in range(G):
                pool.wait_ge(sm["lnv_ready"], G + g + 1)
                pool.tensor_tensor(rstd[:, 1, g:g + 1], lnv[:, 1, g:g + 1], half_neg[0:R, 0:1],
                                   ALU.pow).then_inc(sm["rstd_ready"], 1)

            def less_max(g):
                k, n = g % 2, C2 * images(g)
                pool.wait_ge(sm["sc_ready"], g + 1)
                pool.tensor_tensor(sc[:, k, 0:n], sc[:, k, 0:n], bcast(mx2[:, k, 0:n], 2, S),
                                   ALU.subtract).then_inc(sm["sub_ready"], 1)

            def probabilities(g):
                k, ni = g % 2, images(g)
                n = C2 * ni
                pool.wait_ge(sm["rs_ready"], g + 1)
                pool.tensor_tensor(prob[:, :, g * R:g * R + ni * S].rearrange("p c (i s) -> p c i s", s=S),
                                   pe2[:, k, 0:n].rearrange("p (c i) s -> p c i s", c=C2),
                                   bcast(rs2[:, k, 0:n].rearrange("p (c i) -> p c i", c=C2), 3, S),
                                   ALU.mult).then_inc(sm["p2_ready"], 1)

            def oe_lo(u):
                if u >= NOR:
                    pool.wait_ge(sm["main_ps"], OEU * (u - NOR + 1))
                pool.wait_ge(sm["oehi_ready"], u + 1)
                pool.tensor_tensor(oelo[:, u % NOR], oeraw[:, u % NOR], oehi[:, u % NOR].bitcast(F32),
                                   ALU.subtract).then_inc(sm["oelo_ready"], 1)

            for n in range(NJ):
                if n == LAST - 1:
                    oe_lo(0)
                if n % NT == 0 and n // NT + NVR - 1 in range(NVR, NE) and n < LAST:
                    ve_lo(n // NT + NVR - 1)
                for g in soft_at(n, LAG_MAX):
                    less_max(g)
                for g in soft_at(n, LAG_SUM):
                    probabilities(g)
                if n >= LAST:
                    e, t, h0, h1 = JOBS[n]
                    m, hs = TROWS[t], slice(h0, h1)
                    pool.wait_ge(sm["sel_ready"], n - NT + 1)
                    pool.tensor_tensor(v2[0:m, t, hs], v2[0:m, t, hs], bcast(gtop[0:m, t, hs], 2, DH2),
                                       ALU.mult).then_inc(sm["v2_ready"], 1)

            def oT_lo(c):
                pool.wait_ge(sm["oThi_ready"], c)
                pool.tensor_tensor(oTlo[:, c % 2], ot[:], oThi[:, c % 2].bitcast(F32),
                                   ALU.subtract).then_inc(sm["oTlo_ready"], 1)

            for u in range(1, NOU):
                oe_lo(u)
                if u % 2 and u // 2 + 1 < C2:
                    oT_lo(u // 2 + 1)

        @block.scalar
        def _(act):
            def square(g):
                act.wait_ge(x_in[g], 16)
                if g >= 2:
                    act.wait_ge(sm["sq_done"], g - 1)
                act.activation(sqjunk[:, g % 2], xp[:, g], ACT.Square,
                               accum_out=ssq[:, g:g + 1]).then_inc(sm["sq_done"], 1)

            def round_up(g):
                act.wait_ge(sm["qpar"], g // GI + 1)
                act.activation(xp[:, g], xp[:, g], ACT.Copy, bias=ROUND,
                               scale=qsc[:, g:g + 1]).then_inc(sm["yround_ready"], 1)

            def quantised_T(g):
                act.wait_ge(sm["qT_ps"], g + 1)
                act.wait_ge(sm["proj_ps"], g - 1)
                src = ps[:, g % 2, :].bitcast(BF16)[:, 0:DC * (R + 1)].rearrange("p (c t) -> p c t", c=DC)
                act.activation(qT[:, g % 2, :, 0:R], src[:, :, 0:R], ACT.Copy).then_inc(sm["qT2_sb"], 1)

            def x1_hi(g):
                act.wait_ge(sm["x1T_ps"], g + 1)
                act.activation(x1hi[:, :, g * R:(g + 1) * R],
                               ps[:, 4 + g % 2, 0:KC * R].rearrange("p (c t) -> p c t", c=KC),
                               ACT.Copy).then_inc(sm["x1hi_ready"], 1)

            def wq_hi(b):
                act.wait_ge(wqkv_in, 16)
                act.activation(wqhi[:, b], wqraw[:, b], ACT.Copy).then_inc(sm["wqhi_ready"], 1)

            def w2_hi(n):
                part = slice(n % 2 * W2C // 2, (n % 2 + 1) * W2C // 2)
                act.wait_ge(w2_in, 16)
                act.activation(w2hi[:, n // 2, part], w2raw[:, n // 2, part], ACT.Copy).then_inc(sm["w2hi_ready"], 1)

            def proj_evac(n):
                kind_, a, c, kind = PJ[n]
                act.wait_ge(sm["proj1_ps"], n + 1)
                if kind_ == "qk":
                    if n == 0:
                        act.wait_ge(sm["qb_ready"], G)
                        act.wait_ge(sm["sq_done"], G)
                    act.activation(raw[:, c, kind, a * HALF:(a + 1) * HALF], ps[:, PJB[n], 0:HALF],
                                   ACT.Copy).then_inc(sm["proj_sb"], 1)
                else:
                    act.wait_ge(sm["vsplit_zero"], 1)
                    src = ps[0:R, PJB[n], 0:D].rearrange("p (h a b) -> p h a b", h=PAIRS, a=2)
                    act.activation(vsplit[:, 0, a, :, 0], src[:, :, 0], ACT.Copy)
                    act.activation(vsplit[:, 1, a, :, 1], src[:, :, 1], ACT.Copy).then_inc(sm["proj_sb"], 1)

            for g in range(G):
                square(g)
                if g == G // 2:
                    act.wait_ge(sm["bias_ps"], 1)
                    act.activation(biasb[:], ps[0:R, 7, :].rearrange("p (a d) -> p a d", a=2),
                                   ACT.Copy).then_inc(sm["bias_sb"], 1)
            round_up(0)
            act.wait_ge(sm["tern_pre"], 1)
            act.activation(tern[:], tw[:], ACT.Copy, bias=-ROUND).then_inc(sm["tern_ready"], 1)
            round_up(1)
            round_up(2)
            wq_hi(0)
            round_up(3)
            quantised_T(2)
            round_up(4)
            wq_hi(1)
            quantised_T(3)
            round_up(5)
            wq_hi(2)
            quantised_T(4)
            x1_hi(0)
            wq_hi(3)
            quantised_T(5)
            x1_hi(1)
            wq_hi(4)
            for g in range(2, G):
                x1_hi(g)
                w2_hi(g - 2)
                if g >= G - 2:
                    proj_evac(g - G + 2)

            def q_strips(hf, c):
                col, im = slice(hf * HALF, (hf + 1) * HALF), slice(hf * B // 2, (hf + 1) * B // 2)
                act.wait_ge(sm["proj_sb"], raw_jobs(hf, c)[0])
                if hf == c == 0:
                    act.wait_ge(sm["x1lo_ready"], G)
                for j in range(JP):
                    act.activation(qun[:, c, im, j], raw[:, c, 0, col].rearrange("p (i s) -> p i s", s=S), ACT.Copy,
                                   scale=cols("par")[:, 4 + j:5 + j]).then_inc(sm["qun_ready"], 1)

            def exps(b, kind):
                if kind == 0 and b >= 2:
                    act.wait_ge(sm["pv_ps"], b - 1)
                if kind == 1 and b >= 1:
                    act.wait_ge(sm["den_ps"], b)
                for i in range(0, BI, 2):
                    act.wait_ge(sm["s_ps"], 4 * b + 2 * kind + i // 2 + 1)
                    dst = (en[:, b % 2] if kind == 0 else ed)[:, i:i + 2].rearrange("p i c j s -> p i (c j s)")
                    act.activation(dst, ps[0:2 * S, i:i + 2, 0:KC * JP * S], ACT.Exp,
                                   scale=DH1 ** -0.5).then_inc(sm["exp_ready"], 1)

            for n, job in enumerate(PJ):
                if n >= 2:
                    proj_evac(n)
                if job[0] == "qk" and job[3] == 3 and n < NPJ - 1:
                    q_strips(job[1], job[2])

            def ve_hi(e):
                act.wait_ge(ve_in[e % NVR], 16 * (e // NVR + 1))
                if e >= NVR:
                    act.wait_ge(sm["ve_ps"], NT * (e - NVR + 1))
                act.activation(vehi[:, e % NVR], veraw[:, e % NVR], ACT.Copy).then_inc(sm["vehi_ready"], 1)

            for b in range(NB):
                exps(b, 0)
                if b == 0:
                    q_strips(1, KC - 1)
                exps(b, 1)
                if b < NVR:
                    ve_hi(b)
            def x2_hi(g):
                act.wait_ge(sm["x2T_ps"], g + 1)
                src = ps[:, 2 + g % 2, 0:2 * KC * R].rearrange("p (a c t) -> p a c t", a=2, c=KC)
                act.activation(h1T[:, :, g * R:(g + 1) * R], src[:, 1], ACT.Copy)
                act.activation(x2hi[:, :, g * R:(g + 1) * R], src[:, 0], ACT.Copy).then_inc(sm["x2hi_ready"], 1)

            def exp_gate(t):
                act.wait_ge(sm["gate_ps"], t + 1)
                act.activation(ez[0:TROWS[t], t], ps[0:TROWS[t], t % 2, 0:NH2 * NE], ACT.Exp,
                               scale=-1.0).then_inc(sm["ez_ready"], 1)

            def qk2_evac(n):
                hf, c, kind = QK2[n]
                act.wait_ge(sm["qk2_ps"], n + 1)
                src, col = ps[:, 4 + n % 4, 0:HALF], slice(hf * HALF, (hf + 1) * HALF)
                if kind == "k":
                    act.activation(k2[:, c, col], src, ACT.Copy).then_inc(sm["qk2_ready"], 1)
                else:
                    for p_ in range(2):
                        ins = act.activation(q2[:, c, 8 * hf:8 * hf + 8, p_], src.rearrange("p (i s) -> p i s", s=S),
                                             ACT.Copy, scale=cols("par")[:, 2 + p_:3 + p_])
                    ins.then_inc(sm["qk2_ready"], 1)

            for kind, n in D_ORDER:
                if kind == "turn":
                    x2_hi(n)
                elif kind == "gate":
                    exp_gate(n)
                elif kind == "qk":
                    qk2_evac(n)

            def first_expert(g):
                act.wait_ge(sm["ve_ps"], g + 1)
                act.activation(v2[0:TROWS[g], g].rearrange("p a b -> p (a b)"), ps[0:TROWS[g], 4 + g % 4, :],
                               ACT.Copy).then_inc(sm["sel0_ready"], 1)

            def exp2(g):
                act.wait_ge(sm["sub_ready"], g + 1)
                if g >= 2:
                    act.wait_ge(sm["p2_ready"], g - 1)
                n = C2 * images(g)
                act.activation(pe2[:, g % 2, 0:n], sc[:, g % 2, 0:n], ACT.Exp).then_inc(sm["e2_ready"], 1)

            def gmT_evac(g):
                act.wait_ge(sm["gmT_ps"], g + 1)
                act.activation(gmThi[:, g * P:g * P + TROWS[g]], ps[0:NH2 * NE, g % 2, 0:TROWS[g]],
                               ACT.Copy).then_inc(sm["gmThi_ready"], 1)

            def spread_p(t):
                m = TROWS[t]
                act.wait_ge(sm["pt_ps"], t + 1)
                src = ps[0:m, t % 2, 0:NH2 * S].rearrange("p (h s) -> p h s", h=NH2)
                for j in range(len(TI[t])):
                    ins = act.activation(ptb[0:m, t, :, j], src, ACT.Copy,
                                         scale=cols("blk", m)[:, t * TI_MAX + j:t * TI_MAX + j + 1])
                ins.then_inc(sm["ptb_ready"], 1)

            def oe_hi(u):
                act.wait_ge(oe_in[u % NOR], 16 * (u // NOR + 1))
                if u >= NOR:
                    act.wait_ge(sm["main_ps"], OEU * (u - NOR + 1))
                act.activation(oehi[:, u % NOR], oeraw[:, u % NOR], ACT.Copy).then_inc(sm["oehi_ready"], 1)

            for g in range(NT):
                first_expert(g)
                gmT_evac(g)
            ve_hi(NVR)
            for n in range(2 * C2):
                c, hf = n // 2, n % 2
                act.wait_ge(sm["gateb_ps"], n + 1)
                act.activation(gateb[:, c, hf * HALF:(hf + 1) * HALF], ps[:, hf, 0:HALF],
                               ACT.Copy).then_inc(sm["gateb_ready"], 1)
            for n in range(NT, NJ):
                if n % NT == 0 and n // NT + NVR - 1 in range(NVR + 1, NE):
                    ve_hi(n // NT + NVR - 1)
                for g in soft_at(n, LAG_MAX):
                    exp2(g)
                if n == LAST:
                    oe_hi(0)
                for t in turn_at(n):
                    spread_p(t)

            def oT_hi(c):
                act.wait_ge(sm["ot_ready"], c)
                if c >= 2:
                    act.wait_ge(sm["glo_ready"], (c - 1) * NE)
                act.activation(oThi[:, c % 2], ot[:], ACT.Copy).then_inc(sm["oThi_ready"], 1)

            for u in range(1, NOU):
                oe_hi(u)
                if u % 2 and u // 2 + 1 < C2:
                    oT_hi(u // 2 + 1)

        @block.vector
        def _(dve):
            count = {}

            def step(name, ins):
                count[name] = count.get(name, 0) + 1
                ins.then_inc(sm[name], 1)
                dve.wait_ge(sm[name], count[name])

            def absmax(g):
                dve.wait_ge(x_in[g], 16)
                dve.tensor_reduce(amax[:, g:g + 1], xp[:, g], AX, ALU.max,
                                  apply_absolute_value=True).then_inc(sm["amaxed"], 1)

            def mean_square(b):
                dve.wait_ge(sm["sq_done"], GI * (b + 1))
                s_ = slice(GI * b, GI * b + GI)
                dve.tensor_scalar(msq[:, s_], ssq[:, s_], 1.0 / DIN, 1e-6, ALU.mult,
                                  ALU.add).then_inc(sm["msq_ready"], 1)

            def quant_scales(b):
                dve.wait_ge(sm["rrms_ready"], b + 1)
                s_ = slice(GI * b, GI * b + GI)
                step("qchain", dve.tensor_tensor(amn[:, s_], amax[:, s_], rrms[:, s_], ALU.mult))
                step("qchain", dve.tensor_scalar(amc[:, s_], amn[:, s_], Q_EPS, None, ALU.max))
                step("qchain", dve.reciprocal(iam[:, s_], amc[:, s_]))
                dve.scalar_tensor_tensor(out=qsc[:, s_], in0=rrms[:, s_], scalar=127.0, in1=iam[:, s_],
                                         op0=ALU.mult, op1=ALU.mult).then_inc(sm["qpar"], 1)
                step("qchain", dve.tensor_scalar(dqs[:, s_], amc[:, s_], small[0:R, 3:4], None, ALU.mult))

            for g in range(GI):
                absmax(g)
                if g == 0:
                    dve.wait_ge(tokw_in, 16)
                    dve.tensor_reduce(small[:, 0:1], tw[:], AX, ALU.add,
                                      apply_absolute_value=True).then_inc(sm["wabs"], 1)
            dve.wait_ge(const_in, 16)
            dve.tensor_copy(ident_bf[:], cols("ident")).then_inc(sm["ident_ready"], 1)
            dve.wait_ge(sm["amaxed"], GI)
            mean_square(0)
            dve.wait_ge(sm["tot_ps"], 1)
            step("wscale", dve.tensor_scalar(small[:, 1:2], ps[:, 6, 0:1], 1.0 / (D * DIN), Q_EPS, ALU.mult, ALU.max))
            step("wscale", dve.reciprocal(small[:, 2:3], small[:, 1:2]))
            step("wscale", dve.tensor_scalar(small[:, 3:4], small[:, 1:2], 1.0 / 127.0, None, ALU.mult))
            step("clip_t", dve.tensor_scalar(tw[:], tw[:], small[:, 2:3], 1.0, ALU.mult, ALU.min))
            quant_scales(0)
            dve.tensor_scalar(tw[:], tw[:], -1.0, ROUND, ALU.max, ALU.add).then_inc(sm["tern_pre"], 1)

            def quantised(g):
                dve.wait_ge(sm["yround_ready"], g + 1)
                if g >= NQB:
                    dve.wait_ge(sm["qT_ps"], g - NQB + 1)
                dve.tensor_scalar(qb[:, g % NQB], xp[:, g], ROUND, 127.0, ALU.subtract,
                                  ALU.min).then_inc(sm["qb_ready"], 1)

            def quantised_T(g):
                dve.wait_ge(sm["qT_ps"], g + 1)
                src = ps[:, g % 2, :].bitcast(BF16)[:, 0:DC * (R + 1)].rearrange("p (c t) -> p c t", c=DC)
                dve.tensor_copy(qT[:, g % 2, :, 0:R], src[:, :, 0:R]).then_inc(sm["qT_sb"], 1)

            def ln_stats(which, g):
                step("lnchain", dve.bn_stats(stat6[:, which], h[:, g]))
                step("lnchain", dve.bn_aggr(mv[:, which, g], stat6[:, which]))
                dve.tensor_scalar(lnv[:, which, g:g + 1], mv[:, which, g, 1:2], 1e-5, None,
                                  ALU.add).then_inc(sm["lnv_ready"], 1)

            def ln_apply(which, g):
                n = which * G + g
                dve.wait_ge(sm["rstd_ready"], n + 1)
                if g >= 2:
                    dve.wait_ge(sm["x2T_ps" if which else "x1T_ps"], g - 1)
                dve.tensor_scalar(xhat[:, g % 2], h[:, g], mv[:, which, g, 0:1], rstd[:, which, g:g + 1],
                                  ALU.subtract, ALU.mult).then_inc(sm["xhat_ready"], 1)

            def embed(g):
                dve.wait_ge(sm["proj_ps"], g + 1)
                if g == 0:
                    dve.wait_ge(sm["bias_sb"], 1)
                step("h0_ready", dve.scalar_tensor_tensor(
                    out=h[:, g], in0=ps[0:R, 2 + g % 2, 0:D], scalar=dqs[:, g:g + 1], in1=biasb[:, 0],
                    op0=ALU.mult, op1=ALU.add))
                ln_stats(0, g)

            def x1_lo(g):
                dve.wait_ge(sm["x1hi_ready"], g + 1)
                tc = slice(g * R, (g + 1) * R)
                dve.tensor_tensor(x1lo[:, :, tc], ps[:, 4 + g % 2, 0:KC * R].rearrange("p (c t) -> p c t", c=KC),
                                  x1hi[:, :, tc].bitcast(F32), ALU.subtract).then_inc(sm["x1lo_ready"], 1)

            absmax(3)
            quantised(0)
            absmax(4)
            absmax(5)
            dve.wait_ge(sm["amaxed"], G)
            mean_square(1)
            quantised_T(0)
            quantised(1)
            quantised(2)
            quant_scales(1)
            quantised_T(1)
            embed(0)
            quantised(3)
            embed(1)
            ln_apply(0, 0)
            quantised(4)
            embed(2)
            ln_apply(0, 1)
            x1_lo(0)
            quantised(5)
            embed(3)
            ln_apply(0, 2)
            x1_lo(1)
            embed(4)
            ln_apply(0, 3)
            x1_lo(2)
            embed(5)
            ln_apply(0, 4)
            x1_lo(3)
            ln_apply(0, 5)
            x1_lo(4)
            x1_lo(5)

            def rope(hf, c, kinds=(0, 2)):
                col, im = slice(hf * HALF, (hf + 1) * HALF), slice(hf * B // 2, (hf + 1) * B // 2)

                def by_image(a):
                    return a.rearrange("p (i s) -> p i s", s=S)

                def many(ins):
                    ins.then_inc(sm["rope_t"], 1)
                    count["rope_t"] = count.get("rope_t", 0) + 1

                tmp = by_image(ropet[:, col])
                cos, sin = bcast(cols("cos"), 1, B // 2), bcast(cols("sin"), 1, B // 2)
                for kind in kinds:
                    dve.wait_ge(sm["proj_sb"], raw_jobs(hf, c)[kind // 2])
                    own, other = by_image(raw[:, c, kind, col]), by_image(raw[:, c, kind + 1, col])
                    many(dve.tensor_tensor(tmp, own, cos, ALU.mult))
                    step("rope_t", dve.tensor_tensor(other, other, sin, ALU.mult))
                    step("rope_t", dve.tensor_tensor(tmp, tmp, other, ALU.add))
                    if hf == c == 0 and kind:
                        dve.wait_ge(sm["wqlo_ready"], 5)
                    if kind == 0:
                        for j in range(JP):
                            many(dve.tensor_scalar(qrot[:, c, im, j], tmp, cols("par")[:, 4 + j:5 + j], None, ALU.mult))
                    else:
                        for p_ in range(2):
                            sel = cols("par")[:, p_:p_ + 1]
                            many(dve.tensor_scalar(krot[:, c, im, p_], tmp, sel, None, ALU.mult))
                    dve.wait_ge(sm["rope_t"], count["rope_t"])

            def causal(b):
                for i in range(0, BI, 2):
                    dve.wait_ge(sm["exp_ready"], 4 * b + i // 2 + 1)
                    v = en[:, b % 2, i:i + 2].rearrange("p i c j s -> p (i c j) s")
                    dve.tensor_tensor(v, v, bcast(cols("keep", 2 * S), 1, 2 * KC * JP),
                                      ALU.mult).then_inc(sm["en_ready"], 1)

            rope(0, 0)
            rope(0, 1)
            rope(1, 0)
            rope(1, 1, (0,))
            causal(0)
            rope(1, 1, (2,))
            dve.wait_ge(sm["proj1_ps"], NPJ)
            dve.memset(yT[:, :, T:TP], 0.0).then_inc(sm["yT_pad"], 1)

            def denominators(b):
                if b:
                    dve.wait_ge(sm["yT_ready"], b)
                dve.wait_ge(sm["den_ps"], b + 1)
                dve.reciprocal(rden[:], ps[:, 5 + 2 * (b % 2), 0:UN * S]).then_inc(sm["rden_ready"], 1)

            def normalise(b):
                dve.wait_ge(sm["rden_ready"], b + 1)
                dve.wait_ge(sm["pv_ps"], b + 1)
                dve.tensor_tensor(yT[:, :, b * BI * S:(b + 1) * BI * S],
                                  ps[:, 4 + 2 * (b % 2), 0:UN * S].rearrange("p (c t) -> p c t", c=KC),
                                  rden[:].rearrange("p (c t) -> p c t", c=KC), ALU.mult).then_inc(sm["yT_ready"], 1)

            for b in range(1, NB - 1):
                causal(b)
                denominators(b - 1)
                normalise(b - 1)
            denominators(NB - 2)
            normalise(NB - 2)
            causal(NB - 1)

            def residual(g):
                dve.wait_ge(sm["op_ps"], g // 2 * 2 + 2)
                dve.wait_ge(sm["h0b_ready"], g + 1)
                step("h1_ready", dve.tensor_tensor(
                    h[:, g], h[:, g], ps[0:R, OPB[g][0], OPB[g][1]:OPB[g][1] + D], ALU.add))
                ln_stats(1, g)

            def x2_lo(g):
                dve.wait_ge(sm["x2hi_ready"], g + 1)
                tc = slice(g * R, (g + 1) * R)
                dve.tensor_tensor(x2lo[:, :, tc], ps[:, 2 + g % 2, 0:KC * R].rearrange("p (c t) -> p c t", c=KC),
                                  x2hi[:, :, tc].bitcast(F32), ALU.subtract).then_inc(sm["x2lo_ready"], 1)

            residual(0)
            residual(1)
            ln_apply(1, 0)
            residual(2)
            ln_apply(1, 1)
            x2_lo(0)
            ln_apply(1, 2)
            x2_lo(1)
            x2_lo(2)
            denominators(NB - 1)
            normalise(NB - 1)
            residual(3)
            ln_apply(1, 3)
            residual(4)
            residual(5)
            ln_apply(1, 4)
            x2_lo(3)
            ln_apply(1, 5)
            x2_lo(4)
            x2_lo(5)

            def gates(tiles):
                m, n, w = TROWS[tiles[0]], len(tiles), slice(tiles[0], tiles[-1] + 1)
                dve.wait_ge(sm["ez_ready"], tiles[-1] + 1)

                def heads(a):
                    return a.rearrange("p t h e -> p (t h) e")

                z, gt, eq, hot = ez[0:m, w], heads(gate[0:m, w]), heads(geq[0:m, 0:n]), heads(onehot[0:m, w])
                top, first = gtop[0:m, w].rearrange("p t h -> p (t h)"), grk[0:m, 0:n].rearrange("p t h -> p (t h)")
                step("gchain", dve.tensor_scalar(z, z, 1.0, None, ALU.add))
                step("gchain", dve.reciprocal(gt.rearrange("p a b -> p (a b)"), z.rearrange("p t x -> p (t x)")))
                step("gchain", dve.tensor_reduce(top, gt, AX, ALU.max))
                step("gchain", dve.tensor_tensor(eq, gt, bcast(top, 2, NE), ALU.is_equal))
                step("gchain", dve.tensor_tensor(eq, eq, bcast(cols("rank", m), 1, n * NH2), ALU.mult))
                step("gchain", dve.tensor_reduce(first, eq, AX, ALU.max))
                step("gchain", dve.tensor_tensor(hot, eq, bcast(first, 2, NE), ALU.is_equal))
                dve.tensor_tensor(heads(gm[0:m, w]), hot, gt, ALU.mult).then_inc(sm["gm_ready"], 1)

            def row_max(g):
                k, n = g % 2, C2 * images(g)
                dve.wait_ge(sm["s2_ps"], g + 1)
                if g >= 2:
                    dve.wait_ge(sm["e2_ready"], g - 1)
                src = ps[0:2 * S, 2 + g % 2, 0:n * S].rearrange("p (u s) -> p u s", s=S)
                step("schain", dve.tensor_tensor(sc[:, k, 0:n], src, bcast(cols("cbias", 2 * S), 1, n), ALU.add))
                dve.tensor_reduce(mx2[:, k, 0:n], sc[:, k, 0:n], AX, ALU.max).then_inc(sm["sc_ready"], 1)

            def row_sum(g):
                k, n = g % 2, C2 * images(g)
                dve.wait_ge(sm["e2_ready"], g + 1)
                if g >= 2:
                    dve.wait_ge(sm["p2_ready"], g - 1)
                step("schain", dve.tensor_reduce(sm2[:, k, 0:n], pe2[:, k, 0:n], AX, ALU.add))
                dve.reciprocal(rs2[:, k, 0:n], sm2[:, k, 0:n]).then_inc(sm["rs_ready"], 1)

            def gate_halves(t):
                dve.wait_ge(sm["gmThi_ready"], t + 1)
                tc, m = slice(t * P, t * P + TROWS[t]), TROWS[t]
                dve.tensor_tensor(gmTlo[:, tc], ps[0:NH2 * NE, t % 2, 0:m], gmThi[:, tc].bitcast(F32),
                                  ALU.subtract).then_inc(sm["gmTlo_ready"], 1)
                dve.tensor_scalar(maskT[:, tc], gmThi[:, tc].bitcast(F32), 0.0, None,
                                  ALU.is_gt).then_inc(sm["maskT_ready"], 1)

            def select(n):
                e, t, h0, h1 = JOBS[n]
                dve.wait_ge(sm["ve_ps"], n + 1)
                if e == 1:
                    dve.wait_ge(sm["sel0_ready"], t + 1)
                else:
                    dve.wait_ge(sm["sel_ready"], n - 2 * NT + 1)
                m = TROWS[t]
                dve.copy_predicated(v2[0:m, t, h0:h1], bcast(onehot[0:m, t, h0:h1, e], 2, DH2),
                                    ps[0:m, JBANK[n], 0:(h1 - h0) * DH2].rearrange("p (a b) -> p a b", b=DH2)).then_inc(
                    sm["sel_ready"], 1)

            def first_chunk(hf):
                col = slice(hf * HALF, (hf + 1) * HALF)
                dve.wait_ge(sm["pv0_ps"], hf + 1)
                if hf == 0:
                    dve.wait_ge(sm["gateb_ready"], 2 * C2)
                step("oT_hi", dve.tensor_tensor(ot[:, col], ps[:, 2 + hf, 0:HALF], gateb[:, 0, col], ALU.mult))
                step("oT_hi", dve.tensor_copy(oThi[:, 0, col], ot[:, col]))
                dve.wait_ge(mask_in[0], 32)
                dve.tensor_tensor(ghi[:, 0, hf], maskb[:, 0, 0, col], oThi[:, 0, col].bitcast(F32),
                                  ALU.mult).then_inc(sm["g_ready"], 1)
                step("oT_hi", dve.tensor_tensor(oTlo[:, 0, col], ot[:, col], oThi[:, 0, col].bitcast(F32), ALU.subtract))
                dve.tensor_tensor(glo[:, 0, hf], maskb[:, 0, 0, col], oTlo[:, 0, col].bitcast(F32),
                                  ALU.mult).then_inc(sm["glo_ready" if hf else "g0_ready"], 1)

            for tiles in GATES:
                gates(tiles)
            for t in range(NT):
                gate_halves(t)
            for n in range(NT, NJ):
                select(n)
                if n >= LAST + NT and n < LAST + NT + 2:
                    first_chunk(n - LAST - NT)
                for g in soft_at(n, LAG_MAX):
                    row_max(g)
                for g in soft_at(n, LAG_SUM):
                    row_sum(g)

            def by_half(a):
                return a.rearrange("p (a t) -> p a t", a=2)

            for k in range(1, C2 * NE):
                c, w = k // NE, k // MEU
                if k % NE == PV_AT + 3 and c + 1 < C2:
                    if c >= 1:
                        dve.wait_ge(sm["oThi_ready"], c)
                        dve.wait_ge(sm["oTlo_ready"], c)
                    o = PVB[c + 1]
                    dve.wait_ge(sm["pv2_ps"], c + 1)
                    dve.tensor_tensor(by_half(ot[:]), ps[:, o:o + 2, 0:HALF], by_half(gateb[:, c + 1]),
                                      ALU.mult).then_inc(sm["ot_ready"], 1)
                if k >= NGR:
                    dve.wait_ge(sm["main_ps"], k - NGR + 1)
                if k % NE == 0:
                    dve.wait_ge(sm["oThi_ready"], c)
                    dve.wait_ge(sm["oTlo_ready"], c)
                if k % MEU == 0:
                    dve.wait_ge(mask_in[w % NMR], 32 * (w // NMR + 1))
                msk = by_half(maskb[:, w % NMR, k % MEU])
                dve.tensor_tensor(ghi[:, k % NGR], msk, by_half(oThi[:, c % 2].bitcast(F32)),
                                  ALU.mult).then_inc(sm["g_ready"], 1)
                dve.tensor_tensor(glo[:, k % NGR], msk, by_half(oTlo[:, c % 2].bitcast(F32)),
                                  ALU.mult).then_inc(sm["glo_ready"], 1)
            for m in range(KC):
                for hf in range(2):
                    dve.wait_ge(sm["acc_done"], 2 * m + hf + 1)
                    dve.tensor_tensor(yo[:, m, hf], ps[:, 2 * m + hf, 0:HALF], h1T[:, m, hf * HALF:(hf + 1) * HALF],
                                      ALU.add).then_inc(sm["out_ready"], 1)

        @block.tensor
        def _(pe):
            pe.wait_ge(const_in, 16)
            pe.wait_ge(vec_in, 16)
            for a in range(2):
                ins = pe.matmul(ps[0:R, 7, a * D:(a + 1) * D], cols("rowsel", 3)[:, a * R:(a + 1) * R], vrow[:],
                                start=True, stop=True)
            ins.then_inc(sm["bias_ps"], 1)
            pe.wait_ge(sm["pool_setup"], 2)
            pe.wait_ge(sm["wabs"], 1)
            pe.matmul(ps[:, 6, 0:1], ones[:], small[:, 0:1], start=True, stop=True).then_inc(sm["tot_ps"], 1)

            def qT_there(g):
                if g < 2:
                    pe.wait_ge(sm["qT_sb"], g + 1)
                else:
                    pe.wait_ge(sm["qT2_sb"], g - 1)

            def turn_q(g):
                pe.wait_ge(sm["qb_ready"], g + 1)
                if g == 0:
                    pe.wait_ge(sm["ident_ready"], 1)
                if g >= 2:
                    qT_there(g - 2)
                dst = ps[:, g % 2, :].bitcast(BF16)
                for c in range(DC):
                    ins = pe.transpose(dst[:, c * (R + 1):c * (R + 1) + R], qb[:, g % NQB, c * P:(c + 1) * P],
                                       ident_bf[0:R, 0:R])
                ins.then_inc(sm["qT_ps"], 1)

            def embed(g):
                qT_there(g)
                if g == 0:
                    pe.wait_ge(sm["tern_ready"], 1)
                if g >= 2:
                    pe.wait_ge(sm["h0_ready"], g - 1)
                for c in range(DC):
                    ins = pe.matmul(ps[0:R, 2 + g % 2, 0:D], qT[:, g % 2, c, 0:R], tern[:, c * D:(c + 1) * D],
                                    start=(c == 0), stop=(c == DC - 1))
                ins.then_inc(sm["proj_ps"], 1)

            def turn_x(g):
                pe.wait_ge(sm["xhat_ready"], g + 1)
                if g >= 2:
                    pe.wait_ge(sm["x1lo_ready"], g - 1)
                for c in range(KC):
                    ins = pe.transpose(ps[:, 4 + g % 2, c * R:(c + 1) * R], xhat[:, g % 2, c * P:(c + 1) * P],
                                       cst[0:R, 0:R])
                ins.then_inc(sm["x1T_ps"], 1)

            WB = (0, 2, 1, 3)

            def proj_job(n):
                kind_, a, c, kind = PJ[n]
                pe.wait_ge(sm["x1lo_ready"], GI if n < NEARLY else G)
                pe.wait_ge(sm["wqlo_ready"], WB[kind] + 1 if kind_ == "qk" else 5)
                if PJPREV[n] >= 0:
                    pe.wait_ge(sm["proj_sb"], PJPREV[n] + 1)
                elif PJB[n] >= 6:
                    pe.wait_ge(sm["bias_sb"], 1)
                else:
                    pe.wait_ge(sm["x1lo_ready"], G)
                for k in range(KC):
                    if kind_ == "qk":
                        wb, tc, col = WB[kind], slice(a * HALF, (a + 1) * HALF), slice(c * P, (c + 1) * P)
                        ins = split3(pe, ps[:, PJB[n], 0:HALF], wqhi[:, wb, k, col], wqlo[:, wb, k, col],
                                     x1hi[:, k, tc], x1lo[:, k, tc], k == 0, k == KC - 1)
                    else:
                        tc = slice(a * R, (a + 1) * R)
                        ins = split3(pe, ps[0:R, PJB[n], 0:D], x1hi[:, k, tc], x1lo[:, k, tc],
                                     wqhi[:, 4, k], wqlo[:, 4, k], k == 0, k == KC - 1)
                ins.then_inc(sm["proj1_ps"], 1)

            for s_ in range(G + 4):
                if s_ < G:
                    turn_q(s_)
                if 0 <= s_ - 1 < G:
                    embed(s_ - 1)
                if s_ == G + 2:
                    proj_job(0)
                if 0 <= s_ - 4 < G:
                    turn_x(s_ - 4)
                if s_ >= G + 2:
                    proj_job(s_ - G - 1)
            for n in range(3, NPJ):
                proj_job(n)

            def scores(b, kind):
                if b == kind == 0:
                    pe.wait_ge(sm["h0_ready"], G)
                    qT_there(G - 1)
                late = b * BI * 2 // B + 1
                pe.wait_ge(sm["rope_t"], 12 * KC * late)
                pe.wait_ge(sm["kun_ready"], KC * 2 * late)
                pe.wait_ge(sm["qun_ready"], KC * JP * late)
                for ii in range(BI):
                    i = b * BI + ii
                    if ii % 2 == 0 and b + kind:
                        pe.wait_ge(sm["exp_ready"], 4 * b + 2 * kind + ii // 2 - 1)
                    for c in range(KC):
                        key = (kun if kind else krot)[:, c, i].rearrange("p a b -> p (a b)")
                        qry = (qun if kind else qrot)[:, c, i].rearrange("p a b -> p (a b)")
                        ins = pe.matmul(ps[0:2 * S, ii, c * JP * S:(c + 1) * JP * S], key, qry, start=True, stop=True)
                    if ii % 2:
                        ins.then_inc(sm["s_ps"], 1)

            def attend(b):
                if b == 0:
                    pe.wait_ge(sm["proj_sb"], NPJ)
                    pe.wait_ge(v_in, 16 * 2 * GI)
                if b >= 2:
                    pe.wait_ge(sm["yT_ready"], b - 1)
                for ii in range(BI):
                    if ii % 2 == 0:
                        pe.wait_ge(sm["en_ready"], 2 * b + ii // 2 + 1)
                    if b == NB - 1 and ii == 2:
                        turn_x2(0)
                    for c in range(KC):
                        u = c * BI + ii
                        for j in range(JP):
                            vv = vblk[:, b * BI + ii, c * JP + j].rearrange("p a b -> p (a b)")
                            ins = pe.matmul(ps[32 * j:32 * j + 32, 4 + 2 * (b % 2), u * S:(u + 1) * S], vv,
                                            en[:, b % 2, ii, c, j], start=True, stop=True)
                ins.then_inc(sm["pv_ps"], 1)

            def denominators(b):
                pe.wait_ge(sm["exp_ready"], 4 * b + 4)
                if b >= 2:
                    pe.wait_ge(sm["yT_ready"], b - 1)
                for j in range(JP):
                    ins = pe.matmul(ps[32 * j:32 * j + 32, 5 + 2 * (b % 2), 0:UN * S], cols("blk2", 2 * S),
                                    ed[:, :, :, j].rearrange("p i c s -> p c i s"), start=True, stop=True)
                ins.then_inc(sm["den_ps"], 1)

            def out_proj(g):
                if g < NOP:
                    pe.wait_ge(wout_in, 16)
                    pe.wait_ge(sm["yT_ready"], NB - 1)
                else:
                    pe.wait_ge(sm["yT_pad"], 1)
                    pe.wait_ge(sm["yT_ready"], NB)
                o, w = OPB[g]
                for k in range(KC):
                    ins = pe.matmul(ps[0:R, o, w:w + D], yT[:, k, g * R:(g + 1) * R], wo[:, k],
                                    start=(k == 0), stop=(k == KC - 1))
                ins.then_inc(sm["op_ps"], 1)

            def turn_x2(g):
                pe.wait_ge(sm["xhat_ready"], G + g + 1)
                if g >= 2:
                    pe.wait_ge(sm["x2lo_ready"], g - 1)
                else:
                    pe.wait_ge(sm["exp_ready"], 4 * NB)
                for a in range(2):
                    for c in range(KC):
                        src = (h[:, g] if a else xhat[:, g % 2])[:, c * P:(c + 1) * P]
                        o = (a * KC + c) * R
                        ins = pe.transpose(ps[:, 2 + g % 2, o:o + R], src, cst[0:R, 0:R])
                ins.then_inc(sm["x2T_ps"], 1)

            for b in range(NB):
                scores(b, 0)
                if b:
                    denominators(b - 1)
                scores(b, 1)
                if b == NB - 1:
                    out_proj(0)
                    out_proj(1)
                    denominators(b)
                    for g in range(2, NOP):
                        out_proj(g)
                attend(b)

            NQ = NH2 * DH2

            def gate_job(t):
                if t == 1:
                    pe.wait_ge(sm["h1_ready"], G)
                elif t >= 2:
                    pe.wait_ge(sm["ez_ready"], t - 1)
                pe.wait_ge(sm["x2lo_ready"], groups_of(t))
                tc = slice(t * P, t * P + TROWS[t])
                for k in range(KC):
                    ins = split3(pe, ps[0:TROWS[t], t % 2, 0:NH2 * NE], x2hi[:, k, tc], x2lo[:, k, tc],
                                 w2hi[:, k, 2 * NQ:], w2lo[:, k, 2 * NQ:], k == 0, k == KC - 1)
                ins.then_inc(sm["gate_ps"], 1)

            def qk2_job(n):
                hf, c, kind = QK2[n]
                if n == 0:
                    pe.wait_ge(sm["h1_ready"], 2)
                elif n == 1:
                    pe.wait_ge(sm["h1_ready"], NOP)
                elif n < 4:
                    pe.wait_ge(sm["yT_ready"], NB)
                else:
                    pe.wait_ge(sm["qk2_ready"], n - 3)
                base = (NQ if kind == "k" else 0) + c * P
                tc = slice(hf * HALF, (hf + 1) * HALF)
                pe.wait_ge(sm["x2lo_ready"], 3 if hf == 0 else G)
                for k in range(KC):
                    ins = split3(pe, ps[:, 4 + n % 4, 0:HALF], w2hi[:, k, base:base + P], w2lo[:, k, base:base + P],
                                 x2hi[:, k, tc], x2lo[:, k, tc], k == 0, k == KC - 1)
                ins.then_inc(sm["qk2_ps"], 1)

            pe.wait_ge(sm["w2lo_ready"], 4)
            for kind, n in D_ORDER:
                if kind == "turn":
                    if n:
                        turn_x2(n)
                elif kind == "gate":
                    gate_job(n)
                elif kind == "out":
                    out_proj(n)
                else:
                    qk2_job(n)

            def value_job(n):
                e, t, h0, h1 = JOBS[n]
                before = JPREV[n]
                if before < 0:
                    pe.wait_ge(sm["qk2_ready"], 4 * C2 - 4 + n + 1)
                elif before < NT:
                    pe.wait_ge(sm["sel0_ready"], before + 1)
                else:
                    pe.wait_ge(sm["sel_ready"], before - NT + 1)
                if t == 0:
                    pe.wait_ge(sm["velo_ready"], e + 1)
                tc, f = slice(t * P, t * P + TROWS[t]), slice(h0 * DH2, h1 * DH2)
                for k in range(KC):
                    ins = split3(pe, ps[0:TROWS[t], JBANK[n], 0:(h1 - h0) * DH2], x2hi[:, k, tc], x2lo[:, k, tc],
                                 vehi[:, e % NVR, k, f], velo[:, e % NVR, k, f], k == 0, k == KC - 1)
                ins.then_inc(sm["ve_ps"], 1)

            def turn_gates(t):
                pe.wait_ge(sm["gm_ready"], t // 2 + 1)
                if t < 2:
                    pe.wait_ge(sm["ez_ready"], NT)
                else:
                    pe.wait_ge(sm["gmTlo_ready"], t - 1)
                m = TROWS[t]
                pe.transpose(ps[0:NH2 * NE, t % 2, 0:m], gm[0:m, t].rearrange("p a b -> p (a b)"),
                             cst[0:m, 0:m]).then_inc(sm["gmT_ps"], 1)

            def gate_rows(n):
                c, hf = n // 2, n % 2
                if n < 2:
                    pe.wait_ge(sm["gmTlo_ready"], NT)
                    pe.wait_ge(sm["pool_setup"], 3)
                else:
                    pe.wait_ge(sm["gateb_ready"], n - 1)
                rows, col = gate_sel[:, 2 * c:2 * c + 2].rearrange("p a b -> p (a b)"), slice(hf * HALF, (hf + 1) * HALF)
                pe.matmul(ps[:, hf, 0:HALF], rows, gmTlo[:, col], start=True, stop=False)
                pe.matmul(ps[:, hf, 0:HALF], rows, gmThi[:, col], start=False, stop=True).then_inc(sm["gateb_ps"], 1)

            def scores2(g):
                if g < 2:
                    pe.wait_ge(sm["x2lo_ready"], G)
                    pe.wait_ge(sm["qk2_ready"], 4 * C2)
                else:
                    pe.wait_ge(sm["sc_ready"], g - 1)
                ni = images(g)
                for c in range(C2):
                    for ii in range(ni):
                        i = g * GI + ii
                        tc = slice(i * S, (i + 1) * S)
                        u = c * ni + ii
                        ins = pe.matmul(ps[0:2 * S, 2 + g % 2, u * S:(u + 1) * S], q2[:, c, i].rearrange("p a b -> p (a b)"), k2[:, c, tc],
                                        start=True, stop=True)
                ins.then_inc(sm["s2_ps"], 1)

            def turn_p(t):
                pe.wait_ge(sm["p2_ready"], TILE_G[t] + 1)
                if t < 2:
                    pe.wait_ge(sm["gateb_ready"], 2 * C2)
                else:
                    pe.wait_ge(sm["ptb_ready"], t - 1)
                m = TROWS[t]
                for c in range(C2):
                    ins = pe.transpose(ps[0:m, t % 2, c * 2 * S:(c + 1) * 2 * S], prob[:, c, t * P:t * P + m],
                                       cst[0:2 * S, 0:2 * S])
                ins.then_inc(sm["pt_ps"], 1)

            def attend2(c, t, o):
                m, runs = TROWS[t], []
                for i in TI[t]:
                    kind = (i // (B // 2), t > 0 and i in TI[t - 1], t + 1 < NT and i in TI[t + 1])
                    if runs and runs[-1][0] == kind:
                        runs[-1][1].append(i)
                    else:
                        runs.append((kind, [i]))
                for p_ in range(2):
                    for (hf, more, open_), im in runs:
                        j, q0 = im[0] - TI[t][0], im[0] % (B // 2) * S
                        ins = pe.matmul(ps[DH2 * p_:DH2 * p_ + DH2, o + hf, q0:q0 + len(im) * S],
                                        v2[0:m, t, 2 * c + p_],
                                        ptb[0:m, t, 2 * c + p_, j:j + len(im)].rearrange("p a b -> p (a b)"),
                                        start=not more, stop=not open_)
                return ins

            def pair_attention(c):
                o = PVB[c]
                if c < 3:
                    pe.wait_ge(sm["sel_ready"], max(m for m in range(NJ) if JBANK[m] in (o, o + 1)) - NT + 1)
                else:
                    pe.wait_ge(sm["ot_ready"], c - 2)
                pe.wait_ge(sm["v2_ready"], NT if c < C2 // 2 else 2 * NT)
                for t in range(NT):
                    ins = attend2(c, t, o)
                ins.then_inc(sm["pv2_ps"], 1)

            def product(k, m, hf):
                u = k // OEU
                col = slice(m * P, (m + 1) * P)
                return split3(pe, ps[:, 2 * m + hf, 0:HALF], oehi[:, u % NOR, k % OEU, col], oelo[:, u % NOR, k % OEU, col],
                              ghi[:, k % NGR, hf], glo[:, k % NGR, hf], k == 0, k == C2 * NE - 1)

            def first_product(hf):
                def operands(m):
                    return ps[:, 2 * m + hf, 0:HALF], slice(m * P, (m + 1) * P)

                if hf == 0:
                    pe.wait_ge(sm["oelo_ready"], 1)
                    pe.wait_ge(sm["ptb_ready"], NT)
                pe.wait_ge(sm["g_ready"], hf + 1)
                for m in range(KC):
                    o, col = operands(m)
                    pe.matmul(o, oelo[:, 0, 0, col], ghi[:, 0, hf], start=True, stop=False)
                    pe.matmul(o, oehi[:, 0, 0, col], ghi[:, 0, hf], start=False, stop=False)
                pe.wait_ge(sm["glo_ready" if hf else "g0_ready"], 1)
                for m in range(KC):
                    o, col = operands(m)
                    ins = pe.matmul(o, oehi[:, 0, 0, col], glo[:, 0, hf], start=False, stop=False)
                return ins

            half_tile = next(t for t in range(NT) if B // 2 - 1 in TI[t] and B // 2 - 1 not in (TI[t + 1] if t + 1 < NT else ()))
            for n in range(NJ):
                value_job(n)
                if n < NT:
                    turn_gates(n)
                if NT <= n < NT + C2:
                    gate_rows(2 * (n - NT))
                    gate_rows(2 * (n - NT) + 1)
                for g in soft_at(n, 0):
                    scores2(g)
                for t in turn_at(n):
                    turn_p(t)
                if n in (LAST + NT, LAST + NT + 1):
                    hf = n - LAST - NT
                    for t in range(half_tile + 1) if hf == 0 else range(half_tile + 1, NT):
                        pe.wait_ge(sm["v2_ready"], t + 1)
                        pe.wait_ge(sm["ptb_ready"], t + 1)
                        if t == 0:
                            pe.wait_ge(sm["sc_ready"], G)
                        ins = attend2(0, t, 2)
                    ins.then_inc(sm["pv0_ps"], 1)
                if n == LAST + NT + 3:
                    first_product(0)

            first_product(1).then_inc(sm["main_ps"], 1)
            pair_attention(1)

            for k in range(1, C2 * NE):
                pe.wait_ge(sm["oelo_ready"], k // OEU + 1)
                pe.wait_ge(sm["glo_ready"], k + 1)
                for m in range(KC):
                    for hf in range(2):
                        ins = product(k, m, hf)
                        if k == C2 * NE - 1:
                            ins.then_inc(sm["acc_done"], 1)
                if k < C2 * NE - 1:
                    ins.then_inc(sm["main_ps"], 1)
                if k % NE == PV_AT and 1 < k // NE + 1 < C2:
                    pair_attention(k // NE + 1)


def kernel(**inputs):
    import concourse.bacc as bacc
    from concourse.bass_utils import run_bass_kernel_spmd

    x = np.asarray(inputs["x"])
    patches = x.reshape(B, CH, SIDE, PATCH, SIDE, PATCH).transpose(0, 2, 4, 3, 5, 1).reshape(B, NPATCH, DIN)
    rows = np.zeros((G * GI, S, DIN), np.float32)
    rows[:B, 1:] = patches
    tokw = np.asarray(inputs["L0_tok_weight"]).T.reshape(DC, P, D).transpose(1, 0, 2).reshape(P, DC * D)
    vecs = np.concatenate([np.asarray(inputs["L0_tok_pos_embedding"]).reshape(1, D),
                           np.asarray(inputs["L0_tok_class_token"]).reshape(1, D),
                           np.asarray(inputs["L0_attn_bout"]).reshape(1, D)])
    w = np.asarray(inputs["L0_attn_Wqkv"])
    wq, wk, wv = w[:, :D], w[:, D:2 * D], w[:, 2 * D:]
    swap = np.arange(D) ^ 1
    wqkv = np.stack([wq, wk, wq[:, swap], wk[:, swap], wv], 1).reshape(KC, P, 5, D).transpose(1, 2, 0, 3)
    wout = np.asarray(inputs["L0_attn_Wout"]).reshape(KC, P, D).transpose(1, 0, 2)
    w2 = np.concatenate([np.asarray(inputs["L0_ffn_w_q"]), np.asarray(inputs["L0_ffn_w_k"]),
                         np.asarray(inputs["L0_ffn_w_gate"])], 1).reshape(KC, P, -1).transpose(1, 0, 2)
    ve = np.asarray(inputs["L0_ffn_value_experts"]).transpose(0, 2, 1, 3)
    ve = ve.reshape(NE, KC, P, NH2 * DH2).transpose(0, 2, 1, 3)
    oe = np.asarray(inputs["L0_ffn_output_experts"]).reshape(NE, C2, 2 * DH2, D).transpose(1, 0, 2, 3)
    oe = oe.reshape(C2, NE // OEU, OEU, P, D).transpose(0, 1, 3, 2, 4).reshape(NOU, P, OEU, D)
    arrays = {"x_rows": rows.reshape(G, R, DIN), "tok_weight": tokw, "vectors": vecs, "constants": shape_constants(),
              "w_qkv": wqkv, "w_out": wout, "w_qkgate": w2, "value_w": ve, "output_w": oe}
    arrays = {n: np.ascontiguousarray(a) for n, a in arrays.items()}

    nc = bacc.Bacc("TRN2", target_bir_lowering=False, num_devices=1)
    args = [nc.dram_tensor(n, a.shape, F32, kind="ExternalInput").ap() for n, a in arrays.items()]
    out = nc.dram_tensor("out", [KC, P, 2, HALF], F32, kind="ExternalOutput").ap()
    mask_rows = nc.dram_tensor("mask_rows", [NH2 * NE, T], mybir.dt.bfloat16, kind="Internal").ap()
    vit_block(nc, *args, mask_rows, out)
    r = run_bass_kernel_spmd(nc, [arrays], core_ids=[0])
    y = r.results[0]["out"].reshape(D, T)
    return np.ascontiguousarray(y.T).reshape(B, S, D)
```
